# Optimizing a Trainium2 kernel written in Bass

```python
import numpy as np
import jax
import jax.numpy as jnp

def _softmax(x, axis=-1):
    return jax.nn.softmax(x, axis=axis)

def _gelu(x):
    return jax.nn.gelu(x, approximate=True)

def _silu(x):
    return jax.nn.silu(x)

def _sigmoid(x):
    return jax.nn.sigmoid(x)

def _layernorm(x, axis=-1, eps=1e-05):
    m = jnp.mean(x, axis=axis, keepdims=True)
    v = jnp.var(x, axis=axis, keepdims=True)
    return (x - m) / jnp.sqrt(v + eps)

def _scatter_add(tgt, idx, src, axis=0):
    return tgt.at[idx].add(src)

def _segment_sum(src, seg, n):
    return jax.ops.segment_sum(src, seg, n)
kernel_name = 'mk_seq_preln_d1_jaxref_r4_46ddff'

def setup_inputs(seed: int=0):
    np.random.seed(seed)
    _w = jnp.asarray

    def _L0_attn_setup():
        import jax, jax.numpy as jnp
        import numpy as np
        B, L, D, H = (1, 512, 256, 16)
        d = D // H

        def _forward(x, Wqkv_w, Wqkv_b, out_w, out_b, W_static, Lambda_raw, Gamma, gate_w1, gate_b1, gate_w2, gate_b2):
            Bb, Ll, Dm = x.shape
            Hh = Gamma.shape[0]
            dd = Dm // Hh
            scale = 1.0 / np.sqrt(dd)
            qkv = (x @ Wqkv_w + Wqkv_b).reshape(Bb, Ll, 3, Hh, dd)
            q = jnp.transpose(qkv[:, :, 0], (0, 2, 1, 3))
            k = jnp.transpose(qkv[:, :, 1], (0, 2, 1, 3))
            v = jnp.transpose(qkv[:, :, 2], (0, 2, 1, 3))
            scores = jnp.einsum('bhid,bhjd->bhij', q, k) * scale
            causal_mask = jnp.triu(jnp.full((Ll, Ll), -10000.0, dtype=scores.dtype), 1)
            attn = jax.nn.softmax(scores + causal_mask, axis=-1)
            y_softmax = jnp.einsum('bhij,bhjd->bhid', attn, v)
            retention = 1.0 - jax.nn.sigmoid(Lambda_raw)
            k_stp = k * scale

            def step(state, inp):
                q_t, k_t, v_t = inp
                hebbian = v_t[..., :, None] * k_t[..., None, :]
                state = retention * state + Gamma * hebbian
                y_t = jnp.einsum('bhij,bhj->bhi', W_static + state, q_t)
                return (state, y_t)
            state0 = jnp.zeros((Bb, Hh, dd, dd), x.dtype)
            qT = jnp.moveaxis(q, 2, 0)
            kT = jnp.moveaxis(k_stp, 2, 0)
            vT = jnp.moveaxis(v, 2, 0)
            _, ys = jax.lax.scan(step, state0, (qT, kT, vT))
            y_stp = jnp.moveaxis(ys, 0, 2)
            g = jax.nn.gelu(x @ gate_w1 + gate_b1, approximate=False)
            alpha = jax.nn.sigmoid(g @ gate_w2 + gate_b2)
            alpha = jnp.transpose(alpha, (0, 2, 1))[..., None]
            y = alpha * y_softmax + (1.0 - alpha) * y_stp
            y = jnp.transpose(y, (0, 2, 1, 3)).reshape(Bb, Ll, Dm)
            return y @ out_w + out_b
        key = jax.random.key(seed)
        ks = jax.random.split(key, 8)
        s = 1.0 / np.sqrt(D)
        return {'x': jax.random.normal(ks[0], (B, L, D), jnp.float32), 'Wqkv_w': jax.random.normal(ks[1], (D, 3 * D), jnp.float32) * s, 'Wqkv_b': jnp.zeros((3 * D,), jnp.float32), 'out_w': jax.random.normal(ks[2], (D, D), jnp.float32) * s, 'out_b': jnp.zeros((D,), jnp.float32), 'W_static': jnp.zeros((H, d, d), jnp.float32), 'Lambda_raw': jax.random.uniform(ks[3], (H, d, d), jnp.float32, -3.0, 3.0), 'Gamma': jax.random.uniform(ks[4], (H, d, d), jnp.float32, -0.5 / np.sqrt(d), 0.5 / np.sqrt(d)), 'gate_w1': jax.random.normal(ks[5], (D, D // 2), jnp.float32) * s, 'gate_b1': jnp.zeros((D // 2,), jnp.float32), 'gate_w2': jax.random.normal(ks[6], (D // 2, H), jnp.float32) * (1.0 / np.sqrt(D // 2)), 'gate_b2': jnp.zeros((H,), jnp.float32)}
    _L0_attn_in = _L0_attn_setup()

    def _L0_ffn_setup():
        import jax, jax.numpy as jnp
        import numpy as np
        FP8_MAX = 448.0

        def quant_fp8(x):
            amax = jnp.max(jnp.abs(x)).astype(jnp.float32)
            scale = jnp.minimum(FP8_MAX / jnp.maximum(amax, 1e-12), FP8_MAX)
            x_fp8 = jnp.clip(x * scale, -FP8_MAX, FP8_MAX).astype(jnp.float8_e4m3fn)
            return (x_fp8, 1.0 / scale)
        key = jax.random.key(seed)
        k1, k2, k3 = jax.random.split(key, 3)
        B, S, IN, OUT = (4, 2048, 256, 256)
        input = jax.random.normal(k1, (B, S, IN), dtype=jnp.float32)
        bound = 1.0 / np.sqrt(IN)
        weight = jax.random.uniform(k2, (OUT, IN), dtype=jnp.float32, minval=-bound, maxval=bound)
        bias = jax.random.uniform(k3, (OUT,), dtype=jnp.float32, minval=-bound, maxval=bound)
        return {'input': input, 'weight': weight, 'bias': bias}
    _L0_ffn_in = _L0_ffn_setup()
    _d = {'L0_attn_x': _L0_attn_in['x'], 'L0_attn_Wqkv_w': _L0_attn_in['Wqkv_w'], 'L0_attn_Wqkv_b': _L0_attn_in['Wqkv_b'], 'L0_attn_out_w': _L0_attn_in['out_w'], 'L0_attn_out_b': _L0_attn_in['out_b'], 'L0_attn_W_static': _L0_attn_in['W_static'], 'L0_attn_Lambda_raw': _L0_attn_in['Lambda_raw'], 'L0_attn_Gamma': _L0_attn_in['Gamma'], 'L0_attn_gate_w1': _L0_attn_in['gate_w1'], 'L0_attn_gate_b1': _L0_attn_in['gate_b1'], 'L0_attn_gate_w2': _L0_attn_in['gate_w2'], 'L0_attn_gate_b2': _L0_attn_in['gate_b2'], 'L0_ffn_weight': _L0_ffn_in['weight'], 'L0_ffn_bias': _L0_ffn_in['bias']}
    _x0 = _d['L0_attn_x']
    _d['L0_attn_x'] = jax.random.normal(jax.random.fold_in(jax.random.key(seed), 1), (1, 4096, 256), dtype=_x0.dtype)
    del _x0
    return _d

def reference(L0_attn_x, L0_attn_Wqkv_w, L0_attn_Wqkv_b, L0_attn_out_w, L0_attn_out_b, L0_attn_W_static, L0_attn_Lambda_raw, L0_attn_Gamma, L0_attn_gate_w1, L0_attn_gate_b1, L0_attn_gate_w2, L0_attn_gate_b2, L0_ffn_weight, L0_ffn_bias):

    def _L0_attn_ref(x, Wqkv_w, Wqkv_b, out_w, out_b, W_static, Lambda_raw, Gamma, gate_w1, gate_b1, gate_w2, gate_b2):
        import jax, jax.numpy as jnp
        import numpy as np
        B, L, D, H = (1, 512, 256, 16)
        d = D // H

        def _forward(x, Wqkv_w, Wqkv_b, out_w, out_b, W_static, Lambda_raw, Gamma, gate_w1, gate_b1, gate_w2, gate_b2):
            Bb, Ll, Dm = x.shape
            Hh = Gamma.shape[0]
            dd = Dm // Hh
            scale = 1.0 / np.sqrt(dd)
            qkv = (x @ Wqkv_w + Wqkv_b).reshape(Bb, Ll, 3, Hh, dd)
            q = jnp.transpose(qkv[:, :, 0], (0, 2, 1, 3))
            k = jnp.transpose(qkv[:, :, 1], (0, 2, 1, 3))
            v = jnp.transpose(qkv[:, :, 2], (0, 2, 1, 3))
            scores = jnp.einsum('bhid,bhjd->bhij', q, k) * scale
            causal_mask = jnp.triu(jnp.full((Ll, Ll), -10000.0, dtype=scores.dtype), 1)
            attn = jax.nn.softmax(scores + causal_mask, axis=-1)
            y_softmax = jnp.einsum('bhij,bhjd->bhid', attn, v)
            retention = 1.0 - jax.nn.sigmoid(Lambda_raw)
            k_stp = k * scale

            def step(state, inp):
                q_t, k_t, v_t = inp
                hebbian = v_t[..., :, None] * k_t[..., None, :]
                state = retention * state + Gamma * hebbian
                y_t = jnp.einsum('bhij,bhj->bhi', W_static + state, q_t)
                return (state, y_t)
            state0 = jnp.zeros((Bb, Hh, dd, dd), x.dtype)
            qT = jnp.moveaxis(q, 2, 0)
            kT = jnp.moveaxis(k_stp, 2, 0)
            vT = jnp.moveaxis(v, 2, 0)
            _, ys = jax.lax.scan(step, state0, (qT, kT, vT))
            y_stp = jnp.moveaxis(ys, 0, 2)
            g = jax.nn.gelu(x @ gate_w1 + gate_b1, approximate=False)
            alpha = jax.nn.sigmoid(g @ gate_w2 + gate_b2)
            alpha = jnp.transpose(alpha, (0, 2, 1))[..., None]
            y = alpha * y_softmax + (1.0 - alpha) * y_stp
            y = jnp.transpose(y, (0, 2, 1, 3)).reshape(Bb, Ll, Dm)
            return y @ out_w + out_b
        return _forward(x, Wqkv_w, Wqkv_b, out_w, out_b, W_static, Lambda_raw, Gamma, gate_w1, gate_b1, gate_w2, gate_b2)

    def _L0_ffn_ref(input, weight, bias):
        import jax, jax.numpy as jnp
        import numpy as np
        FP8_MAX = 448.0

        def quant_fp8(x):
            amax = jnp.max(jnp.abs(x)).astype(jnp.float32)
            scale = jnp.minimum(FP8_MAX / jnp.maximum(amax, 1e-12), FP8_MAX)
            x_fp8 = jnp.clip(x * scale, -FP8_MAX, FP8_MAX).astype(jnp.float8_e4m3fn)
            return (x_fp8, 1.0 / scale)
        prev_shape = input.shape
        x2d = input.reshape(-1, weight.shape[1])
        w_fp8, w_scale = quant_fp8(weight)
        x_fp8, x_scale = quant_fp8(x2d)
        acc = jnp.matmul(x_fp8.astype(jnp.float32), w_fp8.astype(jnp.float32).T)
        out2d = (acc * (x_scale * w_scale) + bias).astype(jnp.bfloat16)
        out = out2d.reshape(*prev_shape[:-1], weight.shape[0]).astype(input.dtype)
        return out
    x = L0_attn_x
    x = x + _L0_attn_ref(_layernorm(x, axis=-1), L0_attn_Wqkv_w, L0_attn_Wqkv_b, L0_attn_out_w, L0_attn_out_b, L0_attn_W_static, L0_attn_Lambda_raw, L0_attn_Gamma, L0_attn_gate_w1, L0_attn_gate_b1, L0_attn_gate_w2, L0_attn_gate_b2)
    x = x + _L0_ffn_ref(_layernorm(x, axis=-1), L0_ffn_weight, L0_ffn_bias)
    return x

_drawn_inputs = setup_inputs


def setup_inputs(seed=0):
    import zlib

    import numpy as np

    out = dict(_drawn_inputs(seed))
    spreads = {'L0_attn_Wqkv_b': (0.0, 0.1),
     'L0_attn_out_b': (0.0, 0.1),
     'L0_attn_W_static': (0.0, 0.1),
     'L0_attn_gate_b1': (0.0, 0.653),
     'L0_attn_gate_b2': (0.0, 0.567)}
    factors = {}
    for name, (base, spread) in spreads.items():
        noise = np.random.default_rng([zlib.crc32(name.encode()), seed]).standard_normal(out[name].shape)
        drawn = base * np.exp(spread * noise) if base else spread * noise
        out[name] = jnp.asarray(drawn.astype(out[name].dtype))
    for name, factor in factors.items():
        out[name] = (out[name] * factor).astype(out[name].dtype)
    return out
```

```python
from contextlib import ExitStack

import concourse.bass as bass
from concourse import mybir

F32 = mybir.dt.float32
BF16 = mybir.dt.bfloat16
I32 = mybir.dt.int32
ALU = mybir.AluOpType
ACT = mybir.ActivationFunctionType
AX = mybir.AxisListType

P = 128
T, D, H = 4096, 256, 16
HD = D // H
CH = 512
NCH = T // CH
TPC = CH // P
NT = T // P
GH = 4
NG = H // GH
HALF = 2
HPH = H // HALF
GATE = D // 2
VW = 32
SPLIT_Q = (0, 0, 1, 1, 0, 2)
SPLIT_K = (0, 1, 0, 1, 2, 0)
KS = len(SPLIT_Q) * HD
KR = KS + 2
SCALE = HD ** -0.5
MASKED = -10000.0 / SCALE
EPS = 1e-5
FP8_MAX = 448.0
FP8_MIN_NORMAL = 2.0 ** -6
ROUND_TO_3_BITS = 1.5 * 2.0 ** 20
EXPONENT_BITS = 0x7F800000

ORDER = (1, 3, 5, 7, 6, 4, 2, 0)
KEY_TILES = tuple(TPC * (c + 1) for c in ORDER)
TILE_AT = tuple(sum(KEY_TILES[:s]) for s in range(NCH))
TILES = sum(KEY_TILES)
MAXES = tuple(GH * TPC * (c + 1) for c in ORDER)
MAX_AT = tuple(sum(MAXES[:s]) for s in range(NCH))
N_MAX = sum(MAXES)
UNITS = 64
BURST = 16
N_BURST = UNITS // BURST
MAX_PER_TILE = 5
P_SLOTS = 3
RING = 4
V_PIECES = 4
UNITS_PER_CHUNK = 7
STORES_PER_CHUNK = 16 * (3 + 3 + NG)
LOADS_PER_CHUNK = 16 * (2 + NG)
N_WEIGHTS = 13
PAD = 1024


def group_steps():
    steps, late = [], []

    def emit(step):
        steps.append(step)
        if step[0] in ("max", "scores"):
            for x in late:
                x[0] -= 1
            while late and late[0][0] <= 0:
                steps.append(late.pop(0)[1])
            late.sort(key=lambda x: x[0])

    def after(n, step):
        late.append([n, step])
        late.sort(key=lambda x: x[0])

    def drain():
        while late:
            steps.append(late.pop(0)[1])

    todo = [(s, n) for s in range(NCH) for n in range(MAXES[s])]

    def max_item():
        s, n = todo.pop(0)
        if n == 0 and s + 1 < NCH:
            emit(("load", s + 1))
        emit(("max", s, n))
        if n == MAXES[s] - 1:
            emit(("fold", s))
            after(3, ("shift_turn", s))
            after(7, ("shift_split", s))

    emit(("load", 0))
    while todo[0][0] == 0:
        max_item()
    done_units, at, pending = 0, 0, None
    for s in range(NCH):
        while todo and todo[0][0] <= s:
            max_item()
        if ("shift_split", s) not in steps:
            drain()
        for kt in range(KEY_TILES[s]):
            emit(("scores", s, kt))
            if pending:
                emit(("values",) + pending)
                if pending[1] == KEY_TILES[pending[0]] - 1:
                    emit(("out_evac", pending[0]))
                    after(3, ("out_turn", pending[0]))
                    after(6, ("out_norm", pending[0]))
            pending = (s, kt)
            at += 1
            while done_units < UNITS and done_units * TILES <= at * UNITS:
                emit(("unit", done_units))
                done_units += 1
                if done_units % BURST == 2 and done_units > BURST:
                    emit(("burst", done_units // BURST - 1))
            for _ in range(MAX_PER_TILE):
                if todo:
                    max_item()
    emit(("values",) + pending)
    emit(("out_evac", NCH - 1))
    drain()
    emit(("out_turn", NCH - 1))
    emit(("out_norm", NCH - 1))
    emit(("burst", N_BURST - 1))
    return steps


STEPS = group_steps()
BANK_USES = [x for x in STEPS if x[0] in ("shift_turn", "out_turn", "burst")]
BANK_AT = {x: n for n, x in enumerate(BANK_USES)}
N_BANK = len(BANK_USES)


def preln_attention_ffn_kernel(nc, x, wqkv, bqkv, out_w, out_b, w_static, lam, gamma, gate_w1,
                               gate_b1, gate_w2, gate_b2, ffn_wt, ffn_b, out):
    ctx = ExitStack()
    with ctx:
        def sb(name, shape, dt=F32, where=ctx):
            return where.enter_context(nc.sbuf_tensor(name, shape, dt))

        def sem(name):
            return ctx.enter_context(nc.semaphore(name))

        PS = ctx.enter_context(nc.psum_tensor("PS", [P, 8, CH], F32))

        qk_parts = nc.dram_tensor("qk_parts", [3, 2 * D, T], BF16).ap()
        qkv_t = nc.dram_tensor("qkv_t", [3 * D, T], F32).ap()
        v_rows = nc.dram_tensor("v_rows", [NG, P, NT, GH * VW], F32).ap()
        y_soft = nc.dram_tensor("y_soft", [NG, T, GH * HD], F32).ap()
        y_stp_t = nc.dram_tensor("y_stp_t", [HALF, P, PAD + T], F32).ap()

        ident = sb("ident", [P, P])
        ident_bf = sb("ident_bf", [P, P], BF16)
        mask_qk = sb("mask_qk", [P, P], BF16)
        mask_kq = sb("mask_kq", [P, P], BF16)
        same_head = sb("same_head", [P, HPH])
        retention = sb("retention", [P, HALF * HD])
        sum_j = sb("sum_j", [P, HALF, HD, VW])
        static_j = sb("static_j", [P, HALF, P])
        carry = sb("carry", [P, HALF * HD])
        alpha = sb("alpha", [P, NT, H])
        outw_sb = sb("outw_sb", [P, HALF, D])
        outb_sb = sb("outb_sb", [P, D])
        ffnb_sb = sb("ffnb_sb", [P, D])
        wq = sb("wq", [P, HALF, D], BF16)
        w_step = sb("w_step", [P, 1])

        neg_half = sb("neg_half", [P, TPC])

        weights_loaded = sem("weights_loaded")
        beats = sem("beats")


        credits = {}

        def free_sem(name, credit):
            s = sem(name)
            credits[name] = (s, credit)
            return s

        x_loaded = [sem(f"x_loaded{k}") for k in range(2)]
        stored = [free_sem(f"stored{k}", STORES_PER_CHUNK) for k in range(2)]
        stats_done, mv_done, rstd_done = sem("stats_done"), sem("mv_done"), sem("rstd_done")
        var_done, var2 = sem("var_done"), sem("var2")
        xn_ready = free_sem("xn_ready", 2)
        xnt_ready = free_sem("xnt_ready", 4)
        xnt_evac = free_sem("xnt_evac", 2)
        proj_ready = free_sem("proj_ready", 2 * UNITS_PER_CHUNK)
        proj_evac = free_sem("proj_evac", UNITS_PER_CHUNK)
        high_done, rest1_done, mid_done = sem("high_done"), sem("rest1_done"), sem("mid_done")
        low_done = sem("low_done")
        vrow_ready, vrow_evac = sem("vrow_ready"), free_sem("vrow_evac", 2)
        z_ready, z_evac = free_sem("z_ready", 2), free_sem("z_evac", 1)
        dve_setup, act_setup, pool_setup = sem("dve_setup"), sem("act_setup"), sem("pool_setup")
        vaug_ready = sem("vaug_ready")
        k_loaded = [sem(f"k_loaded{c}") for c in range(NCH)]
        q_loaded = [sem(f"q_loaded{c}") for c in range(NCH)]
        v_loaded = [sem(f"v_loaded{c}") for c in range(V_PIECES)]
        max_ready, max_done = sem("max_ready"), free_sem("max_done", 2)
        folded, shift_turned, shift_high = sem("folded"), sem("shift_turned"), sem("shift_high")
        shift_loaded = [free_sem(f"shift_loaded{k}", 32) for k in range(2)]
        scores_ready, exp_done = sem("scores_ready"), free_sem("exp_done", 2)
        values_done = free_sem("values_done", P_SLOTS)
        out_evacuated, out_turned = free_sem("out_evacuated", 1), free_sem("out_turned", 2)
        denom_ready, ones_ready = sem("denom_ready"), sem("ones_ready")
        y_stored = [free_sem(f"y_stored{k}", 16) for k in range(2)]
        bank_free = free_sem("bank_free", 1)
        kq_loaded = [sem(f"kq_loaded{k}") for k in range(2)]
        vexp_loaded = [sem(f"vexp_loaded{k}") for k in range(RING)]
        u_made, scanned = free_sem("u_made", 1), free_sem("scanned", RING)
        weighted, burst_done = free_sem("weighted", RING), free_sem("burst_done", 1)
        stp_stored = [free_sem(f"stp_stored{k}", 16) for k in range(2)]
        soft_loaded = [sem(f"soft_loaded{k}") for k in range(2)]
        stp_turned, diff_made, diff_weighted = sem("stp_turned"), sem("diff_made"), sem("diff_weighted")
        xb_made, y_made, y_turned = sem("xb_made"), free_sem("y_made", 2), sem("y_turned")
        yt_evac, attn_ready, x1_made = free_sem("yt_evac", 2), free_sem("attn_ready", 2), free_sem("x1_made", 2)
        stats2, mv2, rstd2, nmr2 = sem("stats2"), sem("mv2"), sem("rstd2"), sem("nmr2")
        xn2_made, amax_made, amax_all = sem("xn2_made"), sem("amax_made"), sem("amax_all")
        scale_chain, peak_ready = sem("scale_chain"), sem("peak_ready")
        scaled, exponent_done, magic_done = sem("scaled"), sem("exponent_done"), sem("magic_done")
        shifted, rounded, r_turned = sem("shifted"), free_sem("rounded", 2), free_sem("r_turned", 2)
        rt_evac, ffn_ready = free_sem("rt_evac", 2), free_sem("ffn_ready", 2)
        ffn_biased, out_made = free_sem("ffn_biased", 2), free_sem("out_made", 2)
        out_stored = [free_sem(f"out_stored{k}", 16) for k in range(2)]

        with nc.Block() as block:
            @block.gpsimd
            def _(pool):
                for s, n in credits.values():
                    pool.sem_inc(s, n)

        pro = ExitStack()
        with pro:
            wqkv_sb = sb("wqkv_sb", [P, HALF, 3 * D], where=pro)
            bqkv_sb = sb("bqkv_sb", [P, 6], where=pro)
            w1_sb = sb("w1_sb", [P, HALF, GATE], where=pro)
            b1_sb = sb("b1_sb", [P, 1], where=pro)
            w2_sb = sb("w2_sb", [P, H], where=pro)
            b2_sb = sb("b2_sb", [P, H], where=pro)
            lam_sb = sb("lam_sb", [P, HALF * HD], where=pro)
            gamma_sb = sb("gamma_sb", [P, HALF * HD], where=pro)
            wst_sb = sb("wst_sb", [P, HALF * HD], where=pro)
            ffnw_sb = sb("ffnw_sb", [P, HALF * D], where=pro)
            wtmp = sb("wtmp", [P, 3, HALF * D], where=pro)
            wsmall = sb("wsmall", [P, 8], where=pro)
            xin = sb("xin", [P, 2, TPC, D], where=pro)
            xn = sb("xn", [P, 2, TPC, D], where=pro)
            stats = sb("stats", [P, TPC, 6], where=pro)
            mv = sb("mv", [P, TPC, 2], where=pro)
            rstd = sb("rstd", [P, TPC], where=pro)
            var_eps = sb("var_eps", [P, TPC], where=pro)
            xn_t = sb("xn_t", [P, 2, HALF, CH], where=pro)
            proj = sb("proj", [P, 2, 6, CH], where=pro)
            gate_t = sb("gate_t", [P, 2, CH], where=pro)
            parts = sb("parts", [P, 2, 3, 4, CH], BF16, where=pro)
            rest = sb("rest", [P, 2, 4, CH], where=pro)
            vaug = sb("vaug", [P, 2, TPC, H, VW], where=pro)
            z = sb("z", [P, NT, H], where=pro)
            x_tiles = x.rearrange("(t p) n -> p t n", p=P)

            with nc.Block() as block:
                @block.sync
                def _(sp):
                    with sp.Fori(0, NCH // 2) as it:
                        for par in range(2):
                            sp.wait_ge(xn_ready, it * 2 + par + 1)
                            sp.dma_start(xin[:, par], x_tiles[:, bass.ds(it * (2 * TPC) + par * TPC, TPC), :])\
                                .then_inc(x_loaded[par], 16)
                        for par in range(2):
                            rows = bass.ds(it * (2 * CH) + par * CH, CH)
                            sp.wait_ge(proj_evac, it * 14 + par * 7 + 13)
                            for w in range(3):
                                sp.dma_start(qkv_t[w * D:(w + 1) * D, rows].rearrange("(u p) t -> p u t", p=P),
                                             proj[:, par, 2 * w:2 * w + 2, :]).then_inc(stored[par], 16)
                            for n, (made, k) in enumerate([(high_done, 1), (mid_done, 1), (low_done, 1)]):
                                sp.wait_ge(made, it * 2 + par + k)
                                sp.sem_inc(beats, 1)
                                sp.dma_start(qk_parts[n, :, rows].rearrange("(u p) t -> p u t", p=P),
                                             parts[:, par, n, :, :]).then_inc(stored[par], 16)
                            sp.wait_ge(vrow_evac, it * 4 + par * 2 + 4)
                            for g in range(NG):
                                sp.dma_start(
                                    v_rows[g, :, bass.ds(it * (2 * TPC) + par * TPC, TPC), :],
                                    vaug[:, par, :, g * GH:(g + 1) * GH, :].rearrange("p t h v -> p t (h v)"),
                                ).then_inc(stored[par], 16)
                    for par in range(2):
                        sp.wait_ge(stored[par], STORES_PER_CHUNK * (NCH // 2 + 1))

                @block.gpsimd
                def _(pool):
                    pool.memset(ident[:, :], 0.0).then_inc(pool_setup, 1)
                    pool.memset(mask_qk[:, :], 0.0).then_inc(pool_setup, 1)
                    pool.memset(mask_kq[:, :], 0.0).then_inc(pool_setup, 1)
                    pool.memset(same_head[:, :], 1.0).then_inc(pool_setup, 1)
                    pool.wait_ge(pool_setup, 4)
                    pool.affine_select(out=ident[:, :], in_=ident[:, :], compare_op=ALU.not_equal, fill=1.0,
                                       base=0, pattern=[[-1, P]], channel_multiplier=1).then_inc(pool_setup, 1)
                    pool.affine_select(out=mask_qk[:, :], in_=mask_qk[:, :], compare_op=ALU.is_ge, fill=MASKED,
                                       base=0, pattern=[[-1, P]], channel_multiplier=1).then_inc(pool_setup, 1)
                    pool.affine_select(out=mask_kq[:, :], in_=mask_kq[:, :], compare_op=ALU.is_ge, fill=MASKED,
                                       base=0, pattern=[[1, P]], channel_multiplier=-1).then_inc(pool_setup, 1)
                    pool.affine_select(out=same_head[:, :], in_=same_head[:, :], compare_op=ALU.is_ge, fill=0.0,
                                       base=0, pattern=[[-HD, HPH]], channel_multiplier=1).then_inc(pool_setup, 1)
                    pool.wait_ge(pool_setup, 8)
                    pool.affine_select(out=same_head[:, :], in_=same_head[:, :], compare_op=ALU.is_ge, fill=0.0,
                                       base=HD - 1, pattern=[[HD, HPH]], channel_multiplier=-1)\
                        .then_inc(pool_setup, 1)
                    pool.tensor_copy(ident_bf[:, :], ident[:, :]).then_inc(pool_setup, 1)
                    for par in range(2):
                        pool.memset(vaug[:, par, :, :, HD:HD + 1], 1.0).then_inc(vaug_ready, 1)
                        pool.memset(vaug[:, par, :, :, HD + 1:VW], 0.0).then_inc(vaug_ready, 1)
                    pool.memset(neg_half[:, :], -0.5).then_inc(pool_setup, 1)
                    pool.wait_ge(pool_setup, 11)
                    with pool.Fori(0, NCH // 2) as it:
                        for par in range(2):
                            pool.wait_ge(var_done, it * 2 + par + 1)
                            pool.tensor_tensor(rstd[:, :], var_eps[:, :], neg_half[:, :], ALU.pow).then_inc(rstd_done, 1)
                            pool.wait_ge(mid_done, it * 2 + par + 1)
                            pool.tensor_tensor(parts[:, par, 2], rest[:, par], parts[:, par, 1], ALU.subtract)\
                                .then_inc(low_done, 1)
                    pool.wait_ge(dve_setup, 1)
                    pool.partition_all_reduce(wsmall[:, 1:2], wsmall[:, 0:1], P, bass.bass_isa.ReduceOp.max)\
                        .then_inc(pool_setup, 1)

                @block.tensor
                def _(pe):
                    pe.wait_ge(pool_setup, 10)
                    pe.wait_ge(weights_loaded, 16 * N_WEIGHTS)
                    with pe.Fori(0, NCH // 2) as it:
                        for par in range(2):
                            pe.wait_ge(xn_ready, it * 2 + par + 3)
                            for c in range(HALF):
                                pe.wait_ge(xnt_evac, it * 4 + par * 2 + c + 1)
                                for j in range(TPC):
                                    mm = pe.transpose(PS[:, c, j * P:(j + 1) * P],
                                                      xn[:, par, j, c * P:(c + 1) * P], ident[:, :])
                                mm.then_inc(xnt_ready, 1)
                            pe.wait_ge(xnt_evac, it * 4 + par * 2 + 4)
                            for u in range(UNITS_PER_CHUNK):
                                pe.wait_ge(proj_evac, it * 14 + par * 7 + (u + 5 if u < 3 else u + 4 if u > 3 else 4))
                                for c in range(HALF):
                                    w = wqkv_sb[:, c, u * P:(u + 1) * P] if u < 6 else w1_sb[:, c, :]
                                    mm = pe.matmul(PS[:, 2 + u % 4, :], w, xn_t[:, par, c, :],
                                                   start=(c == 0), stop=(c == HALF - 1))
                                mm.then_inc(proj_ready, 1)
                            pe.wait_ge(proj_evac, it * 14 + par * 7 + 13)
                            for half in range(HALF):
                                pe.wait_ge(vrow_evac, it * 4 + par * 2 + half + 2)
                                for j in range(TPC):
                                    mm = pe.transpose(PS[:, 7, j * P:(j + 1) * P],
                                                      proj[:, par, 4 + half, j * P:(j + 1) * P], ident[:, :])
                                mm.then_inc(vrow_ready, 1)
                            pe.wait_ge(proj_evac, it * 14 + par * 7 + 14)
                            pe.wait_ge(z_evac, it * 2 + par + 1)
                            for j in range(TPC):
                                mm = pe.matmul(PS[:, 6, j * H:(j + 1) * H], gate_t[:, par, j * P:(j + 1) * P],
                                               w2_sb[:, :], start=True, stop=True)
                            mm.then_inc(z_ready, 1)

                @block.scalar
                def _(act):
                    for dst, src in [
                            (wqkv_sb[:, :, :], wqkv.rearrange("(c p) n -> p c n", p=P)),
                            (bqkv_sb[:, :], bqkv),
                            (w1_sb[:, :, :], gate_w1.rearrange("(c p) n -> p c n", p=P)),
                            (b1_sb[:, :], gate_b1), (w2_sb[:, :], gate_w2),
                            (b2_sb[:, :], gate_b2.broadcast_to([P, H])),
                            (lam_sb[:, :], lam), (gamma_sb[:, :], gamma), (wst_sb[:, :], w_static),
                            (ffnw_sb[:, :].rearrange("p (c n) -> p c n", c=HALF),
                             ffn_wt.rearrange("(c p) n -> p c n", p=P)),
                            (outw_sb[:, :, :], out_w.rearrange("(c p) n -> p c n", p=P)),
                            (outb_sb[:, :], out_b.broadcast_to([P, D])),
                            (ffnb_sb[:, :], ffn_b.broadcast_to([P, D]))]:
                        act.dma_start(dst, src).then_inc(weights_loaded, 16)
                    act.wait_ge(weights_loaded, 16 * N_WEIGHTS)
                    act.wait_ge(vaug_ready, 4)
                    with act.Fori(0, NCH // 2) as it:
                        for par in range(2):
                            for c in range(HALF):
                                act.wait_ge(xnt_ready, it * 4 + par * 2 + c + 5)
                                act.wait_ge(proj_ready, it * 14 + par * 7 + 7)
                                act.activation(xn_t[:, par, c, :], PS[:, c, :], ACT.Identity).then_inc(xnt_evac, 1)
                            act.wait_ge(stored[par], it * STORES_PER_CHUNK + STORES_PER_CHUNK)
                            for u in range(6):
                                act.wait_ge(proj_ready, it * 14 + par * 7 + u + 15)
                                act.activation(proj[:, par, u, :], PS[:, 2 + u % 4, :], ACT.Identity,
                                               bias=bqkv_sb[:, u:u + 1]).then_inc(proj_evac, 1)
                            act.wait_ge(proj_ready, it * 14 + par * 7 + 21)
                            act.wait_ge(z_ready, it * 2 + par + 1)
                            act.activation(gate_t[:, par, :], PS[:, 4, :], ACT.Gelu, bias=b1_sb[:, 0:1])\
                                .then_inc(proj_evac, 1)
                            for half in range(HALF):
                                act.wait_ge(vrow_ready, it * 4 + par * 2 + half + 1)
                                act.activation(vaug[:, par, :, half * HPH:(half + 1) * HPH, 0:HD],
                                               PS[:, 7, :].rearrange("p (j h d) -> p j h d", j=TPC, h=HPH),
                                               ACT.Identity).then_inc(vrow_evac, 1)
                            act.wait_ge(z_ready, it * 2 + par + 3)
                            act.activation(z[:, bass.ds(it * (2 * TPC) + par * TPC, TPC), :],
                                           PS[:, 6, 0:TPC * H].rearrange("p (j h) -> p j h", j=TPC),
                                           ACT.Identity).then_inc(z_evac, 1)
                    act.activation(lam_sb[:, :], lam_sb[:, :], ACT.Exp, scale=-1.0).then_inc(act_setup, 1)
                    act.wait_ge(dve_setup, 2)
                    act.activation(alpha[:, :, :], z[:, :, :], ACT.Exp, scale=-1.0).then_inc(act_setup, 1)

                @block.vector
                def _(dve):
                    with dve.Fori(0, NCH // 2) as it:
                        for par in range(2):
                            c1 = it * 2 + par + 1
                            dve.wait_ge(x_loaded[par], it * 16 + 16)
                            for j in range(TPC):
                                ins = dve.bn_stats(stats[:, j, :], xin[:, par, j, :])
                            ins.then_inc(stats_done, 1)
                            dve.wait_ge(stats_done, c1)
                            dve.sem_inc(beats, 1)
                            for j in range(TPC):
                                ins = dve.bn_aggr(mv[:, j, :], stats[:, j, :])
                            ins.then_inc(mv_done, 1)
                            dve.wait_ge(mv_done, c1)
                            dve.tensor_scalar(var_eps[:, :], mv[:, :, 1], EPS, None, ALU.add).then_inc(var_done, 1)
                            dve.wait_ge(rstd_done, c1)
                            dve.wait_ge(xnt_ready, it * 4 + par * 2 + 2)
                            for j in range(TPC):
                                ins = dve.tensor_scalar(xn[:, par, j, :], xin[:, par, j, :], mv[:, j, 0:1],
                                                        rstd[:, j:j + 1], ALU.subtract, ALU.mult)
                            ins.then_inc(xn_ready, 1)
                            dve.wait_ge(proj_evac, it * 14 + par * 7 + 11)
                            dve.wait_ge(stored[par], it * STORES_PER_CHUNK + STORES_PER_CHUNK)
                            dve.tensor_copy(parts[:, par, 0], proj[:, par, 0:4]).then_inc(high_done, 1)
                            dve.wait_ge(high_done, c1)
                            dve.tensor_tensor(rest[:, par], proj[:, par, 0:4], parts[:, par, 0], ALU.subtract)\
                                .then_inc(rest1_done, 1)
                            dve.wait_ge(rest1_done, c1)
                            dve.tensor_copy(parts[:, par, 1], rest[:, par]).then_inc(mid_done, 1)
                    dve.tensor_reduce(wsmall[:, 0:1], ffnw_sb[:, :], AX.X, ALU.max, apply_absolute_value=True)\
                        .then_inc(dve_setup, 1)
                    dve.wait_ge(z_evac, NCH + 1)
                    dve.tensor_tensor(z[:, :, :], z[:, :, :], b2_sb[:, :].unsqueeze(1).broadcast_to([P, NT, H]),
                                      ALU.add).then_inc(dve_setup, 1)
                    n_setup = 2

                    def link(ins):
                        nonlocal n_setup
                        n_setup += 1
                        ins.then_inc(dve_setup, 1)
                        dve.wait_ge(dve_setup, n_setup)

                    dve.wait_ge(act_setup, 1)
                    link(dve.tensor_scalar(lam_sb[:, :], lam_sb[:, :], 1.0, None, ALU.add))
                    link(dve.reciprocal(lam_sb[:, :], lam_sb[:, :]))
                    link(dve.tensor_scalar(retention[:, :], lam_sb[:, :], -1.0, 1.0, ALU.mult, ALU.add))
                    link(dve.memset(carry[:, :], 0.0))
                    link(dve.memset(sum_j[:, :, :, :], 0.0))
                    link(dve.tensor_scalar(gamma_sb[:, :], gamma_sb[:, :], SCALE, None, ALU.mult))
                    n_c = HD // TPC
                    heads = same_head[:, :].unsqueeze(1).broadcast_to([P, HALF * n_c, HPH])
                    for k in range(TPC):
                        link(dve.tensor_tensor(
                            sum_j[:, :, :, :].rearrange("p f (c k) v -> p (f c) k v", k=TPC)[:, :, k, k * HPH:(k + 1) * HPH],
                            heads,
                            gamma_sb[:, :].rearrange("p (c k) -> p c k", k=TPC)[:, :, k:k + 1]
                            .broadcast_to([P, HALF * n_c, HPH]), ALU.mult))
                        link(dve.tensor_tensor(
                            static_j[:, :, :].rearrange("p f (c k v) -> p (f c) k v", c=n_c, k=TPC)[:, :, k, :],
                            heads,
                            wst_sb[:, :].rearrange("p (c k) -> p c k", k=TPC)[:, :, k:k + 1]
                            .broadcast_to([P, HALF * n_c, HPH]), ALU.mult))
                    dve.wait_ge(act_setup, 2)
                    link(dve.tensor_scalar(alpha[:, :, :], alpha[:, :, :], 1.0, None, ALU.add))
                    link(dve.reciprocal(alpha[:, :, :], alpha[:, :, :]))
                    dve.wait_ge(pool_setup, 12)
                    link(dve.tensor_scalar(wsmall[:, 2:3], wsmall[:, 1:2], 1e-12, None, ALU.max))
                    link(dve.reciprocal(wsmall[:, 3:4], wsmall[:, 2:3]))
                    link(dve.tensor_scalar(wsmall[:, 4:5], wsmall[:, 3:4], FP8_MAX, FP8_MAX, ALU.mult, ALU.min))
                    link(dve.reciprocal(w_step[:, :], wsmall[:, 4:5]))
                    link(dve.tensor_scalar(wtmp[:, 0], ffnw_sb[:, :], wsmall[:, 4:5], FP8_MAX, ALU.mult, ALU.min))
                    link(dve.tensor_scalar(wtmp[:, 1].bitcast(I32), wtmp[:, 0].bitcast(I32), EXPONENT_BITS, None,
                                           ALU.bitwise_and))
                    link(dve.tensor_scalar(wtmp[:, 1], wtmp[:, 1], FP8_MIN_NORMAL, ROUND_TO_3_BITS, ALU.max, ALU.mult))
                    link(dve.scalar_tensor_tensor(out=wtmp[:, 2], in0=wtmp[:, 0], scalar=-FP8_MAX, in1=wtmp[:, 1],
                                                  op0=ALU.max, op1=ALU.add))
                    link(dve.tensor_tensor(wq[:, :, :].rearrange("p c n -> p (c n)"), wtmp[:, 2], wtmp[:, 1],
                                           ALU.subtract))

        att = ExitStack()
        with att:
            K_st = sb("K_st", [KR, NCH, GH, CH], BF16, where=att)
            Q_st = sb("Q_st", [KR, NCH, GH, CH], BF16, where=att)
            V_g = sb("V_g", [P, NT, GH * VW], where=att)
            probs = sb("probs", [P, P_SLOTS, GH, CH], where=att)
            pmax = sb("pmax", [P, 2, GH * TPC, NCH], where=att)
            neg_max = sb("neg_max", [P, 2, GH * TPC], where=att)
            shift = sb("shift", [GH * TPC, 2, 2, P], BF16, where=att)
            o_t = sb("o_t", [P, 2, CH], where=att)
            rden = sb("rden", [P, TPC, GH], where=att)
            y_sb = sb("y_sb", [P, 2, TPC, GH * HD], where=att)
            k_rows = sb("k_rows", [P, 2, CH], where=att)
            q_rows = sb("q_rows", [P, 2, CH], where=att)
            v_exp = sb("v_exp", [P, RING, CH], where=att)
            hebb = sb("hebb", [P, RING, CH], where=att)
            state = sb("state", [P, RING, CH], where=att)
            state_q = sb("state_q", [P, BURST, CH], where=att)
            stp_sb = sb("stp_sb", [P, 2, CH], where=att)

            with nc.Block() as block:
                @block.sync
                def _(sp):
                    def load_parts(g, stack, chunk, first_row, split, loaded):
                        for n, part in enumerate(split):
                            sp.dma_start(
                                stack[n * HD:(n + 1) * HD, chunk],
                                qk_parts[part, bass.ds(g * (GH * HD) + first_row, GH * HD),
                                         chunk * CH:(chunk + 1) * CH].rearrange("(h d) t -> d h t", d=HD),
                            ).then_inc(loaded[chunk], 16)

                    def load_kq(g, b):
                        cols = bass.ds(g * (2 * CH) + (b // HALF) * CH, CH)
                        half = b % HALF
                        for dst, first in ((k_rows, D), (q_rows, 0)):
                            sp.dma_start(dst[:, b % 2], qkv_t[first + half * P:first + (half + 1) * P, cols])\
                                .then_inc(kq_loaded[b % 2], 16)

                    def load_v_exp(g, n):
                        b, i = n // BURST, n % BURST
                        first = 2 * D + (b % HALF) * P
                        v = qkv_t[first:first + P, bass.ds(g * (2 * CH) + (b // HALF) * CH, CH)]
                        sp.dma_start(v_exp[:, n % RING], v.rearrange("(h i) t -> h i t", i=HD)[:, i, :]
                                     .unsqueeze(1).broadcast_to([HPH, HD, CH])).then_inc(vexp_loaded[n % RING], 16)

                    with sp.Fori(0, NG) as g:
                        for step in STEPS:
                            kind, s = step[0], step[1]
                            if kind == "load":
                                if s == 0:
                                    sp.wait_ge(values_done, g * TILES + P_SLOTS)
                                for c in range(ORDER[s] + 1):
                                    if c > max(ORDER[:s], default=-1):
                                        load_parts(g, K_st, c, D, SPLIT_K, k_loaded)
                                load_parts(g, Q_st, ORDER[s], 0, SPLIT_Q, q_loaded)
                                if s < V_PIECES:
                                    n = NT // V_PIECES
                                    sp.dma_start(V_g[:, s * n:(s + 1) * n, :],
                                                 v_rows[bass.ds(g, 1), :, s * n:(s + 1) * n, :]
                                                 .rearrange("g p t v -> (g p) t v")).then_inc(v_loaded[s], 16)
                                if s == 0:
                                    sp.wait_ge(burst_done, g * N_BURST + 1)
                                    load_kq(g, 0)
                                    sp.wait_ge(u_made, g * UNITS + 1)
                                    for n in range(RING - 1):
                                        load_v_exp(g, n)
                            elif kind == "unit":
                                if s % BURST == 0 and s // BURST + 1 < N_BURST:
                                    sp.wait_ge(burst_done, g * N_BURST + s // BURST + 1)
                                    load_kq(g, s // BURST + 1)
                                if s + RING - 1 < UNITS:
                                    sp.wait_ge(u_made, g * UNITS + s + 1)
                                    load_v_exp(g, s + RING - 1)
                            elif kind == "shift_split":
                                sp.wait_ge(bank_free, g * N_BANK + BANK_AT["shift_turn", s] + 2)
                                for k in range(2):
                                    sp.dma_start(Q_st[KS + k:KS + k + 1, ORDER[s]].rearrange("a h (j t) -> a (h j) t", t=P),
                                                 shift[:, s % 2, k, :]).then_inc(shift_loaded[s % 2], 16)
                            elif kind == "out_norm":
                                sp.wait_ge(bank_free, g * N_BANK + BANK_AT["out_turn", s] + 2)
                                sp.sem_inc(beats, 1)
                                c = ORDER[s]
                                sp.dma_start(y_soft[bass.ds(g, 1), c * CH:(c + 1) * CH, :]
                                             .rearrange("g (j p) v -> p (g j) v", p=P), y_sb[:, s % 2])\
                                    .then_inc(y_stored[s % 2], 16)
                            elif kind == "burst":
                                sp.wait_ge(bank_free, g * N_BANK + BANK_AT["burst", s] + 2)
                                sp.sem_inc(beats, 1)
                                sp.dma_start(y_stp_t[s % HALF, :, bass.ds(g * (2 * CH) + (s // HALF) * CH + PAD, CH)],
                                             stp_sb[:, s % 2]).then_inc(stp_stored[s % 2], 16)
                    for k in range(2):
                        sp.wait_ge(y_stored[k], 16 * (NG * NCH // 2 + 1))
                        sp.wait_ge(stp_stored[k], 16 * (NG * N_BURST // 2 + 1))

                @block.gpsimd
                def _(pool):
                    def weigh(g, n):
                        pool.wait_ge(scanned, g * UNITS + n + RING + 1)
                        if n % BURST == 0:
                            pool.wait_ge(burst_done, g * N_BURST + n // BURST + 1)
                        b, i = n // BURST, n % BURST
                        pool.tensor_tensor(state_q[:, i], state[:, n % RING], q_rows[:, b % 2], ALU.mult)
                        col = (b % HALF) * HD + i
                        pool.tensor_copy(carry[:, col:col + 1], state[:, n % RING, CH - 1:CH]).then_inc(weighted, 1)

                    with pool.Fori(0, NG) as g:
                        for n in range(UNITS):
                            b = n // BURST
                            if n % BURST == 0:
                                pool.wait_ge(kq_loaded[b % 2], g * 64 + 32 * (b // 2) + 32)
                            pool.wait_ge(vexp_loaded[n % RING], g * (16 * UNITS // RING) + 16 * (n // RING) + 16)
                            pool.wait_ge(scanned, g * UNITS + n + 1)
                            pool.tensor_tensor(hebb[:, n % RING], v_exp[:, n % RING], k_rows[:, b % 2], ALU.mult)\
                                .then_inc(u_made, 1)
                            if n >= 1:
                                weigh(g, n - 1)
                        weigh(g, UNITS - 1)

                @block.tensor
                def _(pe):
                    pe.wait_ge(ones_ready, 1)
                    with pe.Fori(0, NG) as g:
                        for step in STEPS:
                            kind, s = step[0], step[1]
                            c = ORDER[s] if kind not in ("unit", "burst") else None
                            if kind == "max":
                                n = step[2]
                                if n == 0:
                                    pe.wait_ge(q_loaded[c], g * (16 * len(SPLIT_Q)) + 16 * len(SPLIT_Q))
                                    for k in range(c + 1):
                                        if k > max(ORDER[:s], default=-1):
                                            pe.wait_ge(k_loaded[k], g * (16 * len(SPLIT_K)) + 16 * len(SPLIT_K))
                                hj, blk = n // (c + 1), n % (c + 1)
                                h, j = hj // TPC, hj % TPC
                                item = MAX_AT[s] + n
                                width = CH if blk < c else (j + 1) * P
                                bank = 4 + item % 2
                                pe.wait_ge(max_done, g * N_MAX + item + 1)
                                mm = pe.matmul(PS[:, bank, 0:width], Q_st[0:KS, c, h, j * P:(j + 1) * P],
                                               K_st[0:KS, blk, h, 0:width], start=True, stop=(blk < c))
                                if blk == c:
                                    mm = pe.matmul(PS[:, bank, j * P:(j + 1) * P], ident_bf[:, :], mask_qk[:, :],
                                                   start=False, stop=True)
                                mm.then_inc(max_ready, 1)
                            elif kind == "shift_turn":
                                pe.wait_ge(folded, g * NCH + s + 1)
                                pe.wait_ge(bank_free, g * N_BANK + BANK_AT[step] + 1)
                                pe.transpose(PS[0:GH * TPC, 7, 0:P], neg_max[:, s % 2, :], ident[:, :])\
                                    .then_inc(shift_turned, 1)
                            elif kind == "scores":
                                kt = step[2]
                                tile = TILE_AT[s] + kt
                                r = max(kt - TPC * c, 0)
                                if kt == 0:
                                    pe.wait_ge(shift_loaded[s % 2], g * (32 * NCH // 2) + 32 * (s // 2) + 64)
                                for pair in range(2):
                                    pe.wait_ge(exp_done, g * (2 * TILES) + 2 * tile + pair + 1)
                                    for i in range(2):
                                        h = 2 * pair + i
                                        keys = K_st[:, kt // TPC, h, (kt % TPC) * P:(kt % TPC + 1) * P]
                                        mm = pe.matmul(PS[:, h, 0:CH - r * P], keys, Q_st[:, c, h, r * P:CH],
                                                       start=True, stop=(kt < TPC * c))
                                        if kt >= TPC * c:
                                            mm = pe.matmul(PS[:, h, 0:P], ident_bf[:, :], mask_kq[:, :],
                                                           start=False, stop=True)
                                    mm.then_inc(scores_ready, 1)
                            elif kind == "values":
                                kt = step[2]
                                tile = TILE_AT[s] + kt
                                r = max(kt - TPC * c, 0)
                                if kt == 0:
                                    pe.wait_ge(out_evacuated, g * NCH + s + 1)
                                    if s < V_PIECES:
                                        pe.wait_ge(v_loaded[s], g * 16 + 16)
                                pe.wait_ge(exp_done, g * (2 * TILES) + 2 * tile + 4)
                                for h in range(GH):
                                    mm = pe.matmul(PS[h * VW:(h + 1) * VW, 6, r * P:CH], V_g[:, kt, h * VW:(h + 1) * VW],
                                                   probs[:, tile % P_SLOTS, h, 0:CH - r * P],
                                                   start=(kt == 0), stop=(kt == KEY_TILES[s] - 1))
                                mm.then_inc(values_done, 1)
                            elif kind == "out_turn":
                                pe.wait_ge(out_evacuated, g * NCH + s + 2)
                                pe.wait_ge(bank_free, g * N_BANK + BANK_AT[step] + 1)
                                for j in range(TPC):
                                    mm = pe.transpose(PS[:, 7, j * P:(j + 1) * P], o_t[:, s % 2, j * P:(j + 1) * P],
                                                      ident[:, :])
                                mm.then_inc(out_turned, 1)
                            elif kind == "burst":
                                half = s % HALF
                                pe.wait_ge(weighted, g * UNITS + BURST * (s + 1) + RING)
                                pe.wait_ge(bank_free, g * N_BANK + BANK_AT[step] + 1)
                                n_c = HD // TPC
                                for q in range(n_c):
                                    pe.matmul(PS[q * VW:(q + 1) * VW, 7, :], static_j[:, half, q * VW:(q + 1) * VW],
                                              q_rows[:, s % 2], start=True, stop=False)
                                for k in range(TPC):
                                    for q in range(n_c):
                                        i = q * TPC + k
                                        mm = pe.matmul(PS[q * VW:(q + 1) * VW, 7, :], sum_j[:, half, i, :],
                                                       state_q[:, i], start=False, stop=(k == TPC - 1))
                                mm.then_inc(burst_done, 1)

                @block.scalar
                def _(act):
                    with act.Fori(0, NG) as g:
                        for step in STEPS:
                            kind, s = step[0], step[1]
                            if kind == "scores":
                                tile = TILE_AT[s] + step[2]
                                r = max(step[2] - TPC * ORDER[s], 0)
                                act.wait_ge(values_done, g * TILES + tile + 1)
                                for pair in range(2):
                                    act.wait_ge(scores_ready, g * (2 * TILES) + 2 * tile + pair + 1)
                                    act.activation(probs[:, tile % P_SLOTS, 2 * pair:2 * pair + 2, 0:CH - r * P],
                                                   PS[:, 2 * pair:2 * pair + 2, 0:CH - r * P], ACT.Exp,
                                                   scale=SCALE).then_inc(exp_done, 1)
                            elif kind == "out_evac":
                                act.wait_ge(values_done, g * TILES + TILE_AT[s] + KEY_TILES[s] + P_SLOTS)
                                act.wait_ge(out_turned, g * NCH + s + 1)
                                act.activation(o_t[:, s % 2], PS[:, 6, :], ACT.Identity).then_inc(out_evacuated, 1)
                            elif kind == "burst":
                                act.wait_ge(burst_done, g * N_BURST + s + 2)
                                act.wait_ge(stp_stored[s % 2], g * (16 * N_BURST // 2) + 16 * (s // 2) + 16)
                                act.activation(stp_sb[:, s % 2], PS[:, 7, :], ACT.Identity).then_inc(bank_free, 1)

                @block.vector
                def _(dve):
                    dve.memset(K_st[KS:KR], 1.0).then_inc(ones_ready, 1)
                    with dve.Fori(0, NG) as g:
                        for step in STEPS:
                            kind, s = step[0], step[1]
                            if kind == "max":
                                c, n = ORDER[s], step[2]
                                hj, blk = n // (c + 1), n % (c + 1)
                                item = MAX_AT[s] + n
                                width = CH if blk < c else (hj % TPC + 1) * P
                                dve.wait_ge(max_ready, g * N_MAX + item + 1)
                                dve.tensor_reduce(pmax[:, s % 2, hj, blk:blk + 1], PS[:, 4 + item % 2, 0:width], AX.X,
                                                  ALU.max).then_inc(max_done, 1)
                            elif kind == "fold":
                                dve.wait_ge(max_done, g * N_MAX + MAX_AT[s] + MAXES[s] + 2)
                                dve.tensor_reduce(neg_max[:, s % 2, :], pmax[:, s % 2, :, 0:ORDER[s] + 1], AX.X, ALU.max,
                                                  negate=True).then_inc(folded, 1)
                            elif kind == "shift_split":
                                dve.wait_ge(shift_turned, g * NCH + s + 1)
                                dve.wait_ge(shift_loaded[s % 2], g * (32 * NCH // 2) + 32 * (s // 2) + 32)
                                turned = PS[0:GH * TPC, 7, 0:P]
                                dve.tensor_copy(shift[:, s % 2, 0, :], turned).then_inc(shift_high, 1)
                                dve.wait_ge(shift_high, g * NCH + s + 1)
                                dve.tensor_tensor(shift[:, s % 2, 1, :], turned, shift[:, s % 2, 0, :], ALU.subtract)\
                                    .then_inc(bank_free, 1)
                            elif kind == "out_norm":
                                dve.wait_ge(out_turned, g * NCH + s + 3)
                                dve.wait_ge(y_stored[s % 2], g * (16 * NCH // 2) + 16 * (s // 2) + 16)
                                sums = PS[:, 7, :].rearrange("p (j h v) -> p j h v", j=TPC, h=GH)
                                dve.reciprocal(rden[:, :, :], sums[:, :, :, HD]).then_inc(denom_ready, 1)
                                dve.wait_ge(denom_ready, g * NCH + s + 1)
                                dve.tensor_tensor(y_sb[:, s % 2].rearrange("p j (h v) -> p j h v", h=GH),
                                                  sums[:, :, :, 0:HD],
                                                  rden[:, :, :].unsqueeze(3).broadcast_to([P, TPC, GH, HD]), ALU.mult)\
                                    .then_inc(bank_free, 1)
                            elif kind == "unit":
                                b, i = s // BURST, s % BURST
                                col = (b % HALF) * HD + i
                                dve.wait_ge(u_made, g * UNITS + s + 2)
                                dve.wait_ge(weighted, g * UNITS + s + 1)
                                dve.tensor_tensor_scan(state[:, s % RING], retention[:, col:col + 1].broadcast_to([P, CH]),
                                                       hebb[:, s % RING], carry[:, col:col + 1], ALU.mult, ALU.add)\
                                    .then_inc(scanned, 1)

        fin = ExitStack()
        with fin:
            x1 = sb("x1", [P, NT, D], where=fin)
            xn2 = sb("xn2", [P, NT, D], where=fin)
            soft = sb("soft", [P, 2, TPC, D], where=fin)
            stp = sb("stp", [P, 2, HALF, CH], where=fin)
            xres = sb("xres", [P, 2, TPC, D], where=fin)
            diff = sb("diff", [P, 2, TPC, D], where=fin)
            y = sb("y", [P, 2, TPC, D], where=fin)
            y_t = sb("y_t", [P, 2, HALF, CH], where=fin)
            stats = sb("stats2", [P, TPC, 6], where=fin)
            mv = sb("mv2", [P, TPC, 2], where=fin)
            rstd = sb("rstd2", [P, 2 * TPC], where=fin)
            var_eps = sb("var_eps2", [P, TPC], where=fin)
            nmr = sb("nmr2", [P, 2 * TPC], where=fin)
            amax = sb("amax", [P, NCH], where=fin)
            small = sb("small", [P, 8], where=fin)
            scl = sb("scl", [P, 2, TPC * D], where=fin)
            magic = sb("magic", [P, 2, TPC * D], where=fin)
            moved = sb("moved", [P, 2, TPC * D], where=fin)
            r_bf = sb("r_bf", [P, 2, TPC, D], BF16, where=fin)
            r_t = sb("r_t", [P, 2, HALF, CH], BF16, where=fin)
            o_bf = sb("o_bf", [P, 2, TPC, D], BF16, where=fin)
            o_f = sb("o_f", [P, 2, TPC, D], where=fin)
            x_tiles = x.rearrange("(t p) n -> p t n", p=P)
            soft_tiles = y_soft.rearrange("g (t p) v -> g p t v", p=P)
            out_tiles = out.rearrange("(t p) n -> p t n", p=P)

            def tiles(it, par):
                return bass.ds(it * (2 * TPC) + par * TPC, TPC)

            with nc.Block() as block:
                @block.sync
                def _(sp):
                    with sp.Fori(0, NCH // 2) as it:
                        for par in range(2):
                            sp.wait_ge(x1_made, it * 2 + par + 1)
                            for g in range(NG):
                                sp.dma_start(soft[:, par, :, g * GH * HD:(g + 1) * GH * HD], soft_tiles[g, :, tiles(it, par), :])\
                                    .then_inc(soft_loaded[par], 16)
                            sp.dma_start(stp[:, par], y_stp_t[:, :, bass.ds(it * (2 * CH) + par * CH + PAD, CH)]
                                         .rearrange("f p t -> p f t")).then_inc(soft_loaded[par], 16)
                            sp.dma_start(xres[:, par], x_tiles[:, tiles(it, par), :]).then_inc(soft_loaded[par], 16)
                    with sp.Fori(0, NCH // 2) as it:
                        for par in range(2):
                            sp.wait_ge(out_made, it * 2 + par + 3)
                            sp.dma_start(out_tiles[:, tiles(it, par), :], o_f[:, par]).then_inc(out_stored[par], 16)
                    for par in range(2):
                        sp.wait_ge(out_stored[par], 16 * (NCH // 2 + 1))

                @block.gpsimd
                def _(pool):
                    with pool.Fori(0, NCH // 2) as it:
                        for par in range(2):
                            pool.wait_ge(soft_loaded[par], it * LOADS_PER_CHUNK + LOADS_PER_CHUNK)
                            pool.tensor_tensor(xres[:, par], xres[:, par],
                                               outb_sb[:, :].unsqueeze(1).broadcast_to([P, TPC, D]), ALU.add)\
                                .then_inc(xb_made, 1)
                        for par in range(2):
                            pool.wait_ge(diff_made, it * 2 + par + 1)
                            pool.tensor_tensor(diff[:, par].rearrange("p j (h v) -> p j h v", h=H),
                                               diff[:, par].rearrange("p j (h v) -> p j h v", h=H),
                                               alpha[:, tiles(it, par), :].unsqueeze(3).broadcast_to([P, TPC, H, HD]),
                                               ALU.mult).then_inc(diff_weighted, 1)
                        for par in range(2):
                            pool.wait_ge(var2, it * 2 + par + 1)
                            pool.tensor_tensor(rstd[:, par * TPC:(par + 1) * TPC], var_eps[:, :], neg_half[:, :], ALU.pow)\
                                .then_inc(rstd2, 1)
                    pool.wait_ge(peak_ready, 1)
                    pool.partition_all_reduce(small[:, 1:2], small[:, 0:1], P, bass.bass_isa.ReduceOp.max)\
                        .then_inc(amax_all, 1)
                    with pool.Fori(0, NCH // 2) as it:
                        for par in range(2):
                            pool.wait_ge(shifted, it * 2 + par + 1)
                            pool.wait_ge(r_turned, it * 2 + par + 1)
                            pool.tensor_tensor(r_bf[:, par].rearrange("p j n -> p (j n)"), moved[:, par], magic[:, par],
                                               ALU.subtract).then_inc(rounded, 1)
                        for par in range(2):
                            pool.wait_ge(ffn_biased, it * 2 + par + 3)
                            pool.wait_ge(out_stored[par], it * 16 + 16)
                            pool.tensor_tensor(o_f[:, par], x1[:, tiles(it, par), :], o_bf[:, par], ALU.add)\
                                .then_inc(out_made, 1)

                @block.tensor
                def _(pe):
                    with pe.Fori(0, NCH // 2) as it:
                        for par in range(2):
                            pe.wait_ge(soft_loaded[par], it * LOADS_PER_CHUNK + LOADS_PER_CHUNK)
                            pe.wait_ge(y_made, it * 2 + par + 1)
                            for half in range(HALF):
                                for j in range(TPC):
                                    mm = pe.transpose(PS[:, 2 * par + half, j * P:(j + 1) * P],
                                                      stp[:, par, half, j * P:(j + 1) * P], ident[:, :])
                            mm.then_inc(stp_turned, 1)
                        for par in range(2):
                            pe.wait_ge(y_made, it * 2 + par + 3)
                            pe.wait_ge(yt_evac, it * 4 + par * 2 + 2)
                            for c in range(HALF):
                                for j in range(TPC):
                                    mm = pe.transpose(PS[:, 4 + c, j * P:(j + 1) * P], y[:, par, j, c * P:(c + 1) * P],
                                                      ident[:, :])
                            mm.then_inc(y_turned, 1)
                            pe.wait_ge(yt_evac, it * 4 + par * 2 + 4)
                            pe.wait_ge(x1_made, it * 2 + par + 2)
                            for j in range(TPC):
                                for c in range(HALF):
                                    mm = pe.matmul(PS[:, 6 + j // 2, (j % 2) * D:(j % 2 + 1) * D],
                                                   y_t[:, par, c, j * P:(j + 1) * P], outw_sb[:, c, :],
                                                   start=(c == 0), stop=(c == HALF - 1))
                            mm.then_inc(attn_ready, 1)
                    with pe.Fori(0, NCH // 2) as it:
                        for par in range(2):
                            pe.wait_ge(rounded, it * 2 + par + 3)
                            pe.wait_ge(rt_evac, it * 2 + par + 1)
                            turned = PS[:, par, :].bitcast(BF16)
                            for c in range(HALF):
                                for j in range(TPC):
                                    mm = pe.transpose(turned[:, c * CH + j * P:c * CH + (j + 1) * P],
                                                      r_bf[:, par, j, c * P:(c + 1) * P], ident_bf[:, :])
                            mm.then_inc(r_turned, 1)
                        for par in range(2):
                            pe.wait_ge(rt_evac, it * 2 + par + 3)
                            pe.wait_ge(ffn_biased, it * 2 + par + 1)
                            for j in range(TPC):
                                for c in range(HALF):
                                    mm = pe.matmul(PS[:, 2 + 2 * par + j // 2, (j % 2) * D:(j % 2 + 1) * D],
                                                   r_t[:, par, c, j * P:(j + 1) * P], wq[:, c, :],
                                                   start=(c == 0), stop=(c == HALF - 1))
                            mm.then_inc(ffn_ready, 1)

                @block.scalar
                def _(act):
                    with act.Fori(0, NCH // 2) as it:
                        for par in range(2):
                            act.wait_ge(y_turned, it * 2 + par + 1)
                            act.wait_ge(attn_ready, it * 2 + par + 1)
                            for c in range(HALF):
                                act.activation(y_t[:, par, c, :], PS[:, 4 + c, :], ACT.Identity).then_inc(yt_evac, 1)
                        for par in range(2):
                            act.wait_ge(nmr2, it * 2 + par + 1)
                            for j in range(TPC):
                                ins = act.activation(xn2[:, bass.ds(it * (2 * TPC) + par * TPC + j, 1), :],
                                                     x1[:, bass.ds(it * (2 * TPC) + par * TPC + j, 1), :], ACT.Identity,
                                                     bias=nmr[:, par * TPC + j:par * TPC + j + 1],
                                                     scale=rstd[:, par * TPC + j:par * TPC + j + 1])
                            ins.then_inc(xn2_made, 1)
                    with act.Fori(0, NCH // 2) as it:
                        for par in range(2):
                            act.wait_ge(r_turned, it * 2 + par + 3)
                            act.wait_ge(ffn_ready, it * 2 + par + 1)
                            act.activation(r_t[:, par].rearrange("p c t -> p (c t)"), PS[:, par, :].bitcast(BF16),
                                           ACT.Identity).then_inc(rt_evac, 1)

                @block.vector
                def _(dve):
                    with dve.Fori(0, NCH // 2) as it:
                        for par in range(2):
                            dve.wait_ge(stp_turned, it * 2 + par + 1)
                            rec = [PS[:, 2 * par + f, :].rearrange("p (j i h) -> p j h i", j=TPC, i=HD)
                                   for f in range(HALF)]
                            sl = [slice(f * P, (f + 1) * P) for f in range(HALF)]
                            for f in range(HALF):
                                ins = dve.tensor_tensor(
                                    diff[:, par, :, sl[f]].rearrange("p j (h i) -> p j h i", h=HPH),
                                    rec[f], soft[:, par, :, sl[f]].rearrange("p j (h i) -> p j h i", h=HPH), ALU.subtract)
                            ins.then_inc(diff_made, 1)
                        for par in range(2):
                            dve.wait_ge(diff_weighted, it * 2 + par + 1)
                            for f in range(HALF):
                                rec = PS[:, 2 * par + f, :].rearrange("p (j i h) -> p j h i", j=TPC, i=HD)
                                cols = slice(f * P, (f + 1) * P)
                                ins = dve.tensor_tensor(
                                    y[:, par, :, cols].rearrange("p j (h i) -> p j h i", h=HPH), rec,
                                    diff[:, par, :, cols].rearrange("p j (h i) -> p j h i", h=HPH), ALU.subtract)
                            ins.then_inc(y_made, 1)
                        for par in range(2):
                            n1 = it * 2 + par + 1
                            dve.wait_ge(attn_ready, it * 2 + par + 3)
                            dve.wait_ge(xb_made, n1)
                            dve.tensor_tensor(x1[:, tiles(it, par), :],
                                              PS[:, 6:8, :].rearrange("p b (j n) -> p (b j) n", n=D), xres[:, par], ALU.add)\
                                .then_inc(x1_made, 1)
                            dve.wait_ge(x1_made, n1 + 2)
                            dve.sem_inc(beats, 1)
                            for j in range(TPC):
                                ins = dve.bn_stats(stats[:, j, :], x1[:, bass.ds(it * (2 * TPC) + par * TPC + j, 1), :]
                                                   .rearrange("p a n -> p (a n)"))
                            ins.then_inc(stats2, 1)
                            dve.wait_ge(stats2, n1)
                            dve.sem_inc(beats, 1)
                            for j in range(TPC):
                                ins = dve.bn_aggr(mv[:, j, :], stats[:, j, :])
                            ins.then_inc(mv2, 1)
                            dve.wait_ge(mv2, n1)
                            dve.tensor_scalar(var_eps[:, :], mv[:, :, 1], EPS, None, ALU.add).then_inc(var2, 1)
                            dve.wait_ge(rstd2, n1)
                            dve.scalar_tensor_tensor(out=nmr[:, par * TPC:(par + 1) * TPC], in0=mv[:, :, 0], scalar=-1.0,
                                                     in1=rstd[:, par * TPC:(par + 1) * TPC], op0=ALU.mult, op1=ALU.mult)\
                                .then_inc(nmr2, 1)
                        for par in range(2):
                            dve.wait_ge(xn2_made, it * 2 + par + 1)
                            dve.tensor_reduce(amax[:, bass.ds(it * 2 + par, 1)],
                                              xn2[:, tiles(it, par), :].rearrange("p j n -> p (j n)"), AX.X, ALU.max,
                                              apply_absolute_value=True).then_inc(amax_made, 1)
                    dve.wait_ge(amax_made, NCH)
                    dve.tensor_reduce(small[:, 0:1], amax[:, :], AX.X, ALU.max).then_inc(peak_ready, 1)
                    n_scale = 0

                    def link(ins):
                        nonlocal n_scale
                        n_scale += 1
                        ins.then_inc(scale_chain, 1)
                        dve.wait_ge(scale_chain, n_scale)

                    dve.wait_ge(amax_all, 1)
                    link(dve.tensor_scalar(small[:, 2:3], small[:, 1:2], 1e-12, None, ALU.max))
                    link(dve.reciprocal(small[:, 3:4], small[:, 2:3]))
                    link(dve.tensor_scalar(small[:, 4:5], small[:, 3:4], FP8_MAX, FP8_MAX, ALU.mult, ALU.min))
                    link(dve.reciprocal(small[:, 5:6], small[:, 4:5]))
                    link(dve.tensor_tensor(small[:, 6:7], small[:, 5:6], w_step[:, :], ALU.mult))
                    with dve.Fori(0, NCH // 2) as it:
                        for par in range(2):
                            n1 = it * 2 + par + 1
                            dve.wait_ge(rounded, n1)
                            dve.tensor_scalar(scl[:, par], xn2[:, tiles(it, par), :].rearrange("p j n -> p (j n)"),
                                              small[:, 4:5], FP8_MAX, ALU.mult, ALU.min).then_inc(scaled, 1)
                            dve.wait_ge(scaled, n1)
                            dve.tensor_scalar(magic[:, par].bitcast(I32), scl[:, par].bitcast(I32), EXPONENT_BITS, None,
                                              ALU.bitwise_and).then_inc(exponent_done, 1)
                            dve.wait_ge(exponent_done, n1)
                            dve.tensor_scalar(magic[:, par], magic[:, par], FP8_MIN_NORMAL, ROUND_TO_3_BITS, ALU.max,
                                              ALU.mult).then_inc(magic_done, 1)
                            dve.wait_ge(magic_done, n1)
                            dve.scalar_tensor_tensor(out=moved[:, par], in0=scl[:, par], scalar=-FP8_MAX, in1=magic[:, par],
                                                     op0=ALU.max, op1=ALU.add).then_inc(shifted, 1)
                        for par in range(2):
                            dve.wait_ge(ffn_ready, it * 2 + par + 3)
                            dve.wait_ge(out_made, it * 2 + par + 1)
                            dve.scalar_tensor_tensor(out=o_bf[:, par],
                                                     in0=PS[:, 2 + 2 * par:4 + 2 * par, :].rearrange("p b (j n) -> p (b j) n", n=D),
                                                     scalar=small[:, 6:7],
                                                     in1=ffnb_sb[:, :].unsqueeze(1).broadcast_to([P, TPC, D]),
                                                     op0=ALU.mult, op1=ALU.add).then_inc(ffn_biased, 1)


def kernel(L0_attn_x, L0_attn_Wqkv_w, L0_attn_Wqkv_b, L0_attn_out_w, L0_attn_out_b, L0_attn_W_static,
           L0_attn_Lambda_raw, L0_attn_Gamma, L0_attn_gate_w1, L0_attn_gate_b1, L0_attn_gate_w2,
           L0_attn_gate_b2, L0_ffn_weight, L0_ffn_bias):
    import numpy as np
    import concourse.bacc as bacc
    from concourse.bass_utils import run_bass_kernel_spmd

    def by_row(a):
        return np.asarray(a).reshape(HALF, HPH, HD, HD).transpose(1, 3, 0, 2).reshape(P, HALF * HD)

    inputs = {
        "x": np.asarray(L0_attn_x).reshape(T, D),
        "wqkv": np.asarray(L0_attn_Wqkv_w),
        "bqkv": np.asarray(L0_attn_Wqkv_b).reshape(6, P).T,
        "out_w": np.asarray(L0_attn_out_w),
        "out_b": np.asarray(L0_attn_out_b).reshape(1, D),
        "w_static": by_row(L0_attn_W_static),
        "lam": by_row(L0_attn_Lambda_raw),
        "gamma": by_row(L0_attn_Gamma),
        "gate_w1": np.asarray(L0_attn_gate_w1),
        "gate_b1": np.asarray(L0_attn_gate_b1).reshape(GATE, 1),
        "gate_w2": np.asarray(L0_attn_gate_w2),
        "gate_b2": np.asarray(L0_attn_gate_b2).reshape(1, H),
        "ffn_wt": np.asarray(L0_ffn_weight).T,
        "ffn_b": np.asarray(L0_ffn_bias).reshape(1, D),
    }
    inputs = {n: np.ascontiguousarray(a) for n, a in inputs.items()}
    nc = bacc.Bacc("TRN2", target_bir_lowering=False, num_devices=1)
    args = {n: nc.dram_tensor(n, a.shape, F32, kind="ExternalInput").ap() for n, a in inputs.items()}
    out = nc.dram_tensor("out", [T, D], F32, kind="ExternalOutput").ap()
    preln_attention_ffn_kernel(nc, out=out, **args)
    r = run_bass_kernel_spmd(nc, [inputs], core_ids=[0])
    return np.asarray(r.results[0]["out"]).reshape(1, T, D)
```

```python
from contextlib import ExitStack

import concourse.bass as bass
from concourse import mybir

F32 = mybir.dt.float32
BF16 = mybir.dt.bfloat16
I32 = mybir.dt.int32
ALU = mybir.AluOpType
ACT = mybir.ActivationFunctionType
AX = mybir.AxisListType

P = 128
T, D, H = 4096, 256, 16
HD = D // H
CH = 512
NCH = T // CH
TPC = CH // P
NT = T // P
GH = 4
NG = H // GH
HALF = 2
HPH = H // HALF
GATE = D // 2
VW = 32
SPLIT_Q = (0, 0, 1, 1, 0, 2)
SPLIT_K = (0, 1, 0, 1, 2, 0)
KS = len(SPLIT_Q) * HD
KR = KS + 2
SCALE = HD ** -0.5
MASKED = -10000.0 / SCALE
EPS = 1e-5
FP8_MAX = 448.0
FP8_MIN_NORMAL = 2.0 ** -6
ROUND_TO_3_BITS = 1.5 * 2.0 ** 20
EXPONENT_BITS = 0x7F800000

ORDER = (3, 4, 5, 6, 7, 2, 1, 0)
FIRST = ORDER[0] + 1
FIRST_USERS = 2
LONG_END = NCH - FIRST + 1
NEEDED_AT = tuple(next(s for s in range(NCH) if ORDER[s] >= k and (k >= FIRST or s >= FIRST_USERS)) for k in range(NCH))
KEY_TILES = tuple(TPC * (c + 1) for c in ORDER)
TILE_AT = tuple(sum(KEY_TILES[:s]) for s in range(NCH))
TILES = sum(KEY_TILES)
MAXES = tuple(GH * TPC * (c + 1) for c in ORDER)
MAX_AT = tuple(sum(MAXES[:s]) for s in range(NCH))
N_MAX = sum(MAXES)
LEAD = 4
UNITS = 64
BURST = 16
N_BURST = UNITS // BURST
BURST_PARTS = 5
P_SLOTS = 3
RING = 4
UNITS_PER_CHUNK = 7
STORES_PER_CHUNK = 16 * (3 + 3 + NG)
LOADS_PER_CHUNK = 16 * (2 + NG)
N_WEIGHTS = 13
PAD = 1024


def first_steps():
    return [("load", 0, 0), ("load", 0, 1), ("load_units", 0, 0)] \
        + [("max", 0, 0, n) for n in range(MAXES[0])] \
        + [("fold", 0, 0), ("shift_turn", 0, 0), ("shift_split", 0, 0)]


def group_steps(last):
    steps, late = [], []
    bank_open = False

    def emit(step, event=True):
        steps.append(step)
        if event:
            for x in late:
                x[0] -= 1
            while late and late[0][0] <= 0 and not bank_open:
                steps.append(late.pop(0)[1])

    def after(n, step):
        late.append([n, step])
        late.sort(key=lambda x: x[0])

    todo = [(0, s, n) for s in range(1, NCH) for n in range(MAXES[s])]
    deadlines = [(TILE_AT[s] - LEAD, MAX_AT[s] + MAXES[s] - MAXES[0]) for s in range(1, NCH)]
    if not last:
        todo += [(1, 0, n) for n in range(MAXES[0])]
        deadlines.append((TILES - LEAD, N_MAX))
    total = len(todo)

    def max_items(n):
        for _ in range(min(n, len(todo))):
            d, s, i = todo.pop(0)
            emit(("max", d, s, i))
            if i == MAXES[s] - 1:
                emit(("fold", d, s), event=False)
                after(5, ("shift_turn", d, s))
                after(8, ("shift_split", d, s))

    slots = []
    for b in range(N_BURST):
        slots += [("unit", b * BURST + i) for i in range(BURST)] + [None] * 3 + [("burst", b)]
    slots_total, slots_due = len(slots), 0.0
    light_from = TILE_AT[5]

    pending = None
    for s in range(NCH):
        for kt in range(KEY_TILES[s]):
            t = TILE_AT[s] + kt
            if s == 0 and 1 <= kt <= NCH - 2:
                emit(("load", 0, 1 + kt), event=False)
            if not last and s == 4 and kt == 4:
                emit(("load", 1, 0), event=False)
            if not last and s == 6 and kt == 1:
                emit(("load", 1, 1), event=False)
            done = total - len(todo)
            need = max([(m - done) / max(at - t, 1) for at, m in deadlines if m > done], default=0)
            n = min(int(-(-need // 1)), len(todo))
            slots_due += 0.35 if t < light_from else (slots_total - 0.35 * light_from) / (TILES - light_from - 2)
            while slots and slots_due >= 1 and not bank_open:
                slots_due -= 1
                item = slots.pop(0)
                if item and item[0] == "unit":
                    emit(("unit", 0, item[1]), event=False)
                elif item:
                    bank_open = True
                    for part in range(BURST_PARTS):
                        steps.append(("burst", 0, item[1], part))
                        if part == BURST_PARTS - 1:
                            bank_open = False
                        max_items(2)
            done = total - len(todo) - done
            n = max(n - done, 0)
            emit(("scores", 0, s, kt, 0))
            max_items(n // 3)
            emit(("scores", 0, s, kt, 1))
            max_items((n + 1) // 3)
            if pending:
                emit(("values", 0) + pending)
                if pending[1] == KEY_TILES[pending[0]] - 1:
                    emit(("out_evac", 0, pending[0]), event=False)
                    after(5, ("out_turn", 0, pending[0]))
                    after(9, ("out_norm", 0, pending[0]))
            pending = (s, kt)
            max_items(n - n // 3 - (n + 1) // 3)
    assert not slots and not todo
    emit(("values", 0) + pending)
    emit(("out_evac", 0, NCH - 1), event=False)
    steps += [x[1] for x in late]
    steps += [("out_turn", 0, NCH - 1), ("out_norm", 0, NCH - 1)]
    return steps


def bank_uses(steps):
    uses = [x for x in steps if x[0] in ("shift_turn", "out_turn") or x[0] == "burst" and x[3] == 0]
    return {x[:3]: n for n, x in enumerate(uses)}


FIRST_STEPS, STEPS, LAST_STEPS = first_steps(), group_steps(False), group_steps(True)
BANK_FIRST = bank_uses(FIRST_STEPS)
N_BANK = len(bank_uses(STEPS))
BANK_STEPS = {x: n + len(BANK_FIRST) for x, n in bank_uses(STEPS).items()}
BANK_LAST = {x: n + len(BANK_FIRST) for x, n in bank_uses(LAST_STEPS).items()}


def preln_attention_ffn_kernel(nc, x, wqkv, bqkv, out_w, out_b, w_static, lam, gamma, gate_w1,
                               gate_b1, gate_w2, gate_b2, ffn_wt, ffn_b, out):
    ctx = ExitStack()
    with ctx:
        def sb(name, shape, dt=F32, where=ctx):
            return where.enter_context(nc.sbuf_tensor(name, shape, dt))

        def sem(name):
            return ctx.enter_context(nc.semaphore(name))

        PS = ctx.enter_context(nc.psum_tensor("PS", [P, 8, CH], F32))

        qk_parts = nc.dram_tensor("qk_parts", [3, 2 * D, T], BF16).ap()
        qkv_t = nc.dram_tensor("qkv_t", [3 * D, T], F32).ap()
        v_rows = nc.dram_tensor("v_rows", [NG, P, NT, GH * VW], F32).ap()
        y_soft = nc.dram_tensor("y_soft", [NG, T, GH * HD], F32).ap()
        y_stp_t = nc.dram_tensor("y_stp_t", [HALF, P, PAD + T], F32).ap()

        ident = sb("ident", [P, P])
        ident_bf = sb("ident_bf", [P, P], BF16)
        mask_qk = sb("mask_qk", [P, P], BF16)
        mask_kq = sb("mask_kq", [P, P], BF16)
        same_head = sb("same_head", [P, HPH])
        retention = sb("retention", [P, HALF * HD])
        sum_j = sb("sum_j", [P, HALF, HD, VW])
        static_j = sb("static_j", [P, HALF, P])
        carry = sb("carry", [P, HALF * HD])
        alpha = sb("alpha", [P, NT, H])
        outw_sb = sb("outw_sb", [P, HALF, D])
        outb_sb = sb("outb_sb", [P, D])
        ffnb_sb = sb("ffnb_sb", [P, D])
        wq = sb("wq", [P, HALF, D], BF16)
        w_step = sb("w_step", [P, 1])

        neg_half = sb("neg_half", [P, TPC])

        weights_loaded = sem("weights_loaded")
        beats = sem("beats")


        credits = {}

        def free_sem(name, credit):
            s = sem(name)
            credits[name] = (s, credit)
            return s

        x_loaded = [sem(f"x_loaded{k}") for k in range(2)]
        stored = [free_sem(f"stored{k}", STORES_PER_CHUNK) for k in range(2)]
        stats_done, mv_done, rstd_done = sem("stats_done"), sem("mv_done"), sem("rstd_done")
        var_done, var2 = sem("var_done"), sem("var2")
        xn_ready = free_sem("xn_ready", 2)
        xnt_ready = free_sem("xnt_ready", 4)
        xnt_evac = free_sem("xnt_evac", 2)
        proj_ready = free_sem("proj_ready", 2 * UNITS_PER_CHUNK)
        proj_evac = free_sem("proj_evac", UNITS_PER_CHUNK)
        high_done, rest1_done, mid_done = sem("high_done"), sem("rest1_done"), sem("mid_done")
        low_done = sem("low_done")
        vrow_ready, vrow_evac = sem("vrow_ready"), free_sem("vrow_evac", 2)
        z_ready, z_evac = free_sem("z_ready", 2), free_sem("z_evac", 1)
        dve_setup, act_setup, pool_setup = sem("dve_setup"), sem("act_setup"), sem("pool_setup")
        vaug_ready = sem("vaug_ready")
        k_first_loaded, v_first_loaded = sem("k_first_loaded"), sem("v_first_loaded")
        k_loaded = [sem(f"k_loaded{c}") for c in range(NCH)]
        q_loaded = [sem(f"q_loaded{c}") for c in range(NCH)]
        v_loaded = [sem(f"v_loaded{c}") for c in range(NCH)]
        max_ready, max_done = sem("max_ready"), free_sem("max_done", 2)
        folded, shift_turned, shift_high = sem("folded"), sem("shift_turned"), sem("shift_high")
        shift_loaded = [free_sem(f"shift_loaded{k}", 32) for k in range(2)]
        scores_ready, exp_done = sem("scores_ready"), free_sem("exp_done", 2)
        values_done = free_sem("values_done", P_SLOTS)
        out_evacuated, out_turned = free_sem("out_evacuated", 1), free_sem("out_turned", 2)
        denom_ready, ones_ready = sem("denom_ready"), sem("ones_ready")
        y_stored = [free_sem(f"y_stored{k}", 16) for k in range(2)]
        bank_free = free_sem("bank_free", 1)
        kq_loaded = [sem(f"kq_loaded{k}") for k in range(2)]
        vexp_loaded = [sem(f"vexp_loaded{k}") for k in range(RING)]
        u_made, scanned = sem("u_made"), free_sem("scanned", 1)
        carried, weighted = sem("carried"), free_sem("weighted", HALF * HD)
        burst_done = free_sem("burst_done", 1)
        stp_stored = [free_sem(f"stp_stored{k}", 16) for k in range(2)]
        soft_loaded = [sem(f"soft_loaded{k}") for k in range(2)]
        stp_turned, diff_made, diff_weighted = sem("stp_turned"), sem("diff_made"), sem("diff_weighted")
        xb_made, y_made, y_turned = sem("xb_made"), free_sem("y_made", 2), sem("y_turned")
        yt_evac, attn_ready, x1_made = free_sem("yt_evac", 2), free_sem("attn_ready", 2), free_sem("x1_made", 2)
        stats2, mv2, rstd2, nmr2 = sem("stats2"), sem("mv2"), sem("rstd2"), sem("nmr2")
        xn2_made, amax_made, amax_all = sem("xn2_made"), sem("amax_made"), sem("amax_all")
        scale_chain, peak_ready = sem("scale_chain"), sem("peak_ready")
        scaled, exponent_done, magic_done = sem("scaled"), sem("exponent_done"), sem("magic_done")
        shifted, rounded, r_turned = sem("shifted"), free_sem("rounded", 2), free_sem("r_turned", 2)
        rt_evac, ffn_ready = free_sem("rt_evac", 2), free_sem("ffn_ready", 2)
        ffn_biased, out_made = free_sem("ffn_biased", 2), free_sem("out_made", 2)
        out_stored = [free_sem(f"out_stored{k}", 16) for k in range(2)]

        with nc.Block() as block:
            @block.gpsimd
            def _(pool):
                for s, n in credits.values():
                    pool.sem_inc(s, n)

        pro = ExitStack()
        with pro:
            wqkv_sb = sb("wqkv_sb", [P, HALF, 3 * D], where=pro)
            bqkv_sb = sb("bqkv_sb", [P, 6], where=pro)
            w1_sb = sb("w1_sb", [P, HALF, GATE], where=pro)
            b1_sb = sb("b1_sb", [P, 1], where=pro)
            w2_sb = sb("w2_sb", [P, H], where=pro)
            b2_sb = sb("b2_sb", [P, H], where=pro)
            lam_sb = sb("lam_sb", [P, HALF * HD], where=pro)
            gamma_sb = sb("gamma_sb", [P, HALF * HD], where=pro)
            wst_sb = sb("wst_sb", [P, HALF * HD], where=pro)
            ffnw_sb = sb("ffnw_sb", [P, HALF * D], where=pro)
            wtmp = sb("wtmp", [P, 3, HALF * D], where=pro)
            wsmall = sb("wsmall", [P, 8], where=pro)
            xin = sb("xin", [P, 2, TPC, D], where=pro)
            xn = sb("xn", [P, 2, TPC, D], where=pro)
            stats = sb("stats", [P, TPC, 6], where=pro)
            mv = sb("mv", [P, TPC, 2], where=pro)
            rstd = sb("rstd", [P, TPC], where=pro)
            var_eps = sb("var_eps", [P, TPC], where=pro)
            xn_t = sb("xn_t", [P, 2, HALF, CH], where=pro)
            proj = sb("proj", [P, 2, 6, CH], where=pro)
            gate_t = sb("gate_t", [P, 2, CH], where=pro)
            parts = sb("parts", [P, 2, 3, 4, CH], BF16, where=pro)
            rest = sb("rest", [P, 2, 4, CH], where=pro)
            vaug = sb("vaug", [P, 2, TPC, H, VW], where=pro)
            z = sb("z", [P, NT, H], where=pro)
            x_tiles = x.rearrange("(t p) n -> p t n", p=P)

            with nc.Block() as block:
                @block.sync
                def _(sp):
                    with sp.Fori(0, NCH // 2) as it:
                        for par in range(2):
                            sp.wait_ge(xn_ready, it * 2 + par + 1)
                            sp.dma_start(xin[:, par], x_tiles[:, bass.ds(it * (2 * TPC) + par * TPC, TPC), :])\
                                .then_inc(x_loaded[par], 16)
                        for par in range(2):
                            rows = bass.ds(it * (2 * CH) + par * CH, CH)
                            sp.wait_ge(proj_evac, it * 14 + par * 7 + 13)
                            for w in range(3):
                                sp.dma_start(qkv_t[w * D:(w + 1) * D, rows].rearrange("(u p) t -> p u t", p=P),
                                             proj[:, par, 2 * w:2 * w + 2, :]).then_inc(stored[par], 16)
                            for n, (made, k) in enumerate([(high_done, 1), (mid_done, 1), (low_done, 1)]):
                                sp.wait_ge(made, it * 2 + par + k)
                                sp.sem_inc(beats, 1)
                                sp.dma_start(qk_parts[n, :, rows].rearrange("(u p) t -> p u t", p=P),
                                             parts[:, par, n, :, :]).then_inc(stored[par], 16)
                            sp.wait_ge(vrow_evac, it * 4 + par * 2 + 4)
                            for g in range(NG):
                                sp.dma_start(
                                    v_rows[g, :, bass.ds(it * (2 * TPC) + par * TPC, TPC), :],
                                    vaug[:, par, :, g * GH:(g + 1) * GH, :].rearrange("p t h v -> p t (h v)"),
                                ).then_inc(stored[par], 16)
                    for par in range(2):
                        sp.wait_ge(stored[par], STORES_PER_CHUNK * (NCH // 2 + 1))

                @block.gpsimd
                def _(pool):
                    pool.memset(ident[:, :], 0.0).then_inc(pool_setup, 1)
                    pool.memset(mask_qk[:, :], 0.0).then_inc(pool_setup, 1)
                    pool.memset(mask_kq[:, :], 0.0).then_inc(pool_setup, 1)
                    pool.memset(same_head[:, :], 1.0).then_inc(pool_setup, 1)
                    pool.wait_ge(pool_setup, 4)
                    pool.affine_select(out=ident[:, :], in_=ident[:, :], compare_op=ALU.not_equal, fill=1.0,
                                       base=0, pattern=[[-1, P]], channel_multiplier=1).then_inc(pool_setup, 1)
                    pool.affine_select(out=mask_qk[:, :], in_=mask_qk[:, :], compare_op=ALU.is_ge, fill=MASKED,
                                       base=0, pattern=[[-1, P]], channel_multiplier=1).then_inc(pool_setup, 1)
                    pool.affine_select(out=mask_kq[:, :], in_=mask_kq[:, :], compare_op=ALU.is_ge, fill=MASKED,
                                       base=0, pattern=[[1, P]], channel_multiplier=-1).then_inc(pool_setup, 1)
                    pool.affine_select(out=same_head[:, :], in_=same_head[:, :], compare_op=ALU.is_ge, fill=0.0,
                                       base=0, pattern=[[-HD, HPH]], channel_multiplier=1).then_inc(pool_setup, 1)
                    pool.wait_ge(pool_setup, 8)
                    pool.affine_select(out=same_head[:, :], in_=same_head[:, :], compare_op=ALU.is_ge, fill=0.0,
                                       base=HD - 1, pattern=[[HD, HPH]], channel_multiplier=-1)\
                        .then_inc(pool_setup, 1)
                    pool.tensor_copy(ident_bf[:, :], ident[:, :]).then_inc(pool_setup, 1)
                    for par in range(2):
                        pool.memset(vaug[:, par, :, :, HD:HD + 1], 1.0).then_inc(vaug_ready, 1)
                        pool.memset(vaug[:, par, :, :, HD + 1:VW], 0.0).then_inc(vaug_ready, 1)
                    pool.memset(neg_half[:, :], -0.5).then_inc(pool_setup, 1)
                    pool.wait_ge(pool_setup, 11)
                    with pool.Fori(0, NCH // 2) as it:
                        for par in range(2):
                            pool.wait_ge(var_done, it * 2 + par + 1)
                            pool.tensor_tensor(rstd[:, :], var_eps[:, :], neg_half[:, :], ALU.pow).then_inc(rstd_done, 1)
                            pool.wait_ge(mid_done, it * 2 + par + 1)
                            pool.tensor_tensor(parts[:, par, 2], rest[:, par], parts[:, par, 1], ALU.subtract)\
                                .then_inc(low_done, 1)
                    pool.wait_ge(dve_setup, 1)
                    pool.partition_all_reduce(wsmall[:, 1:2], wsmall[:, 0:1], P, bass.bass_isa.ReduceOp.max)\
                        .then_inc(pool_setup, 1)

                @block.tensor
                def _(pe):
                    pe.wait_ge(pool_setup, 10)
                    pe.wait_ge(weights_loaded, 16 * N_WEIGHTS)
                    with pe.Fori(0, NCH // 2) as it:
                        for par in range(2):
                            pe.wait_ge(xn_ready, it * 2 + par + 3)
                            for c in range(HALF):
                                pe.wait_ge(xnt_evac, it * 4 + par * 2 + c + 1)
                                for j in range(TPC):
                                    mm = pe.transpose(PS[:, c, j * P:(j + 1) * P],
                                                      xn[:, par, j, c * P:(c + 1) * P], ident[:, :])
                                mm.then_inc(xnt_ready, 1)
                            pe.wait_ge(xnt_evac, it * 4 + par * 2 + 4)
                            for u in range(UNITS_PER_CHUNK):
                                pe.wait_ge(proj_evac, it * 14 + par * 7 + (u + 5 if u < 3 else u + 4 if u > 3 else 4))
                                for c in range(HALF):
                                    w = wqkv_sb[:, c, u * P:(u + 1) * P] if u < 6 else w1_sb[:, c, :]
                                    mm = pe.matmul(PS[:, 2 + u % 4, :], w, xn_t[:, par, c, :],
                                                   start=(c == 0), stop=(c == HALF - 1))
                                mm.then_inc(proj_ready, 1)
                            pe.wait_ge(proj_evac, it * 14 + par * 7 + 13)
                            for half in range(HALF):
                                pe.wait_ge(vrow_evac, it * 4 + par * 2 + half + 2)
                                for j in range(TPC):
                                    mm = pe.transpose(PS[:, 7, j * P:(j + 1) * P],
                                                      proj[:, par, 4 + half, j * P:(j + 1) * P], ident[:, :])
                                mm.then_inc(vrow_ready, 1)
                            pe.wait_ge(proj_evac, it * 14 + par * 7 + 14)
                            pe.wait_ge(z_evac, it * 2 + par + 1)
                            for j in range(TPC):
                                mm = pe.matmul(PS[:, 6, j * H:(j + 1) * H], gate_t[:, par, j * P:(j + 1) * P],
                                               w2_sb[:, :], start=True, stop=True)
                            mm.then_inc(z_ready, 1)

                @block.scalar
                def _(act):
                    for dst, src in [
                            (wqkv_sb[:, :, :], wqkv.rearrange("(c p) n -> p c n", p=P)),
                            (bqkv_sb[:, :], bqkv),
                            (w1_sb[:, :, :], gate_w1.rearrange("(c p) n -> p c n", p=P)),
                            (b1_sb[:, :], gate_b1), (w2_sb[:, :], gate_w2),
                            (b2_sb[:, :], gate_b2.broadcast_to([P, H])),
                            (lam_sb[:, :], lam), (gamma_sb[:, :], gamma), (wst_sb[:, :], w_static),
                            (ffnw_sb[:, :].rearrange("p (c n) -> p c n", c=HALF),
                             ffn_wt.rearrange("(c p) n -> p c n", p=P)),
                            (outw_sb[:, :, :], out_w.rearrange("(c p) n -> p c n", p=P)),
                            (outb_sb[:, :], out_b.broadcast_to([P, D])),
                            (ffnb_sb[:, :], ffn_b.broadcast_to([P, D]))]:
                        act.dma_start(dst, src).then_inc(weights_loaded, 16)
                    act.wait_ge(weights_loaded, 16 * N_WEIGHTS)
                    act.wait_ge(vaug_ready, 4)
                    with act.Fori(0, NCH // 2) as it:
                        for par in range(2):
                            for c in range(HALF):
                                act.wait_ge(xnt_ready, it * 4 + par * 2 + c + 5)
                                act.wait_ge(proj_ready, it * 14 + par * 7 + 7)
                                act.activation(xn_t[:, par, c, :], PS[:, c, :], ACT.Identity).then_inc(xnt_evac, 1)
                            act.wait_ge(stored[par], it * STORES_PER_CHUNK + STORES_PER_CHUNK)
                            for u in range(6):
                                act.wait_ge(proj_ready, it * 14 + par * 7 + u + 15)
                                act.activation(proj[:, par, u, :], PS[:, 2 + u % 4, :], ACT.Identity,
                                               bias=bqkv_sb[:, u:u + 1]).then_inc(proj_evac, 1)
                            act.wait_ge(proj_ready, it * 14 + par * 7 + 21)
                            act.wait_ge(z_ready, it * 2 + par + 1)
                            act.activation(gate_t[:, par, :], PS[:, 4, :], ACT.Gelu, bias=b1_sb[:, 0:1])\
                                .then_inc(proj_evac, 1)
                            for half in range(HALF):
                                act.wait_ge(vrow_ready, it * 4 + par * 2 + half + 1)
                                act.activation(vaug[:, par, :, half * HPH:(half + 1) * HPH, 0:HD],
                                               PS[:, 7, :].rearrange("p (j h d) -> p j h d", j=TPC, h=HPH),
                                               ACT.Identity).then_inc(vrow_evac, 1)
                            act.wait_ge(z_ready, it * 2 + par + 3)
                            act.activation(z[:, bass.ds(it * (2 * TPC) + par * TPC, TPC), :],
                                           PS[:, 6, 0:TPC * H].rearrange("p (j h) -> p j h", j=TPC),
                                           ACT.Identity).then_inc(z_evac, 1)
                    act.activation(lam_sb[:, :], lam_sb[:, :], ACT.Exp, scale=-1.0).then_inc(act_setup, 1)
                    act.wait_ge(dve_setup, 2)
                    act.activation(alpha[:, :, :], z[:, :, :], ACT.Exp, scale=-1.0).then_inc(act_setup, 1)

                @block.vector
                def _(dve):
                    with dve.Fori(0, NCH // 2) as it:
                        for par in range(2):
                            c1 = it * 2 + par + 1
                            dve.wait_ge(x_loaded[par], it * 16 + 16)
                            for j in range(TPC):
                                ins = dve.bn_stats(stats[:, j, :], xin[:, par, j, :])
                            ins.then_inc(stats_done, 1)
                            dve.wait_ge(stats_done, c1)
                            dve.sem_inc(beats, 1)
                            for j in range(TPC):
                                ins = dve.bn_aggr(mv[:, j, :], stats[:, j, :])
                            ins.then_inc(mv_done, 1)
                            dve.wait_ge(mv_done, c1)
                            dve.tensor_scalar(var_eps[:, :], mv[:, :, 1], EPS, None, ALU.add).then_inc(var_done, 1)
                            dve.wait_ge(rstd_done, c1)
                            dve.wait_ge(xnt_ready, it * 4 + par * 2 + 2)
                            for j in range(TPC):
                                ins = dve.tensor_scalar(xn[:, par, j, :], xin[:, par, j, :], mv[:, j, 0:1],
                                                        rstd[:, j:j + 1], ALU.subtract, ALU.mult)
                            ins.then_inc(xn_ready, 1)
                            dve.wait_ge(proj_evac, it * 14 + par * 7 + 11)
                            dve.wait_ge(stored[par], it * STORES_PER_CHUNK + STORES_PER_CHUNK)
                            dve.tensor_copy(parts[:, par, 0], proj[:, par, 0:4]).then_inc(high_done, 1)
                            dve.wait_ge(high_done, c1)
                            dve.tensor_tensor(rest[:, par], proj[:, par, 0:4], parts[:, par, 0], ALU.subtract)\
                                .then_inc(rest1_done, 1)
                            dve.wait_ge(rest1_done, c1)
                            dve.tensor_copy(parts[:, par, 1], rest[:, par]).then_inc(mid_done, 1)
                    dve.tensor_reduce(wsmall[:, 0:1], ffnw_sb[:, :], AX.X, ALU.max, apply_absolute_value=True)\
                        .then_inc(dve_setup, 1)
                    dve.wait_ge(z_evac, NCH + 1)
                    dve.tensor_tensor(z[:, :, :], z[:, :, :], b2_sb[:, :].unsqueeze(1).broadcast_to([P, NT, H]),
                                      ALU.add).then_inc(dve_setup, 1)
                    n_setup = 2

                    def link(ins):
                        nonlocal n_setup
                        n_setup += 1
                        ins.then_inc(dve_setup, 1)
                        dve.wait_ge(dve_setup, n_setup)

                    dve.wait_ge(act_setup, 1)
                    link(dve.tensor_scalar(lam_sb[:, :], lam_sb[:, :], 1.0, None, ALU.add))
                    link(dve.reciprocal(lam_sb[:, :], lam_sb[:, :]))
                    link(dve.tensor_scalar(retention[:, :], lam_sb[:, :], -1.0, 1.0, ALU.mult, ALU.add))
                    link(dve.memset(carry[:, :], 0.0))
                    link(dve.memset(sum_j[:, :, :, :], 0.0))
                    link(dve.tensor_scalar(gamma_sb[:, :], gamma_sb[:, :], SCALE, None, ALU.mult))
                    n_c = HD // TPC
                    heads = same_head[:, :].unsqueeze(1).broadcast_to([P, HALF * n_c, HPH])
                    for k in range(TPC):
                        link(dve.tensor_tensor(
                            sum_j[:, :, :, :].rearrange("p f (c k) v -> p (f c) k v", k=TPC)[:, :, k, k * HPH:(k + 1) * HPH],
                            heads,
                            gamma_sb[:, :].rearrange("p (c k) -> p c k", k=TPC)[:, :, k:k + 1]
                            .broadcast_to([P, HALF * n_c, HPH]), ALU.mult))
                        link(dve.tensor_tensor(
                            static_j[:, :, :].rearrange("p f (c k v) -> p (f c) k v", c=n_c, k=TPC)[:, :, k, :],
                            heads,
                            wst_sb[:, :].rearrange("p (c k) -> p c k", k=TPC)[:, :, k:k + 1]
                            .broadcast_to([P, HALF * n_c, HPH]), ALU.mult))
                    dve.wait_ge(act_setup, 2)
                    link(dve.tensor_scalar(alpha[:, :, :], alpha[:, :, :], 1.0, None, ALU.add))
                    link(dve.reciprocal(alpha[:, :, :], alpha[:, :, :]))
                    dve.wait_ge(pool_setup, 12)
                    link(dve.tensor_scalar(wsmall[:, 2:3], wsmall[:, 1:2], 1e-12, None, ALU.max))
                    link(dve.reciprocal(wsmall[:, 3:4], wsmall[:, 2:3]))
                    link(dve.tensor_scalar(wsmall[:, 4:5], wsmall[:, 3:4], FP8_MAX, FP8_MAX, ALU.mult, ALU.min))
                    link(dve.reciprocal(w_step[:, :], wsmall[:, 4:5]))
                    link(dve.tensor_scalar(wtmp[:, 0], ffnw_sb[:, :], wsmall[:, 4:5], FP8_MAX, ALU.mult, ALU.min))
                    link(dve.tensor_scalar(wtmp[:, 1].bitcast(I32), wtmp[:, 0].bitcast(I32), EXPONENT_BITS, None,
                                           ALU.bitwise_and))
                    link(dve.tensor_scalar(wtmp[:, 1], wtmp[:, 1], FP8_MIN_NORMAL, ROUND_TO_3_BITS, ALU.max, ALU.mult))
                    link(dve.scalar_tensor_tensor(out=wtmp[:, 2], in0=wtmp[:, 0], scalar=-FP8_MAX, in1=wtmp[:, 1],
                                                  op0=ALU.max, op1=ALU.add))
                    link(dve.tensor_tensor(wq[:, :, :].rearrange("p c n -> p (c n)"), wtmp[:, 2], wtmp[:, 1],
                                           ALU.subtract))

        att = ExitStack()
        with att:
            K_st = sb("K_st", [KR, NCH, GH, CH], BF16, where=att)
            Q_st = sb("Q_st", [KR, NCH, GH, CH], BF16, where=att)
            V_g = sb("V_g", [P, NT, GH * VW], where=att)
            K_first = sb("K_first", [KR, FIRST, GH, CH], BF16, where=att)
            V_first = sb("V_first", [P, FIRST * TPC, GH * VW], where=att)
            probs = sb("probs", [P, P_SLOTS, GH, CH], where=att)
            pmax = sb("pmax", [P, 2, GH * TPC, NCH], where=att)
            neg_max = sb("neg_max", [P, 2, GH * TPC], where=att)
            shift = sb("shift", [GH * TPC, 2, 2, P], BF16, where=att)
            o_t = sb("o_t", [P, 2, CH], where=att)
            rden = sb("rden", [P, TPC, GH], where=att)
            y_sb = sb("y_sb", [P, 2, TPC, GH * HD], where=att)
            k_rows = sb("k_rows", [P, 2, CH], where=att)
            q_rows = sb("q_rows", [P, 2, CH], where=att)
            v_exp = sb("v_exp", [P, RING, CH], where=att)
            state = sb("state", [P, BURST, CH], where=att)
            stp_sb = sb("stp_sb", [P, 2, CH], where=att)

            with nc.Block() as block:
                @block.sync
                def _(sp):
                    def load_parts(g, stack, chunk, first_row, split, loaded):
                        for n, part in enumerate(split):
                            sp.dma_start(
                                stack[n * HD:(n + 1) * HD, chunk],
                                qk_parts[part, bass.ds(g * (GH * HD) + first_row, GH * HD),
                                         chunk * CH:(chunk + 1) * CH].rearrange("(h d) t -> d h t", d=HD),
                            ).then_inc(loaded, 16)

                    def load_values(g, values, first, n, loaded):
                        sp.dma_start(values[:, first:first + n, :],
                                     v_rows[bass.ds(g, 1), :, first:first + n, :].rearrange("g p t v -> (g p) t v"))\
                            .then_inc(loaded, 16)

                    def load_kq(g, b):
                        cols = bass.ds(g * (2 * CH) + (b // HALF) * CH, CH)
                        half = b % HALF
                        for dst, first in ((k_rows, D), (q_rows, 0)):
                            sp.dma_start(dst[:, b % 2], qkv_t[first + half * P:first + (half + 1) * P, cols])\
                                .then_inc(kq_loaded[b % 2], 16)

                    def load_v_exp(g, n):
                        b, i = n // BURST, n % BURST
                        first = 2 * D + (b % HALF) * P
                        v = qkv_t[first:first + P, bass.ds(g * (2 * CH) + (b // HALF) * CH, CH)]
                        sp.dma_start(v_exp[:, n % RING], v.rearrange("(h i) t -> h i t", i=HD)[:, i, :]
                                     .unsqueeze(1).broadcast_to([HPH, HD, CH])).then_inc(vexp_loaded[n % RING], 16)

                    def walk(group, steps, bank, last):
                        for step in steps:
                            kind, g, s = step[0], group + step[1], step[2]
                            if kind == "load":
                                c = ORDER[s]
                                if s == 0:
                                    sp.wait_ge(values_done, g * TILES + (TILE_AT[FIRST_USERS] - TILES + P_SLOTS)
                                               if steps is not FIRST_STEPS else P_SLOTS)
                                    for k in range(FIRST):
                                        load_parts(g, K_first, k, D, SPLIT_K, k_first_loaded)
                                    load_parts(g, Q_st, c, 0, SPLIT_Q, q_loaded[c])
                                    load_values(g, V_first, 0, FIRST * TPC, v_first_loaded)
                                else:
                                    if s == 1 and steps is not FIRST_STEPS:
                                        sp.wait_ge(values_done, g * TILES + (TILE_AT[LONG_END] - TILES + P_SLOTS))
                                    if s == 2:
                                        sp.wait_ge(values_done, g * TILES + P_SLOTS)
                                    new = [k for k in range(c + 1) if NEEDED_AT[k] == s]
                                    load_parts(g, Q_st, c, 0, SPLIT_Q, q_loaded[c])
                                    for k in new[::-1]:
                                        load_parts(g, K_st, k, D, SPLIT_K, k_loaded[k])
                                        load_values(g, V_g, k * TPC, TPC, v_loaded[k])
                            elif kind == "load_units":
                                load_kq(g, 0)
                                for n in range(RING - 1):
                                    load_v_exp(g, n)
                            elif kind == "unit":
                                if s % BURST == 0 and not (last and s // BURST + 1 == N_BURST):
                                    sp.wait_ge(burst_done, g * N_BURST + s // BURST + 1)
                                    b = s // BURST + 1
                                    load_kq(g + b // N_BURST, b % N_BURST)
                                n = s + RING - 1
                                if not (last and n >= UNITS):
                                    sp.wait_ge(scanned, g * UNITS + s + 1)
                                    load_v_exp(g + n // UNITS, n % UNITS)
                            elif kind == "shift_split":
                                sp.wait_ge(bank_free, group * N_BANK + bank["shift_turn", step[1], s] + 2)
                                for k in range(2):
                                    sp.dma_start(Q_st[KS + k:KS + k + 1, ORDER[s]].rearrange("a h (j t) -> a (h j) t", t=P),
                                                 shift[:, s % 2, k, :]).then_inc(shift_loaded[s % 2], 16)
                            elif kind == "out_norm":
                                sp.wait_ge(bank_free, group * N_BANK + bank["out_turn", step[1], s] + 2)
                                sp.sem_inc(beats, 1)
                                c = ORDER[s]
                                sp.dma_start(y_soft[bass.ds(g, 1), c * CH:(c + 1) * CH, :]
                                             .rearrange("g (j p) v -> p (g j) v", p=P), y_sb[:, s % 2])\
                                    .then_inc(y_stored[s % 2], 16)
                            elif kind == "burst" and step[3] == BURST_PARTS - 1:
                                sp.wait_ge(bank_free, group * N_BANK + bank["burst", step[1], s] + 2)
                                sp.sem_inc(beats, 1)
                                sp.dma_start(y_stp_t[s % HALF, :, bass.ds(g * (2 * CH) + (s // HALF) * CH + PAD, CH)],
                                             stp_sb[:, s % 2]).then_inc(stp_stored[s % 2], 16)

                    walk(0, FIRST_STEPS, BANK_FIRST, False)
                    with sp.Fori(0, NG - 1) as group:
                        walk(group, STEPS, BANK_STEPS, False)
                    walk(NG - 1, LAST_STEPS, BANK_LAST, True)
                    for k in range(2):
                        sp.wait_ge(y_stored[k], 16 * (NG * NCH // 2 + 1))
                        sp.wait_ge(stp_stored[k], 16 * (NG * N_BURST // 2 + 1))

                @block.gpsimd
                def _(pool):
                    def weigh(g, n):
                        pool.wait_ge(scanned, g * UNITS + n + 2)
                        b, i = n // BURST, n % BURST
                        col = (b % HALF) * HD + i
                        pool.sem_inc(beats, 1)
                        pool.tensor_copy(carry[:, col:col + 1], state[:, i, CH - 1:CH]).then_inc(carried, 1)
                        pool.wait_ge(carried, g * UNITS + n + 1)
                        pool.tensor_tensor(state[:, i], state[:, i], q_rows[:, b % 2], ALU.mult).then_inc(weighted, 1)

                    with pool.Fori(0, NG) as g:
                        for n in range(UNITS):
                            b = n // BURST
                            if n % BURST == 0:
                                pool.wait_ge(kq_loaded[b % 2], g * 64 + 32 * (b // 2) + 32)
                            pool.wait_ge(vexp_loaded[n % RING], g * (16 * UNITS // RING) + 16 * (n // RING) + 16)
                            pool.tensor_tensor(v_exp[:, n % RING], v_exp[:, n % RING], k_rows[:, b % 2], ALU.mult)\
                                .then_inc(u_made, 1)
                            if n >= 1:
                                weigh(g, n - 1)
                        weigh(g, UNITS - 1)

                @block.tensor
                def _(pe):
                    def max_scores(g, s, n):
                        c = ORDER[s]
                        if n == 0:
                            pe.wait_ge(q_loaded[c], g * (16 * len(SPLIT_Q)) + 16 * len(SPLIT_Q))
                            if s == 0:
                                pe.wait_ge(k_first_loaded, g * (16 * FIRST * len(SPLIT_K)) + 16 * FIRST * len(SPLIT_K))
                            for k in range(c + 1):
                                if NEEDED_AT[k] == s:
                                    pe.wait_ge(k_loaded[k], g * (16 * len(SPLIT_K)) + 16 * len(SPLIT_K))
                        hj, blk = n // (c + 1), n % (c + 1)
                        h, j = hj // TPC, hj % TPC
                        item = MAX_AT[s] + n
                        width = CH if blk < c else (j + 1) * P
                        bank = 4 + item % 2
                        keys = K_first if s < FIRST_USERS and blk < FIRST else K_st
                        pe.wait_ge(max_done, g * N_MAX + item + 1)
                        mm = pe.matmul(PS[:, bank, 0:width], Q_st[0:KS, c, h, j * P:(j + 1) * P],
                                       keys[0:KS, blk, h, 0:width], start=True, stop=(blk < c))
                        if blk == c:
                            mm = pe.matmul(PS[:, bank, j * P:(j + 1) * P], ident_bf[:, :], mask_qk[:, :],
                                           start=False, stop=True)
                        mm.then_inc(max_ready, 1)

                    def scores(g, s, kt, pair):
                        c = ORDER[s]
                        tile = TILE_AT[s] + kt
                        r = max(kt - TPC * c, 0)
                        if kt == 0 and pair == 0:
                            pe.wait_ge(shift_loaded[s % 2], g * (32 * NCH // 2) + 32 * (s // 2) + 64)
                        keys = K_first if s < FIRST_USERS and kt < FIRST * TPC else K_st
                        pe.wait_ge(exp_done, g * (2 * TILES) + 2 * tile + pair + 1)
                        for h in (2 * pair, 2 * pair + 1):
                            mm = pe.matmul(PS[:, h, 0:CH - r * P], keys[:, kt // TPC, h, (kt % TPC) * P:(kt % TPC + 1) * P],
                                           Q_st[:, c, h, r * P:CH], start=True, stop=(kt < TPC * c))
                            if kt >= TPC * c:
                                mm = pe.matmul(PS[:, h, 0:P], ident_bf[:, :], mask_kq[:, :], start=False, stop=True)
                        mm.then_inc(scores_ready, 1)

                    def values(g, s, kt):
                        c = ORDER[s]
                        tile = TILE_AT[s] + kt
                        r = max(kt - TPC * c, 0)
                        if kt == 0:
                            pe.wait_ge(out_evacuated, g * NCH + s + 1)
                            if s == 0:
                                pe.wait_ge(v_first_loaded, g * 16 + 16)
                            for k in range(c + 1):
                                if NEEDED_AT[k] == s:
                                    pe.wait_ge(v_loaded[k], g * 16 + 16)
                        v = V_first if s < FIRST_USERS and kt < FIRST * TPC else V_g
                        pe.wait_ge(exp_done, g * (2 * TILES) + 2 * tile + 4)
                        for h in range(GH):
                            mm = pe.matmul(PS[h * VW:(h + 1) * VW, 6, r * P:CH], v[:, kt, h * VW:(h + 1) * VW],
                                           probs[:, tile % P_SLOTS, h, 0:CH - r * P],
                                           start=(kt == 0), stop=(kt == KEY_TILES[s] - 1))
                        mm.then_inc(values_done, 1)

                    def burst(g, b, part, use):
                        half = b % HALF
                        n_c = HD // TPC
                        if part == 0:
                            pe.wait_ge(weighted, g * UNITS + BURST * (b + 1) + HALF * HD)
                            pe.wait_ge(bank_free, use + 1)
                            for q in range(n_c):
                                pe.matmul(PS[q * VW:(q + 1) * VW, 7, :], static_j[:, half, q * VW:(q + 1) * VW],
                                          q_rows[:, b % 2], start=True, stop=False)
                        else:
                            k = part - 1
                            for q in range(n_c):
                                i = q * TPC + k
                                mm = pe.matmul(PS[q * VW:(q + 1) * VW, 7, :], sum_j[:, half, i, :],
                                               state[:, i], start=False, stop=(k == TPC - 1))
                            if k == TPC - 1:
                                mm.then_inc(burst_done, 1)

                    def walk(group, steps, bank):
                        for step in steps:
                            kind, g, s = step[0], group + step[1], step[2]
                            if kind == "max":
                                max_scores(g, s, step[3])
                            elif kind == "scores":
                                scores(g, s, step[3], step[4])
                            elif kind == "values":
                                values(g, s, step[3])
                            elif kind == "burst":
                                use = group * N_BANK + bank["burst", step[1], s]
                                burst(g, s, step[3], use)
                            elif kind == "shift_turn":
                                pe.wait_ge(folded, g * NCH + s + 1)
                                pe.wait_ge(bank_free, group * N_BANK + bank[step] + 1)
                                pe.transpose(PS[0:GH * TPC, 7, 0:P], neg_max[:, s % 2, :], ident[:, :])\
                                    .then_inc(shift_turned, 1)
                            elif kind == "out_turn":
                                pe.wait_ge(out_evacuated, g * NCH + s + 2)
                                pe.wait_ge(bank_free, group * N_BANK + bank[step] + 1)
                                for j in range(TPC):
                                    mm = pe.transpose(PS[:, 7, j * P:(j + 1) * P], o_t[:, s % 2, j * P:(j + 1) * P],
                                                      ident[:, :])
                                mm.then_inc(out_turned, 1)

                    pe.wait_ge(ones_ready, 2)
                    walk(0, FIRST_STEPS, BANK_FIRST)
                    with pe.Fori(0, NG - 1) as group:
                        walk(group, STEPS, BANK_STEPS)
                    walk(NG - 1, LAST_STEPS, BANK_LAST)

                @block.scalar
                def _(act):
                    def walk(g, steps):
                        for step in steps:
                            kind, s = step[0], step[2]
                            if kind == "scores":
                                tile, pair = TILE_AT[s] + step[3], step[4]
                                r = max(step[3] - TPC * ORDER[s], 0)
                                if pair == 0:
                                    act.wait_ge(values_done, g * TILES + tile + 1)
                                act.wait_ge(scores_ready, g * (2 * TILES) + 2 * tile + pair + 1)
                                act.activation(probs[:, tile % P_SLOTS, 2 * pair:2 * pair + 2, 0:CH - r * P],
                                               PS[:, 2 * pair:2 * pair + 2, 0:CH - r * P], ACT.Exp,
                                               scale=SCALE).then_inc(exp_done, 1)
                            elif kind == "out_evac":
                                act.wait_ge(values_done, g * TILES + TILE_AT[s] + KEY_TILES[s] + P_SLOTS)
                                act.wait_ge(out_turned, g * NCH + s + 1)
                                act.activation(o_t[:, s % 2], PS[:, 6, :], ACT.Identity).then_inc(out_evacuated, 1)
                            elif kind == "burst" and step[3] == BURST_PARTS - 1:
                                act.wait_ge(burst_done, g * N_BURST + s + 2)
                                act.wait_ge(stp_stored[s % 2], g * (16 * N_BURST // 2) + 16 * (s // 2) + 16)
                                act.activation(stp_sb[:, s % 2], PS[:, 7, :], ACT.Identity).then_inc(bank_free, 1)

                    with act.Fori(0, NG - 1) as group:
                        walk(group, STEPS)
                    walk(NG - 1, LAST_STEPS)

                @block.vector
                def _(dve):
                    def walk(group, steps):
                        for step in steps:
                            kind, g, s = step[0], group + step[1], step[2]
                            if kind == "max":
                                c, n = ORDER[s], step[3]
                                hj, blk = n // (c + 1), n % (c + 1)
                                item = MAX_AT[s] + n
                                width = CH if blk < c else (hj % TPC + 1) * P
                                dve.wait_ge(max_ready, g * N_MAX + item + 1)
                                dve.tensor_reduce(pmax[:, s % 2, hj, blk:blk + 1], PS[:, 4 + item % 2, 0:width], AX.X,
                                                  ALU.max).then_inc(max_done, 1)
                            elif kind == "fold":
                                dve.wait_ge(max_done, g * N_MAX + MAX_AT[s] + MAXES[s] + 2)
                                dve.tensor_reduce(neg_max[:, s % 2, :], pmax[:, s % 2, :, 0:ORDER[s] + 1], AX.X, ALU.max,
                                                  negate=True).then_inc(folded, 1)
                            elif kind == "shift_split":
                                dve.wait_ge(shift_turned, g * NCH + s + 1)
                                dve.wait_ge(shift_loaded[s % 2], g * (32 * NCH // 2) + 32 * (s // 2) + 32)
                                turned = PS[0:GH * TPC, 7, 0:P]
                                dve.tensor_copy(shift[:, s % 2, 0, :], turned).then_inc(shift_high, 1)
                                dve.wait_ge(shift_high, g * NCH + s + 1)
                                dve.tensor_tensor(shift[:, s % 2, 1, :], turned, shift[:, s % 2, 0, :], ALU.subtract)\
                                    .then_inc(bank_free, 1)
                            elif kind == "out_norm":
                                dve.wait_ge(out_turned, g * NCH + s + 3)
                                dve.wait_ge(y_stored[s % 2], g * (16 * NCH // 2) + 16 * (s // 2) + 16)
                                sums = PS[:, 7, :].rearrange("p (j h v) -> p j h v", j=TPC, h=GH)
                                dve.reciprocal(rden[:, :, :], sums[:, :, :, HD]).then_inc(denom_ready, 1)
                                dve.wait_ge(denom_ready, g * NCH + s + 1)
                                dve.tensor_tensor(y_sb[:, s % 2].rearrange("p j (h v) -> p j h v", h=GH),
                                                  sums[:, :, :, 0:HD],
                                                  rden[:, :, :].unsqueeze(3).broadcast_to([P, TPC, GH, HD]), ALU.mult)\
                                    .then_inc(bank_free, 1)
                            elif kind == "unit":
                                b, i = s // BURST, s % BURST
                                col = (b % HALF) * HD + i
                                dve.wait_ge(u_made, g * UNITS + s + 1)
                                if i == 0:
                                    dve.wait_ge(burst_done, g * N_BURST + b + 1)
                                dve.wait_ge(weighted, g * UNITS + s + 1)
                                dve.tensor_tensor_scan(state[:, i], retention[:, col:col + 1].broadcast_to([P, CH]),
                                                       v_exp[:, s % RING], carry[:, col:col + 1], ALU.mult, ALU.add)\
                                    .then_inc(scanned, 1)

                    dve.memset(K_st[KS:KR], 1.0).then_inc(ones_ready, 1)
                    dve.memset(K_first[KS:KR], 1.0).then_inc(ones_ready, 1)
                    walk(0, FIRST_STEPS)
                    with dve.Fori(0, NG - 1) as group:
                        walk(group, STEPS)
                    walk(NG - 1, LAST_STEPS)

        fin = ExitStack()
        with fin:
            x1 = sb("x1", [P, NT, D], where=fin)
            xn2 = sb("xn2", [P, NT, D], where=fin)
            soft = sb("soft", [P, 2, TPC, D], where=fin)
            stp = sb("stp", [P, 2, HALF, CH], where=fin)
            xres = sb("xres", [P, 2, TPC, D], where=fin)
            diff = sb("diff", [P, 2, TPC, D], where=fin)
            y = sb("y", [P, 2, TPC, D], where=fin)
            y_t = sb("y_t", [P, 2, HALF, CH], where=fin)
            stats = sb("stats2", [P, TPC, 6], where=fin)
            mv = sb("mv2", [P, TPC, 2], where=fin)
            rstd = sb("rstd2", [P, 2 * TPC], where=fin)
            var_eps = sb("var_eps2", [P, TPC], where=fin)
            nmr = sb("nmr2", [P, 2 * TPC], where=fin)
            amax = sb("amax", [P, NCH], where=fin)
            small = sb("small", [P, 8], where=fin)
            scl = sb("scl", [P, 2, TPC * D], where=fin)
            magic = sb("magic", [P, 2, TPC * D], where=fin)
            moved = sb("moved", [P, 2, TPC * D], where=fin)
            r_bf = sb("r_bf", [P, 2, TPC, D], BF16, where=fin)
            r_t = sb("r_t", [P, 2, HALF, CH], BF16, where=fin)
            o_bf = sb("o_bf", [P, 2, TPC, D], BF16, where=fin)
            o_f = sb("o_f", [P, 2, TPC, D], where=fin)
            x_tiles = x.rearrange("(t p) n -> p t n", p=P)
            soft_tiles = y_soft.rearrange("g (t p) v -> g p t v", p=P)
            out_tiles = out.rearrange("(t p) n -> p t n", p=P)

            def tiles(it, par):
                return bass.ds(it * (2 * TPC) + par * TPC, TPC)

            with nc.Block() as block:
                @block.sync
                def _(sp):
                    with sp.Fori(0, NCH // 2) as it:
                        for par in range(2):
                            sp.wait_ge(x1_made, it * 2 + par + 1)
                            for g in range(NG):
                                sp.dma_start(soft[:, par, :, g * GH * HD:(g + 1) * GH * HD], soft_tiles[g, :, tiles(it, par), :])\
                                    .then_inc(soft_loaded[par], 16)
                            sp.dma_start(stp[:, par], y_stp_t[:, :, bass.ds(it * (2 * CH) + par * CH + PAD, CH)]
                                         .rearrange("f p t -> p f t")).then_inc(soft_loaded[par], 16)
                            sp.dma_start(xres[:, par], x_tiles[:, tiles(it, par), :]).then_inc(soft_loaded[par], 16)
                    with sp.Fori(0, NCH // 2) as it:
                        for par in range(2):
                            sp.wait_ge(out_made, it * 2 + par + 3)
                            sp.dma_start(out_tiles[:, tiles(it, par), :], o_f[:, par]).then_inc(out_stored[par], 16)
                    for par in range(2):
                        sp.wait_ge(out_stored[par], 16 * (NCH // 2 + 1))

                @block.gpsimd
                def _(pool):
                    with pool.Fori(0, NCH // 2) as it:
                        for par in range(2):
                            pool.wait_ge(soft_loaded[par], it * LOADS_PER_CHUNK + LOADS_PER_CHUNK)
                            pool.tensor_tensor(xres[:, par], xres[:, par],
                                               outb_sb[:, :].unsqueeze(1).broadcast_to([P, TPC, D]), ALU.add)\
                                .then_inc(xb_made, 1)
                        for par in range(2):
                            pool.wait_ge(diff_made, it * 2 + par + 1)
                            pool.tensor_tensor(diff[:, par].rearrange("p j (h v) -> p j h v", h=H),
                                               diff[:, par].rearrange("p j (h v) -> p j h v", h=H),
                                               alpha[:, tiles(it, par), :].unsqueeze(3).broadcast_to([P, TPC, H, HD]),
                                               ALU.mult).then_inc(diff_weighted, 1)
                        for par in range(2):
                            pool.wait_ge(var2, it * 2 + par + 1)
                            pool.tensor_tensor(rstd[:, par * TPC:(par + 1) * TPC], var_eps[:, :], neg_half[:, :], ALU.pow)\
                                .then_inc(rstd2, 1)
                    pool.wait_ge(peak_ready, 1)
                    pool.partition_all_reduce(small[:, 1:2], small[:, 0:1], P, bass.bass_isa.ReduceOp.max)\
                        .then_inc(amax_all, 1)
                    with pool.Fori(0, NCH // 2) as it:
                        for par in range(2):
                            pool.wait_ge(shifted, it * 2 + par + 1)
                            pool.wait_ge(r_turned, it * 2 + par + 1)
                            pool.tensor_tensor(r_bf[:, par].rearrange("p j n -> p (j n)"), moved[:, par], magic[:, par],
                                               ALU.subtract).then_inc(rounded, 1)
                        for par in range(2):
                            pool.wait_ge(ffn_biased, it * 2 + par + 3)
                            pool.wait_ge(out_stored[par], it * 16 + 16)
                            pool.tensor_tensor(o_f[:, par], x1[:, tiles(it, par), :], o_bf[:, par], ALU.add)\
                                .then_inc(out_made, 1)

                @block.tensor
                def _(pe):
                    with pe.Fori(0, NCH // 2) as it:
                        for par in range(2):
                            pe.wait_ge(soft_loaded[par], it * LOADS_PER_CHUNK + LOADS_PER_CHUNK)
                            pe.wait_ge(y_made, it * 2 + par + 1)
                            for half in range(HALF):
                                for j in range(TPC):
                                    mm = pe.transpose(PS[:, 2 * par + half, j * P:(j + 1) * P],
                                                      stp[:, par, half, j * P:(j + 1) * P], ident[:, :])
                            mm.then_inc(stp_turned, 1)
                        for par in range(2):
                            pe.wait_ge(y_made, it * 2 + par + 3)
                            pe.wait_ge(yt_evac, it * 4 + par * 2 + 2)
                            for c in range(HALF):
                                for j in range(TPC):
                                    mm = pe.transpose(PS[:, 4 + c, j * P:(j + 1) * P], y[:, par, j, c * P:(c + 1) * P],
                                                      ident[:, :])
                            mm.then_inc(y_turned, 1)
                            pe.wait_ge(yt_evac, it * 4 + par * 2 + 4)
                            pe.wait_ge(x1_made, it * 2 + par + 2)
                            for j in range(TPC):
                                for c in range(HALF):
                                    mm = pe.matmul(PS[:, 6 + j // 2, (j % 2) * D:(j % 2 + 1) * D],
                                                   y_t[:, par, c, j * P:(j + 1) * P], outw_sb[:, c, :],
                                                   start=(c == 0), stop=(c == HALF - 1))
                            mm.then_inc(attn_ready, 1)
                    with pe.Fori(0, NCH // 2) as it:
                        for par in range(2):
                            pe.wait_ge(rounded, it * 2 + par + 3)
                            pe.wait_ge(rt_evac, it * 2 + par + 1)
                            turned = PS[:, par, :].bitcast(BF16)
                            for c in range(HALF):
                                for j in range(TPC):
                                    mm = pe.transpose(turned[:, c * CH + j * P:c * CH + (j + 1) * P],
                                                      r_bf[:, par, j, c * P:(c + 1) * P], ident_bf[:, :])
                            mm.then_inc(r_turned, 1)
                        for par in range(2):
                            pe.wait_ge(rt_evac, it * 2 + par + 3)
                            pe.wait_ge(ffn_biased, it * 2 + par + 1)
                            for j in range(TPC):
                                for c in range(HALF):
                                    mm = pe.matmul(PS[:, 2 + 2 * par + j // 2, (j % 2) * D:(j % 2 + 1) * D],
                                                   r_t[:, par, c, j * P:(j + 1) * P], wq[:, c, :],
                                                   start=(c == 0), stop=(c == HALF - 1))
                            mm.then_inc(ffn_ready, 1)

                @block.scalar
                def _(act):
                    with act.Fori(0, NCH // 2) as it:
                        for par in range(2):
                            act.wait_ge(y_turned, it * 2 + par + 1)
                            act.wait_ge(attn_ready, it * 2 + par + 1)
                            for c in range(HALF):
                                act.activation(y_t[:, par, c, :], PS[:, 4 + c, :], ACT.Identity).then_inc(yt_evac, 1)
                        for par in range(2):
                            act.wait_ge(nmr2, it * 2 + par + 1)
                            for j in range(TPC):
                                ins = act.activation(xn2[:, bass.ds(it * (2 * TPC) + par * TPC + j, 1), :],
                                                     x1[:, bass.ds(it * (2 * TPC) + par * TPC + j, 1), :], ACT.Identity,
                                                     bias=nmr[:, par * TPC + j:par * TPC + j + 1],
                                                     scale=rstd[:, par * TPC + j:par * TPC + j + 1])
                            ins.then_inc(xn2_made, 1)
                    with act.Fori(0, NCH // 2) as it:
                        for par in range(2):
                            act.wait_ge(r_turned, it * 2 + par + 3)
                            act.wait_ge(ffn_ready, it * 2 + par + 1)
                            act.activation(r_t[:, par].rearrange("p c t -> p (c t)"), PS[:, par, :].bitcast(BF16),
                                           ACT.Identity).then_inc(rt_evac, 1)

                @block.vector
                def _(dve):
                    with dve.Fori(0, NCH // 2) as it:
                        for par in range(2):
                            dve.wait_ge(stp_turned, it * 2 + par + 1)
                            rec = [PS[:, 2 * par + f, :].rearrange("p (j i h) -> p j h i", j=TPC, i=HD)
                                   for f in range(HALF)]
                            sl = [slice(f * P, (f + 1) * P) for f in range(HALF)]
                            for f in range(HALF):
                                ins = dve.tensor_tensor(
                                    diff[:, par, :, sl[f]].rearrange("p j (h i) -> p j h i", h=HPH),
                                    rec[f], soft[:, par, :, sl[f]].rearrange("p j (h i) -> p j h i", h=HPH), ALU.subtract)
                            ins.then_inc(diff_made, 1)
                        for par in range(2):
                            dve.wait_ge(diff_weighted, it * 2 + par + 1)
                            for f in range(HALF):
                                rec = PS[:, 2 * par + f, :].rearrange("p (j i h) -> p j h i", j=TPC, i=HD)
                                cols = slice(f * P, (f + 1) * P)
                                ins = dve.tensor_tensor(
                                    y[:, par, :, cols].rearrange("p j (h i) -> p j h i", h=HPH), rec,
                                    diff[:, par, :, cols].rearrange("p j (h i) -> p j h i", h=HPH), ALU.subtract)
                            ins.then_inc(y_made, 1)
                        for par in range(2):
                            n1 = it * 2 + par + 1
                            dve.wait_ge(attn_ready, it * 2 + par + 3)
                            dve.wait_ge(xb_made, n1)
                            dve.tensor_tensor(x1[:, tiles(it, par), :],
                                              PS[:, 6:8, :].rearrange("p b (j n) -> p (b j) n", n=D), xres[:, par], ALU.add)\
                                .then_inc(x1_made, 1)
                            dve.wait_ge(x1_made, n1 + 2)
                            dve.sem_inc(beats, 1)
                            for j in range(TPC):
                                ins = dve.bn_stats(stats[:, j, :], x1[:, bass.ds(it * (2 * TPC) + par * TPC + j, 1), :]
                                                   .rearrange("p a n -> p (a n)"))
                            ins.then_inc(stats2, 1)
                            dve.wait_ge(stats2, n1)
                            dve.sem_inc(beats, 1)
                            for j in range(TPC):
                                ins = dve.bn_aggr(mv[:, j, :], stats[:, j, :])
                            ins.then_inc(mv2, 1)
                            dve.wait_ge(mv2, n1)
                            dve.tensor_scalar(var_eps[:, :], mv[:, :, 1], EPS, None, ALU.add).then_inc(var2, 1)
                            dve.wait_ge(rstd2, n1)
                            dve.scalar_tensor_tensor(out=nmr[:, par * TPC:(par + 1) * TPC], in0=mv[:, :, 0], scalar=-1.0,
                                                     in1=rstd[:, par * TPC:(par + 1) * TPC], op0=ALU.mult, op1=ALU.mult)\
                                .then_inc(nmr2, 1)
                        for par in range(2):
                            dve.wait_ge(xn2_made, it * 2 + par + 1)
                            dve.tensor_reduce(amax[:, bass.ds(it * 2 + par, 1)],
                                              xn2[:, tiles(it, par), :].rearrange("p j n -> p (j n)"), AX.X, ALU.max,
                                              apply_absolute_value=True).then_inc(amax_made, 1)
                    dve.wait_ge(amax_made, NCH)
                    dve.tensor_reduce(small[:, 0:1], amax[:, :], AX.X, ALU.max).then_inc(peak_ready, 1)
                    n_scale = 0

                    def link(ins):
                        nonlocal n_scale
                        n_scale += 1
                        ins.then_inc(scale_chain, 1)
                        dve.wait_ge(scale_chain, n_scale)

                    dve.wait_ge(amax_all, 1)
                    link(dve.tensor_scalar(small[:, 2:3], small[:, 1:2], 1e-12, None, ALU.max))
                    link(dve.reciprocal(small[:, 3:4], small[:, 2:3]))
                    link(dve.tensor_scalar(small[:, 4:5], small[:, 3:4], FP8_MAX, FP8_MAX, ALU.mult, ALU.min))
                    link(dve.reciprocal(small[:, 5:6], small[:, 4:5]))
                    link(dve.tensor_tensor(small[:, 6:7], small[:, 5:6], w_step[:, :], ALU.mult))
                    with dve.Fori(0, NCH // 2) as it:
                        for par in range(2):
                            n1 = it * 2 + par + 1
                            dve.wait_ge(rounded, n1)
                            dve.tensor_scalar(scl[:, par], xn2[:, tiles(it, par), :].rearrange("p j n -> p (j n)"),
                                              small[:, 4:5], FP8_MAX, ALU.mult, ALU.min).then_inc(scaled, 1)
                            dve.wait_ge(scaled, n1)
                            dve.tensor_scalar(magic[:, par].bitcast(I32), scl[:, par].bitcast(I32), EXPONENT_BITS, None,
                                              ALU.bitwise_and).then_inc(exponent_done, 1)
                            dve.wait_ge(exponent_done, n1)
                            dve.tensor_scalar(magic[:, par], magic[:, par], FP8_MIN_NORMAL, ROUND_TO_3_BITS, ALU.max,
                                              ALU.mult).then_inc(magic_done, 1)
                            dve.wait_ge(magic_done, n1)
                            dve.scalar_tensor_tensor(out=moved[:, par], in0=scl[:, par], scalar=-FP8_MAX, in1=magic[:, par],
                                                     op0=ALU.max, op1=ALU.add).then_inc(shifted, 1)
                        for par in range(2):
                            dve.wait_ge(ffn_ready, it * 2 + par + 3)
                            dve.wait_ge(out_made, it * 2 + par + 1)
                            dve.scalar_tensor_tensor(out=o_bf[:, par],
                                                     in0=PS[:, 2 + 2 * par:4 + 2 * par, :].rearrange("p b (j n) -> p (b j) n", n=D),
                                                     scalar=small[:, 6:7],
                                                     in1=ffnb_sb[:, :].unsqueeze(1).broadcast_to([P, TPC, D]),
                                                     op0=ALU.mult, op1=ALU.add).then_inc(ffn_biased, 1)


def kernel(L0_attn_x, L0_attn_Wqkv_w, L0_attn_Wqkv_b, L0_attn_out_w, L0_attn_out_b, L0_attn_W_static,
           L0_attn_Lambda_raw, L0_attn_Gamma, L0_attn_gate_w1, L0_attn_gate_b1, L0_attn_gate_w2,
           L0_attn_gate_b2, L0_ffn_weight, L0_ffn_bias):
    import numpy as np
    import concourse.bacc as bacc
    from concourse.bass_utils import run_bass_kernel_spmd

    def by_row(a):
        return np.asarray(a).reshape(HALF, HPH, HD, HD).transpose(1, 3, 0, 2).reshape(P, HALF * HD)

    inputs = {
        "x": np.asarray(L0_attn_x).reshape(T, D),
        "wqkv": np.asarray(L0_attn_Wqkv_w),
        "bqkv": np.asarray(L0_attn_Wqkv_b).reshape(6, P).T,
        "out_w": np.asarray(L0_attn_out_w),
        "out_b": np.asarray(L0_attn_out_b).reshape(1, D),
        "w_static": by_row(L0_attn_W_static),
        "lam": by_row(L0_attn_Lambda_raw),
        "gamma": by_row(L0_attn_Gamma),
        "gate_w1": np.asarray(L0_attn_gate_w1),
        "gate_b1": np.asarray(L0_attn_gate_b1).reshape(GATE, 1),
        "gate_w2": np.asarray(L0_attn_gate_w2),
        "gate_b2": np.asarray(L0_attn_gate_b2).reshape(1, H),
        "ffn_wt": np.asarray(L0_ffn_weight).T,
        "ffn_b": np.asarray(L0_ffn_bias).reshape(1, D),
    }
    inputs = {n: np.ascontiguousarray(a) for n, a in inputs.items()}
    nc = bacc.Bacc("TRN2", target_bir_lowering=False, num_devices=1)
    args = {n: nc.dram_tensor(n, a.shape, F32, kind="ExternalInput").ap() for n, a in inputs.items()}
    out = nc.dram_tensor("out", [T, D], F32, kind="ExternalOutput").ap()
    preln_attention_ffn_kernel(nc, out=out, **args)
    r = run_bass_kernel_spmd(nc, [inputs], core_ids=[0])
    return np.asarray(r.results[0]["out"]).reshape(1, T, D)
```

```python
from contextlib import ExitStack

import concourse.bass as bass
from concourse import mybir

F32 = mybir.dt.float32
BF16 = mybir.dt.bfloat16
I32 = mybir.dt.int32
ALU = mybir.AluOpType
ACT = mybir.ActivationFunctionType
AX = mybir.AxisListType

P = 128
T, D, H = 4096, 256, 16
HD = D // H
CH = 512
NCH = T // CH
TPC = CH // P
NT = T // P
GH = 4
NG = H // GH
HALF = 2
HPH = H // HALF
GATE = D // 2
VW = 32
VN = HD + 1
SPLIT_Q = (0, 0, 1, 1, 0, 2)
SPLIT_K = (0, 1, 0, 1, 2, 0)
KS = len(SPLIT_Q) * HD
KR = KS + 2
SCALE = HD ** -0.5
MASKED = -10000.0 / SCALE
EPS = 1e-5
FP8_MAX = 448.0
FP8_MIN_NORMAL = 2.0 ** -6
ROUND_TO_3_BITS = 1.5 * 2.0 ** 20
EXPONENT_BITS = 0x7F800000

ORDER = (3, 4, 5, 6, 7, 2, 1, 0)
FIRST = 5
FIRST_USERS = 3
LONG_END = 1 + max(s for s in range(NCH) if ORDER[s] >= FIRST)
KEY_TILES = tuple(TPC * (c + 1) for c in ORDER)
TILE_AT = tuple(sum(KEY_TILES[:s]) for s in range(NCH))
TILES = sum(KEY_TILES)
MAXES = tuple(GH * TPC * (c + 1) for c in ORDER)
MAX_AT = tuple(sum(MAXES[:s]) for s in range(NCH))
N_MAX = sum(MAXES)
ITEMS = [(s, n) for s in range(NCH) for n in range(MAXES[s])]
AHEAD = MAXES[0] + MAXES[1]
LEAD = 4
UNITS = 64
BURST = 16
N_BURST = UNITS // BURST
BURST_PARTS = 5
P_SLOTS = 3
S_BANKS = 3
M_BANKS = 3
BUSY_TILES = TILE_AT[4]
BUSY_SLOTS = 0.5
RING = 4
UNITS_PER_CHUNK = 7
STORES_PER_CHUNK = 16 * (3 + 3 + NG)
LOADS_PER_CHUNK = 16 * (1 + NG)
N_WEIGHTS = 13
PAD = 1024
SHIFTED = 16 * 2
FIRST_USE = {0: "first", 2: "long", 3: "rest"}
LOADS = {
    "q3": ((3,), TILE_AT[1], 30 - TILES),
    "q4": ((4,), TILE_AT[2], 42 - TILES),
    "k_first": (range(FIRST), TILE_AT[FIRST_USERS], 64 - TILES),
    "v_first": (range(FIRST), TILE_AT[FIRST_USERS], 70 - TILES),
    "q5": ((5,), TILE_AT[3], 72 - TILES),
    "q6": ((6,), TILE_AT[4], 92 - TILES),
    "k_long": (range(FIRST, NCH), TILE_AT[LONG_END], 122 - TILES),
    "v_long": (range(FIRST, NCH), TILE_AT[LONG_END], 128 - TILES),
    "q7": ((7,), TILE_AT[LONG_END], 130 - TILES),
    "k_rest": (range(FIRST), TILES, 1),
    "v_rest": (range(FIRST), TILES, 7),
    "q2": ((2,), TILES, 20), "q1": ((1,), TILES, 26), "q0": ((0,), TILES, 32),
}
EARLY = [name for name in LOADS if LOADS[name][2] < 0]
LATER = [name for name in LOADS if LOADS[name][2] >= 0]


def transfers(name):
    return 1 if name[0] == "v" else len(SPLIT_K)


def first_steps():
    loads = [("load", 0, name, n) for name in EARLY for n in range(transfers(name))]
    steps = [("load_units", 0, 0)] + [x for x in loads if x[2] not in (f"q{ORDER[0]}", "k_first")]
    release = None
    for s, n in ITEMS[:AHEAD]:
        steps.append(("max", 0, s, n))
        if release and n == 8:
            steps.append(release)
        if n == MAXES[s] - 1:
            steps += [("fold", 0, s), ("shift_turn", 0, s)]
            release = ("shift_split", 0, s)
    if release not in steps:
        steps.append(release)
    return steps


def group_steps(last):
    steps, turns, release = [], [], []

    def leave_bank():
        while release:
            steps.append(release.pop()[1])

    def emit(step, event=True):
        steps.append(step)
        if not event:
            return
        for x in turns + release:
            x[0] -= 1
        if release and release[0][0] <= 0:
            leave_bank()
        if turns and turns[0][0] <= 0 and not release and not bursting:
            _, turn, lag, leave = turns.pop(0)
            steps.append(turn)
            release.append([lag, leave])

    bursting = []

    todo = [(0,) + x for x in ITEMS[AHEAD:]]
    deadlines = [(TILE_AT[s] - LEAD, MAX_AT[s] + MAXES[s] - AHEAD) for s in range(1, NCH)]
    if not last:
        todo += [(1,) + x for x in ITEMS[:AHEAD]]
        deadlines += [(TILES - LEAD, N_MAX - AHEAD + MAXES[0]), (TILES, N_MAX)]
    total = len(todo)

    def max_items(n):
        for _ in range(min(n, len(todo))):
            d, s, i = todo.pop(0)
            emit(("max", d, s, i))
            if i == MAXES[s] - 1:
                emit(("fold", d, s), event=False)
                turns.append([8, ("shift_turn", d, s), 4, ("shift_split", d, s)])

    slots = []
    for b in range(N_BURST):
        slots += [("unit", b * BURST + i) for i in range(BURST)] + [None] * 3 + [("burst", b)]
    slots_total, slots_due = len(slots), 0.0
    pending = None
    for s in range(NCH):
        for kt in range(KEY_TILES[s]):
            t = TILE_AT[s] + kt
            for d, names in ((0, LATER), (1, [] if last else EARLY)):
                for name in names:
                    n = t - LOADS[name][2] - d * TILES
                    if 0 <= n < transfers(name):
                        emit(("load", d, name, n), event=False)
            done = total - len(todo)
            need = max([(m - done) / max(at - t, 1) for at, m in deadlines if m > done], default=0)
            n = min(int(-(-need // 1)), len(todo))
            slots_due += BUSY_SLOTS if t < BUSY_TILES else (slots_total - BUSY_SLOTS * BUSY_TILES) / (TILES - LEAD - BUSY_TILES)
            while slots and slots_due >= 1:
                slots_due -= 1
                item = slots.pop(0)
                if item and item[0] == "unit":
                    emit(("unit", 0, item[1]), event=False)
                elif item:
                    leave_bank()
                    bursting.append(item)
                    for part in range(BURST_PARTS):
                        steps.append(("burst", 0, item[1], part))
                        if part == BURST_PARTS - 1:
                            bursting.pop()
                        max_items(2)
            done = total - len(todo) - done
            n = max(n - done, 0)
            share = [n * (i + 1) // 5 - n * i // 5 for i in range(5)]
            for h in range(GH):
                emit(("scores", 0, s, kt, h))
                max_items(share[h])
            if pending:
                emit(("values", 0) + pending)
                if pending[1] == KEY_TILES[pending[0]] - 1:
                    emit(("out_evac", 0, pending[0]), event=False)
                    turns.append([6, ("out_turn", 0, pending[0]), 5, ("out_norm", 0, pending[0])])
            pending = (s, kt)
            max_items(share[GH])
    assert not slots and not todo
    emit(("values", 0) + pending)
    emit(("out_evac", 0, NCH - 1), event=False)
    leave_bank()
    for _, turn, _, leave in turns:
        steps += [turn, leave]
    steps += [("out_turn", 0, NCH - 1), ("out_norm", 0, NCH - 1)]
    return steps


def bank_uses(steps):
    uses = [x for x in steps if x[0] in ("shift_turn", "out_turn") or x[0] == "burst" and x[3] == 0]
    return {x[:3]: n for n, x in enumerate(uses)}


FIRST_STEPS, STEPS, LAST_STEPS = first_steps(), group_steps(False), group_steps(True)
BANK_FIRST = bank_uses(FIRST_STEPS)
N_BANK = len(bank_uses(STEPS))
BANK_STEPS = {x: n + len(BANK_FIRST) for x, n in bank_uses(STEPS).items()}
BANK_LAST = {x: n + len(BANK_FIRST) for x, n in bank_uses(LAST_STEPS).items()}


def preln_attention_ffn_kernel(nc, x, wqkv, bqkv, out_w, out_b, w_static, lam, gamma, gate_w1,
                               gate_b1, gate_w2, gate_b2, ffn_wt, ffn_b, out):
    ctx = ExitStack()
    with ctx:
        def sb(name, shape, dt=F32, where=ctx):
            return where.enter_context(nc.sbuf_tensor(name, shape, dt))

        def sem(name):
            return ctx.enter_context(nc.semaphore(name))

        PS = ctx.enter_context(nc.psum_tensor("PS", [P, 8, CH], F32))

        qk_parts = nc.dram_tensor("qk_parts", [3, 2 * D, T], BF16).ap()
        qkv_t = nc.dram_tensor("qkv_t", [3 * D, T], F32).ap()
        v_rows = nc.dram_tensor("v_rows", [NG, P, NT, GH * VN], F32).ap()
        y_soft = nc.dram_tensor("y_soft", [NG, T, GH * HD], F32).ap()
        y_stp_t = nc.dram_tensor("y_stp_t", [HALF, P, PAD + T], F32).ap()

        ident = sb("ident", [P, P])
        ident_bf = sb("ident_bf", [P, P], BF16)
        mask_qk = sb("mask_qk", [P, P], BF16)
        mask_kq = sb("mask_kq", [P, P], BF16)
        same_head = sb("same_head", [P, HPH])
        retention = sb("retention", [P, HALF * HD])
        sum_j = sb("sum_j", [P, HALF, HD, VW])
        static_j = sb("static_j", [P, HALF, P])
        carry = sb("carry", [P, HALF * HD])
        alpha = sb("alpha", [P, NT, H])
        z = sb("z", [P, NT, H])
        b2_sb = sb("b2_sb", [P, H])
        outw_sb = sb("outw_sb", [P, HALF, D])
        outb_sb = sb("outb_sb", [P, D])
        ffnb_sb = sb("ffnb_sb", [P, D])
        wq = sb("wq", [P, HALF, D], BF16)
        w_step = sb("w_step", [P, 1])

        neg_half = sb("neg_half", [P, TPC])

        weights_loaded = sem("weights_loaded")
        beats = sem("beats")


        credits = {}

        def free_sem(name, credit):
            s = sem(name)
            credits[name] = (s, credit)
            return s

        x_loaded = [sem(f"x_loaded{k}") for k in range(2)]
        stored = [free_sem(f"stored{k}", STORES_PER_CHUNK) for k in range(2)]
        stats_done, mv_done, rstd_done = sem("stats_done"), sem("mv_done"), sem("rstd_done")
        var_done, var2 = sem("var_done"), sem("var2")
        xn_ready = free_sem("xn_ready", 2)
        xnt_ready = free_sem("xnt_ready", 4)
        xnt_evac = free_sem("xnt_evac", 2)
        proj_ready = free_sem("proj_ready", 2 * UNITS_PER_CHUNK)
        proj_evac = free_sem("proj_evac", UNITS_PER_CHUNK)
        high_done, rest1_done, mid_done = sem("high_done"), sem("rest1_done"), sem("mid_done")
        low_done = sem("low_done")
        vrow_ready, vrow_evac = sem("vrow_ready"), free_sem("vrow_evac", 2)
        z_ready, z_evac = free_sem("z_ready", 2), free_sem("z_evac", 1)
        dve_setup, act_setup, pool_setup = sem("dve_setup"), sem("act_setup"), sem("pool_setup")
        gate_chain, gate_exp = sem("gate_chain"), sem("gate_exp")
        vaug_ready = sem("vaug_ready")
        loaded = {name: sem(f"{name}_loaded") for name in LOADS}
        max_ready, max_done = sem("max_ready"), free_sem("max_done", M_BANKS)
        folded, shift_turned, shift_high = sem("folded"), sem("shift_turned"), sem("shift_high")
        shift_loaded = [free_sem(f"shift_loaded{k}", SHIFTED) for k in range(2)]
        scores_ready, exp_done = sem("scores_ready"), free_sem("exp_done", S_BANKS)
        values_done = free_sem("values_done", P_SLOTS)
        out_evacuated, out_turned = free_sem("out_evacuated", 1), free_sem("out_turned", 2)
        denom_ready, ones_ready = sem("denom_ready"), sem("ones_ready")
        y_stored = [free_sem(f"y_stored{k}", 16) for k in range(2)]
        bank_free = free_sem("bank_free", 1)
        kq_loaded = [sem(f"kq_loaded{k}") for k in range(2)]
        vexp_loaded = [sem(f"vexp_loaded{k}") for k in range(RING)]
        u_made, scanned = sem("u_made"), free_sem("scanned", 1)
        carried, weighted = sem("carried"), free_sem("weighted", HALF * HD)
        burst_done = free_sem("burst_done", 1)
        stp_stored = [free_sem(f"stp_stored{k}", 16) for k in range(2)]
        soft_loaded = [sem(f"soft_loaded{k}") for k in range(2)]
        x_again = [sem(f"x_again{k}") for k in range(2)]
        stp_turned, diff_made, diff_weighted = free_sem("stp_turned", 2), free_sem("diff_made", 2), sem("diff_weighted")
        xb_made, y_made, y_turned = free_sem("xb_made", 2), free_sem("y_made", 2), sem("y_turned")
        yt_evac, attn_ready, x1_made = free_sem("yt_evac", 2), free_sem("attn_ready", 2), free_sem("x1_made", 2)
        stats2, mv2, rstd2, nmr2 = sem("stats2"), sem("mv2"), sem("rstd2"), sem("nmr2")
        xn2_made, amax_made, amax_all = sem("xn2_made"), sem("amax_made"), sem("amax_all")
        scale_chain, peak_ready = sem("scale_chain"), sem("peak_ready")
        scaled, exponent_done, magic_done = sem("scaled"), sem("exponent_done"), sem("magic_done")
        shifted, rounded, r_turned = sem("shifted"), free_sem("rounded", 2), free_sem("r_turned", 2)
        rt_evac, ffn_ready = free_sem("rt_evac", 2), free_sem("ffn_ready", 2)
        ffn_biased, out_made = free_sem("ffn_biased", 2), free_sem("out_made", 2)
        out_stored = [free_sem(f"out_stored{k}", 16) for k in range(2)]

        with nc.Block() as block:
            @block.gpsimd
            def _(pool):
                for s, n in credits.values():
                    pool.sem_inc(s, n)

        early = ctx.enter_context(ExitStack())
        Q_st = sb("Q_st", [KR, NCH, GH, CH], BF16, where=early)
        K_first = sb("K_first", [KR, GH, FIRST * CH], BF16, where=early)
        pro = ExitStack()
        with pro:
            wqkv_sb = sb("wqkv_sb", [P, HALF, 3 * D], where=pro)
            bqkv_sb = sb("bqkv_sb", [P, 6], where=pro)
            w1_sb = sb("w1_sb", [P, HALF, GATE], where=pro)
            b1_sb = sb("b1_sb", [P, 1], where=pro)
            w2_sb = sb("w2_sb", [P, H], where=pro)
            lam_sb = sb("lam_sb", [P, HALF * HD], where=pro)
            gamma_sb = sb("gamma_sb", [P, HALF * HD], where=pro)
            wst_sb = sb("wst_sb", [P, HALF * HD], where=pro)
            ffnw_sb = sb("ffnw_sb", [P, HALF * D], where=pro)
            wtmp = sb("wtmp", [P, 3, HALF * D], where=pro)
            wsmall = sb("wsmall", [P, 8], where=pro)
            xin = sb("xin", [P, 2, TPC, D], where=pro)
            xn = sb("xn", [P, 2, TPC, D], where=pro)
            stats = sb("stats", [P, TPC, 6], where=pro)
            mv = sb("mv", [P, TPC, 2], where=pro)
            rstd = sb("rstd", [P, TPC], where=pro)
            var_eps = sb("var_eps", [P, TPC], where=pro)
            xn_t = sb("xn_t", [P, 2, HALF, CH], where=pro)
            proj = sb("proj", [P, 2, 6, CH], where=pro)
            gate_t = sb("gate_t", [P, 2, CH], where=pro)
            parts = sb("parts", [P, 2, 3, 4, CH], BF16, where=pro)
            rest = sb("rest", [P, 2, 4, CH], where=pro)
            vaug = sb("vaug", [P, 2, TPC, H, VN], where=pro)
            x_tiles = x.rearrange("(t p) n -> p t n", p=P)

            with nc.Block() as block:
                @block.sync
                def _(sp):
                    def load_x(it, par):
                        sp.dma_start(xin[:, par], x_tiles[:, bass.ds(it * (2 * TPC) + par * TPC, TPC), :])\
                            .then_inc(x_loaded[par], 16)

                    def store(it, par):
                        rows = bass.ds(it * (2 * CH) + par * CH, CH)
                        sp.wait_ge(proj_evac, it * 14 + par * 7 + 13)
                        for w in range(3):
                            sp.dma_start(qkv_t[w * D:(w + 1) * D, rows].rearrange("(u p) t -> p u t", p=P),
                                         proj[:, par, 2 * w:2 * w + 2, :]).then_inc(stored[par], 16)
                        for n, made in enumerate([high_done, mid_done, low_done]):
                            sp.wait_ge(made, it * 2 + par + 1)
                            sp.sem_inc(beats, 1)
                            sp.dma_start(qk_parts[n, :, rows].rearrange("(u p) t -> p u t", p=P),
                                         parts[:, par, n, :, :]).then_inc(stored[par], 16)
                        sp.wait_ge(vrow_evac, it * 4 + par * 2 + 4)
                        for g in range(NG):
                            sp.dma_start(
                                v_rows[g, :, bass.ds(it * (2 * TPC) + par * TPC, TPC), :],
                                vaug[:, par, :, g * GH:(g + 1) * GH, :].rearrange("p t h v -> p t (h v)"),
                            ).then_inc(stored[par], 16)

                    for par in range(2):
                        load_x(0, par)
                    with sp.Fori(0, NCH // 2 - 1) as it:
                        for par in range(2):
                            sp.wait_ge(xn_ready, it * 2 + par + 3)
                            sp.sem_inc(beats, 1)
                            load_x(it + 1, par)
                            store(it, par)
                    store(NCH // 2 - 1, 0)
                    for par in range(2):
                        sp.wait_ge(stored[par], STORES_PER_CHUNK * (1 + (FIRST + 1 - par) // 2))
                    c = ORDER[0]
                    for n, part in enumerate(SPLIT_Q):
                        sp.dma_start(Q_st[n * HD:(n + 1) * HD, c],
                                     qk_parts[part, 0:GH * HD, c * CH:(c + 1) * CH].rearrange("(h d) t -> d h t", d=HD))\
                            .then_inc(loaded[f"q{c}"], 16)
                    for n, part in enumerate(SPLIT_K):
                        sp.dma_start(K_first[n * HD:(n + 1) * HD],
                                     qk_parts[part, D:D + GH * HD, 0:FIRST * CH].rearrange("(h d) t -> d h t", d=HD))\
                            .then_inc(loaded["k_first"], 16)
                    store(NCH // 2 - 1, 1)
                    for par in range(2):
                        sp.wait_ge(stored[par], STORES_PER_CHUNK * (NCH // 2 + 1))

                @block.gpsimd
                def _(pool):
                    pool.memset(ident[:, :], 0.0).then_inc(pool_setup, 1)
                    pool.memset(mask_qk[:, :], 0.0).then_inc(pool_setup, 1)
                    pool.memset(mask_kq[:, :], 0.0).then_inc(pool_setup, 1)
                    pool.memset(same_head[:, :], 1.0).then_inc(pool_setup, 1)
                    pool.wait_ge(pool_setup, 4)
                    pool.affine_select(out=ident[:, :], in_=ident[:, :], compare_op=ALU.not_equal, fill=1.0,
                                       base=0, pattern=[[-1, P]], channel_multiplier=1).then_inc(pool_setup, 1)
                    pool.affine_select(out=mask_qk[:, :], in_=mask_qk[:, :], compare_op=ALU.is_ge, fill=MASKED,
                                       base=0, pattern=[[-1, P]], channel_multiplier=1).then_inc(pool_setup, 1)
                    pool.affine_select(out=mask_kq[:, :], in_=mask_kq[:, :], compare_op=ALU.is_ge, fill=MASKED,
                                       base=0, pattern=[[1, P]], channel_multiplier=-1).then_inc(pool_setup, 1)
                    pool.affine_select(out=same_head[:, :], in_=same_head[:, :], compare_op=ALU.is_ge, fill=0.0,
                                       base=0, pattern=[[-HD, HPH]], channel_multiplier=1).then_inc(pool_setup, 1)
                    pool.wait_ge(pool_setup, 8)
                    pool.affine_select(out=same_head[:, :], in_=same_head[:, :], compare_op=ALU.is_ge, fill=0.0,
                                       base=HD - 1, pattern=[[HD, HPH]], channel_multiplier=-1)\
                        .then_inc(pool_setup, 1)
                    pool.tensor_copy(ident_bf[:, :], ident[:, :]).then_inc(pool_setup, 1)
                    for par in range(2):
                        pool.memset(vaug[:, par, :, :, HD:VN], 1.0).then_inc(vaug_ready, 1)
                    pool.memset(neg_half[:, :], -0.5).then_inc(pool_setup, 1)
                    pool.wait_ge(pool_setup, 11)
                    def power(c1):
                        pool.wait_ge(var_done, c1)
                        pool.tensor_tensor(rstd[:, :], var_eps[:, :], neg_half[:, :], ALU.pow).then_inc(rstd_done, 1)

                    def low_part(it, par):
                        pool.wait_ge(mid_done, it * 2 + par + 1)
                        pool.tensor_tensor(parts[:, par, 2], rest[:, par], parts[:, par, 1], ALU.subtract)\
                            .then_inc(low_done, 1)

                    power(1)
                    pool.wait_ge(dve_setup, 1)
                    pool.partition_all_reduce(wsmall[:, 1:2], wsmall[:, 0:1], P, bass.bass_isa.ReduceOp.max)\
                        .then_inc(pool_setup, 1)
                    with pool.Fori(0, NCH // 2 - 1) as it:
                        for par in range(2):
                            power(it * 2 + par + 2)
                            low_part(it, par)
                    power(NCH)
                    for par in range(2):
                        low_part(NCH // 2 - 1, par)

                @block.tensor
                def _(pe):
                    pe.wait_ge(pool_setup, 10)
                    pe.wait_ge(weights_loaded, 16 * N_WEIGHTS)
                    def turn(it, par):
                        pe.wait_ge(xn_ready, it * 2 + par + 3)
                        for c in range(HALF):
                            pe.wait_ge(xnt_evac, it * 4 + par * 2 + c + 1)
                            for j in range(TPC):
                                mm = pe.transpose(PS[:, c, j * P:(j + 1) * P],
                                                  xn[:, par, j, c * P:(c + 1) * P], ident[:, :])
                            mm.then_inc(xnt_ready, 1)

                    def project(it, par):
                        pe.wait_ge(xnt_evac, it * 4 + par * 2 + 4)
                        for u in range(UNITS_PER_CHUNK):
                            pe.wait_ge(proj_evac, it * 14 + par * 7 + (u + 5 if u < 3 else u + 4 if u > 3 else 4))
                            for c in range(HALF):
                                w = wqkv_sb[:, c, u * P:(u + 1) * P] if u < 6 else w1_sb[:, c, :]
                                mm = pe.matmul(PS[:, 2 + u % 4, :], w, xn_t[:, par, c, :],
                                               start=(c == 0), stop=(c == HALF - 1))
                            mm.then_inc(proj_ready, 1)

                    def turn_back(it, par):
                        pe.wait_ge(proj_evac, it * 14 + par * 7 + 13)
                        for half in range(HALF):
                            pe.wait_ge(vrow_evac, it * 4 + par * 2 + half + 2)
                            for j in range(TPC):
                                mm = pe.transpose(PS[:, 7, j * P:(j + 1) * P],
                                                  proj[:, par, 4 + half, j * P:(j + 1) * P], ident[:, :])
                            mm.then_inc(vrow_ready, 1)
                        pe.wait_ge(proj_evac, it * 14 + par * 7 + 14)
                        pe.wait_ge(z_evac, it * 2 + par + 1)
                        for j in range(TPC):
                            mm = pe.matmul(PS[:, 6, j * H:(j + 1) * H], gate_t[:, par, j * P:(j + 1) * P],
                                           w2_sb[:, :], start=True, stop=True)
                        mm.then_inc(z_ready, 1)

                    turn(0, 0)
                    with pe.Fori(0, NCH // 2 - 1) as it:
                        for par in range(2):
                            project(it, par)
                            turn(it + par, 1 - par)
                            turn_back(it, par)
                    project(NCH // 2 - 1, 0)
                    turn(NCH // 2 - 1, 1)
                    turn_back(NCH // 2 - 1, 0)
                    project(NCH // 2 - 1, 1)
                    turn_back(NCH // 2 - 1, 1)

                @block.scalar
                def _(act):
                    for dst, src in [
                            (wqkv_sb[:, :, :], wqkv.rearrange("(c p) n -> p c n", p=P)),
                            (bqkv_sb[:, :], bqkv),
                            (w1_sb[:, :, :], gate_w1.rearrange("(c p) n -> p c n", p=P)),
                            (b1_sb[:, :], gate_b1), (w2_sb[:, :], gate_w2),
                            (b2_sb[:, :], gate_b2.broadcast_to([P, H])),
                            (lam_sb[:, :], lam), (gamma_sb[:, :], gamma), (wst_sb[:, :], w_static),
                            (ffnw_sb[:, :].rearrange("p (c n) -> p c n", c=HALF),
                             ffn_wt.rearrange("(c p) n -> p c n", p=P)),
                            (outw_sb[:, :, :], out_w.rearrange("(c p) n -> p c n", p=P)),
                            (outb_sb[:, :], out_b.broadcast_to([P, D])),
                            (ffnb_sb[:, :], ffn_b.broadcast_to([P, D]))]:
                        act.dma_start(dst, src).then_inc(weights_loaded, 16)
                    act.wait_ge(weights_loaded, 16 * N_WEIGHTS)
                    act.wait_ge(vaug_ready, 2)
                    def columns(it, par):
                        for c in range(HALF):
                            act.wait_ge(xnt_ready, it * 4 + par * 2 + c + 5)
                            act.wait_ge(proj_ready, it * 14 + par * 7 + 7)
                            act.activation(xn_t[:, par, c, :], PS[:, c, :], ACT.Identity).then_inc(xnt_evac, 1)

                    def products(it, par):
                        act.wait_ge(stored[par], it * STORES_PER_CHUNK + STORES_PER_CHUNK)
                        for u in range(6):
                            act.wait_ge(proj_ready, it * 14 + par * 7 + u + 15)
                            act.activation(proj[:, par, u, :], PS[:, 2 + u % 4, :], ACT.Identity,
                                           bias=bqkv_sb[:, u:u + 1]).then_inc(proj_evac, 1)
                        act.wait_ge(proj_ready, it * 14 + par * 7 + 21)
                        act.wait_ge(z_ready, it * 2 + par + 1)
                        act.activation(gate_t[:, par, :], PS[:, 4, :], ACT.Gelu, bias=b1_sb[:, 0:1])\
                            .then_inc(proj_evac, 1)

                    def rows_and_logits(it, par):
                        for half in range(HALF):
                            act.wait_ge(vrow_ready, it * 4 + par * 2 + half + 1)
                            act.activation(vaug[:, par, :, half * HPH:(half + 1) * HPH, 0:HD],
                                           PS[:, 7, :].rearrange("p (j h d) -> p j h d", j=TPC, h=HPH),
                                           ACT.Identity).then_inc(vrow_evac, 1)
                        act.wait_ge(z_ready, it * 2 + par + 3)
                        act.activation(z[:, bass.ds(it * (2 * TPC) + par * TPC, TPC), :],
                                       PS[:, 6, 0:TPC * H].rearrange("p (j h) -> p j h", j=TPC),
                                       ACT.Identity).then_inc(z_evac, 1)

                    columns(0, 0)
                    act.activation(lam_sb[:, :], lam_sb[:, :], ACT.Exp, scale=-1.0).then_inc(act_setup, 1)
                    with act.Fori(0, NCH // 2 - 1) as it:
                        for par in range(2):
                            products(it, par)
                            columns(it + par, 1 - par)
                            rows_and_logits(it, par)
                    products(NCH // 2 - 1, 0)
                    columns(NCH // 2 - 1, 1)
                    rows_and_logits(NCH // 2 - 1, 0)
                    products(NCH // 2 - 1, 1)
                    rows_and_logits(NCH // 2 - 1, 1)

                @block.vector
                def _(dve):
                    def normalise(it, par):
                        c1 = it * 2 + par + 1
                        dve.wait_ge(x_loaded[par], it * 16 + 16)
                        dve.sem_inc(beats, 1)
                        for j in range(TPC):
                            ins = dve.bn_stats(stats[:, j, :], xin[:, par, j, :])
                        ins.then_inc(stats_done, 1)
                        dve.wait_ge(stats_done, c1)
                        dve.sem_inc(beats, 1)
                        for j in range(TPC):
                            ins = dve.bn_aggr(mv[:, j, :], stats[:, j, :])
                        ins.then_inc(mv_done, 1)
                        dve.wait_ge(mv_done, c1)
                        dve.tensor_scalar(var_eps[:, :], mv[:, :, 1], EPS, None, ALU.add).then_inc(var_done, 1)
                        dve.wait_ge(rstd_done, c1)
                        dve.wait_ge(xnt_ready, it * 4 + par * 2 + 2)
                        for j in range(TPC):
                            ins = dve.tensor_scalar(xn[:, par, j, :], xin[:, par, j, :], mv[:, j, 0:1],
                                                    rstd[:, j:j + 1], ALU.subtract, ALU.mult)
                        ins.then_inc(xn_ready, 1)

                    def split(it, par):
                        c1 = it * 2 + par + 1
                        dve.wait_ge(proj_evac, it * 14 + par * 7 + 11)
                        dve.wait_ge(stored[par], it * STORES_PER_CHUNK + STORES_PER_CHUNK)
                        dve.tensor_copy(parts[:, par, 0], proj[:, par, 0:4]).then_inc(high_done, 1)
                        dve.wait_ge(high_done, c1)
                        dve.tensor_tensor(rest[:, par], proj[:, par, 0:4], parts[:, par, 0], ALU.subtract)\
                            .then_inc(rest1_done, 1)
                        dve.wait_ge(rest1_done, c1)
                        dve.tensor_copy(parts[:, par, 1], rest[:, par]).then_inc(mid_done, 1)

                    normalise(0, 0)
                    dve.wait_ge(weights_loaded, 16 * N_WEIGHTS)
                    dve.tensor_reduce(wsmall[:, 0:1], ffnw_sb[:, :], AX.X, ALU.max, apply_absolute_value=True)\
                        .then_inc(dve_setup, 1)
                    n_setup = 1

                    def link(ins):
                        nonlocal n_setup
                        n_setup += 1
                        ins.then_inc(dve_setup, 1)
                        dve.wait_ge(dve_setup, n_setup)

                    dve.wait_ge(act_setup, 1)
                    link(dve.tensor_scalar(lam_sb[:, :], lam_sb[:, :], 1.0, None, ALU.add))
                    link(dve.reciprocal(lam_sb[:, :], lam_sb[:, :]))
                    link(dve.tensor_scalar(retention[:, :], lam_sb[:, :], -1.0, 1.0, ALU.mult, ALU.add))
                    link(dve.memset(carry[:, :], 0.0))
                    link(dve.memset(sum_j[:, :, :, :], 0.0))
                    link(dve.tensor_scalar(gamma_sb[:, :], gamma_sb[:, :], SCALE, None, ALU.mult))
                    n_c = HD // TPC
                    heads = same_head[:, :].unsqueeze(1).broadcast_to([P, HALF * n_c, HPH])
                    for k in range(TPC):
                        link(dve.tensor_tensor(
                            sum_j[:, :, :, :].rearrange("p f (c k) v -> p (f c) k v", k=TPC)[:, :, k, k * HPH:(k + 1) * HPH],
                            heads,
                            gamma_sb[:, :].rearrange("p (c k) -> p c k", k=TPC)[:, :, k:k + 1]
                            .broadcast_to([P, HALF * n_c, HPH]), ALU.mult))
                        link(dve.tensor_tensor(
                            static_j[:, :, :].rearrange("p f (c k v) -> p (f c) k v", c=n_c, k=TPC)[:, :, k, :],
                            heads,
                            wst_sb[:, :].rearrange("p (c k) -> p c k", k=TPC)[:, :, k:k + 1]
                            .broadcast_to([P, HALF * n_c, HPH]), ALU.mult))
                    dve.wait_ge(pool_setup, 12)
                    link(dve.tensor_scalar(wsmall[:, 2:3], wsmall[:, 1:2], 1e-12, None, ALU.max))
                    link(dve.reciprocal(wsmall[:, 3:4], wsmall[:, 2:3]))
                    link(dve.tensor_scalar(wsmall[:, 4:5], wsmall[:, 3:4], FP8_MAX, FP8_MAX, ALU.mult, ALU.min))
                    link(dve.reciprocal(w_step[:, :], wsmall[:, 4:5]))
                    link(dve.tensor_scalar(wtmp[:, 0], ffnw_sb[:, :], wsmall[:, 4:5], FP8_MAX, ALU.mult, ALU.min))
                    link(dve.tensor_scalar(wtmp[:, 1].bitcast(I32), wtmp[:, 0].bitcast(I32), EXPONENT_BITS, None,
                                           ALU.bitwise_and))
                    link(dve.tensor_scalar(wtmp[:, 1], wtmp[:, 1], FP8_MIN_NORMAL, ROUND_TO_3_BITS, ALU.max, ALU.mult))
                    link(dve.scalar_tensor_tensor(out=wtmp[:, 2], in0=wtmp[:, 0], scalar=-FP8_MAX, in1=wtmp[:, 1],
                                                  op0=ALU.max, op1=ALU.add))
                    link(dve.tensor_tensor(wq[:, :, :].rearrange("p c n -> p (c n)"), wtmp[:, 2], wtmp[:, 1],
                                           ALU.subtract))
                    with dve.Fori(0, NCH // 2 - 1) as it:
                        for par in range(2):
                            normalise(it + par, 1 - par)
                            split(it, par)
                    normalise(NCH // 2 - 1, 1)
                    for par in range(2):
                        split(NCH // 2 - 1, par)
                    dve.memset(K_first[KS:KR], 1.0).then_inc(ones_ready, 1)

        att = ExitStack()
        with att:
            K_st = sb("K_st", [KR, GH, T], BF16, where=att)
            V_g = sb("V_g", [P, NT, GH * VN], where=att)
            V_first = sb("V_first", [P, FIRST * TPC, GH * VN], where=att)
            probs = sb("probs", [P, P_SLOTS, GH, CH], where=att)
            pmax = sb("pmax", [P, 2, GH * TPC, NCH], where=att)
            neg_max = sb("neg_max", [P, 2, GH * TPC], where=att)
            shift = sb("shift", [GH * TPC, 2, 2, P], BF16, where=att)
            o_t = sb("o_t", [P, 2, CH], where=att)
            rden = sb("rden", [P, TPC, GH], where=att)
            y_sb = sb("y_sb", [P, 2, TPC, GH * HD], where=att)
            k_rows = sb("k_rows", [P, 2, CH], where=att)
            q_rows = sb("q_rows", [P, 2, CH], where=att)
            v_exp = sb("v_exp", [P, RING, CH], where=att)
            state = sb("state", [P, BURST, CH], where=att)
            stp_sb = sb("stp_sb", [P, 2, CH], where=att)

            with nc.Block() as block:
                @block.sync
                def _(sp):
                    targets = {"k_first": K_first, "k_long": K_st, "k_rest": K_st,
                               "v_first": V_first, "v_long": V_g, "v_rest": V_g}

                    def load(group, d, name, n):
                        g = group + (d or 0)
                        chunks, free, _ = LOADS[name]
                        if n == 0 and d == 0:
                            sp.wait_ge(values_done, group * TILES + P_SLOTS)
                            sp.sem_inc(beats, 1)
                        elif n == 0 and d == 1:
                            sp.wait_ge(values_done, group * TILES + (free + P_SLOTS))
                            sp.sem_inc(beats, 1)
                        if name[0] == "v":
                            rows = slice(chunks[0] * TPC, (chunks[-1] + 1) * TPC)
                            sp.dma_start(targets[name][:, rows, :],
                                         v_rows[bass.ds(g, 1), :, rows, :].rearrange("g p t v -> (g p) t v"))\
                                .then_inc(loaded[name], 16)
                            return
                        cols = slice(chunks[0] * CH, (chunks[-1] + 1) * CH)
                        part, first_row, stack = (SPLIT_Q[n], 0, Q_st[:, chunks[0]]) if name[0] == "q" \
                            else (SPLIT_K[n], D, targets[name][:, :, cols])
                        sp.dma_start(stack[n * HD:(n + 1) * HD],
                                     qk_parts[part, bass.ds(g * (GH * HD) + first_row, GH * HD), cols]
                                     .rearrange("(h d) t -> d h t", d=HD)).then_inc(loaded[name], 16)

                    def load_kq(g, b):
                        cols = bass.ds(g * (2 * CH) + (b // HALF) * CH, CH)
                        half = b % HALF
                        for dst, first in ((k_rows, D), (q_rows, 0)):
                            sp.dma_start(dst[:, b % 2], qkv_t[first + half * P:first + (half + 1) * P, cols])\
                                .then_inc(kq_loaded[b % 2], 16)

                    def load_v_exp(g, n):
                        b, i = n // BURST, n % BURST
                        first = 2 * D + (b % HALF) * P
                        v = qkv_t[first:first + P, bass.ds(g * (2 * CH) + (b // HALF) * CH, CH)]
                        sp.dma_start(v_exp[:, n % RING], v.rearrange("(h i) t -> h i t", i=HD)[:, i, :]
                                     .unsqueeze(1).broadcast_to([HPH, HD, CH])).then_inc(vexp_loaded[n % RING], 16)

                    def walk(group, steps, bank, last):
                        for step in steps:
                            kind, g, s = step[0], group + step[1], step[2]
                            if kind == "load" and steps is FIRST_STEPS:
                                load(0, None, s, step[3])
                            elif kind == "load":
                                load(group, step[1], s, step[3])
                            elif kind == "load_units":
                                load_kq(g, 0)
                                for n in range(RING - 1):
                                    load_v_exp(g, n)
                            elif kind == "unit":
                                if s % BURST == 0 and not (last and s // BURST + 1 == N_BURST):
                                    sp.wait_ge(burst_done, g * N_BURST + s // BURST + 1)
                                    b = s // BURST + 1
                                    load_kq(g + b // N_BURST, b % N_BURST)
                                n = s + RING - 1
                                if not (last and n >= UNITS):
                                    sp.wait_ge(scanned, g * UNITS + s + 1)
                                    load_v_exp(g + n // UNITS, n % UNITS)
                            elif kind == "shift_split":
                                sp.wait_ge(bank_free, group * N_BANK + bank["shift_turn", step[1], s] + 2)
                                for k in range(2):
                                    sp.dma_start(Q_st[KS + k:KS + k + 1, ORDER[s]].rearrange("a h (j t) -> a (h j) t", t=P),
                                                 shift[:, s % 2, k, :]).then_inc(shift_loaded[s % 2], 16)
                            elif kind == "out_norm":
                                sp.wait_ge(bank_free, group * N_BANK + bank["out_turn", step[1], s] + 2)
                                sp.sem_inc(beats, 1)
                                c = ORDER[s]
                                sp.dma_start(y_soft[bass.ds(g, 1), c * CH:(c + 1) * CH, :]
                                             .rearrange("g (j p) v -> p (g j) v", p=P), y_sb[:, s % 2])\
                                    .then_inc(y_stored[s % 2], 16)
                            elif kind == "burst" and step[3] == BURST_PARTS - 1:
                                sp.wait_ge(bank_free, group * N_BANK + bank["burst", step[1], s] + 2)
                                sp.sem_inc(beats, 1)
                                sp.dma_start(y_stp_t[s % HALF, :, bass.ds(g * (2 * CH) + (s // HALF) * CH + PAD, CH)],
                                             stp_sb[:, s % 2]).then_inc(stp_stored[s % 2], 16)

                    walk(0, FIRST_STEPS, BANK_FIRST, False)
                    with sp.Fori(0, NG - 1) as group:
                        walk(group, STEPS, BANK_STEPS, False)
                    walk(NG - 1, LAST_STEPS, BANK_LAST, True)
                    for k in range(2):
                        sp.wait_ge(y_stored[k], 16 * (NG * NCH // 2 + 1))
                        sp.wait_ge(stp_stored[k], 16 * (NG * N_BURST // 2 + 1))

                @block.gpsimd
                def _(pool):
                    def weigh(g, n):
                        pool.wait_ge(scanned, g * UNITS + n + 2)
                        b, i = n // BURST, n % BURST
                        col = (b % HALF) * HD + i
                        pool.sem_inc(beats, 1)
                        pool.tensor_copy(carry[:, col:col + 1], state[:, i, CH - 1:CH]).then_inc(carried, 1)
                        pool.wait_ge(carried, g * UNITS + n + 1)
                        pool.tensor_tensor(state[:, i], state[:, i], q_rows[:, b % 2], ALU.mult).then_inc(weighted, 1)

                    with pool.Fori(0, NG) as g:
                        for n in range(UNITS):
                            b = n // BURST
                            if n % BURST == 0:
                                pool.wait_ge(kq_loaded[b % 2], g * 64 + 32 * (b // 2) + 32)
                            pool.wait_ge(vexp_loaded[n % RING], g * (16 * UNITS // RING) + 16 * (n // RING) + 16)
                            pool.tensor_tensor(v_exp[:, n % RING], v_exp[:, n % RING], k_rows[:, b % 2], ALU.mult)\
                                .then_inc(u_made, 1)
                            if n >= 1:
                                weigh(g, n - 1)
                        weigh(g, UNITS - 1)

                @block.tensor
                def _(pe):
                    def max_scores(g, s, n):
                        c = ORDER[s]
                        if n == 0:
                            n_parts = 16 * len(SPLIT_K)
                            pe.wait_ge(loaded[f"q{c}"], g * n_parts + n_parts)
                            if s in FIRST_USE:
                                pe.wait_ge(loaded["k_" + FIRST_USE[s]], g * n_parts + n_parts)
                        hj, blk = n // (c + 1), n % (c + 1)
                        h, j = hj // TPC, hj % TPC
                        item = MAX_AT[s] + n
                        width = CH if blk < c else (j + 1) * P
                        bank = S_BANKS + item % M_BANKS
                        keys = K_first if s < FIRST_USERS and blk < FIRST else K_st
                        pe.wait_ge(max_done, g * N_MAX + item + 1)
                        mm = pe.matmul(PS[:, bank, 0:width], Q_st[0:KS, c, h, j * P:(j + 1) * P],
                                       keys[0:KS, h, blk * CH:blk * CH + width], start=True, stop=(blk < c))
                        if blk == c:
                            mm = pe.matmul(PS[:, bank, j * P:(j + 1) * P], ident_bf[:, :], mask_qk[:, :],
                                           start=False, stop=True)
                        mm.then_inc(max_ready, 1)

                    def scores(g, s, kt, h):
                        c = ORDER[s]
                        item = (TILE_AT[s] + kt) * GH + h
                        bank = item % S_BANKS
                        r = max(kt - TPC * c, 0)
                        if kt == 0 and h == 0:
                            pe.wait_ge(shift_loaded[s % 2], g * (SHIFTED * NCH // 2) + SHIFTED * (s // 2 + 2))
                        keys = K_first if s < FIRST_USERS and kt < FIRST * TPC else K_st
                        pe.wait_ge(exp_done, g * GH * TILES + item + 1)
                        mm = pe.matmul(PS[:, bank, 0:CH - r * P], keys[:, h, kt * P:(kt + 1) * P],
                                       Q_st[:, c, h, r * P:CH], start=True, stop=(kt < TPC * c))
                        if kt >= TPC * c:
                            mm = pe.matmul(PS[:, bank, 0:P], ident_bf[:, :], mask_kq[:, :], start=False, stop=True)
                        mm.then_inc(scores_ready, 1)

                    def values(g, s, kt):
                        c = ORDER[s]
                        tile = TILE_AT[s] + kt
                        r = max(kt - TPC * c, 0)
                        if kt == 0:
                            pe.wait_ge(out_evacuated, g * NCH + s + 1)
                            if s in FIRST_USE:
                                pe.wait_ge(loaded["v_" + FIRST_USE[s]], g * 16 + 16)
                        v = V_first if s < FIRST_USERS and kt < FIRST * TPC else V_g
                        pe.wait_ge(exp_done, g * GH * TILES + GH * (tile + 1) + S_BANKS)
                        for h in range(GH):
                            mm = pe.matmul(PS[h * VW:h * VW + VN, 6, r * P:CH], v[:, kt, h * VN:(h + 1) * VN],
                                           probs[:, tile % P_SLOTS, h, 0:CH - r * P],
                                           start=(kt == 0), stop=(kt == KEY_TILES[s] - 1))
                        mm.then_inc(values_done, 1)

                    def burst(g, b, part, use):
                        half = b % HALF
                        n_c = HD // TPC
                        if part == 0:
                            pe.wait_ge(weighted, g * UNITS + BURST * (b + 1) + HALF * HD)
                            pe.wait_ge(bank_free, use + 1)
                            for q in range(n_c):
                                pe.matmul(PS[q * VW:(q + 1) * VW, 7, :], static_j[:, half, q * VW:(q + 1) * VW],
                                          q_rows[:, b % 2], start=True, stop=False)
                        else:
                            k = part - 1
                            for q in range(n_c):
                                i = q * TPC + k
                                mm = pe.matmul(PS[q * VW:(q + 1) * VW, 7, :], sum_j[:, half, i, :],
                                               state[:, i], start=False, stop=(k == TPC - 1))
                            if k == TPC - 1:
                                mm.then_inc(burst_done, 1)

                    def walk(group, steps, bank):
                        for step in steps:
                            kind, g, s = step[0], group + step[1], step[2]
                            if kind == "max":
                                max_scores(g, s, step[3])
                            elif kind == "scores":
                                scores(g, s, step[3], step[4])
                            elif kind == "values":
                                values(g, s, step[3])
                            elif kind == "burst":
                                use = group * N_BANK + bank["burst", step[1], s]
                                burst(g, s, step[3], use)
                            elif kind == "shift_turn":
                                pe.wait_ge(folded, g * NCH + s + 1)
                                pe.wait_ge(bank_free, group * N_BANK + bank[step] + 1)
                                pe.transpose(PS[0:GH * TPC, 7, 0:P], neg_max[:, s % 2, :], ident[:, :])\
                                    .then_inc(shift_turned, 1)
                            elif kind == "out_turn":
                                pe.wait_ge(out_evacuated, g * NCH + s + 2)
                                pe.wait_ge(bank_free, group * N_BANK + bank[step] + 1)
                                for j in range(TPC):
                                    mm = pe.transpose(PS[:, 7, j * P:(j + 1) * P], o_t[:, s % 2, j * P:(j + 1) * P],
                                                      ident[:, :])
                                mm.then_inc(out_turned, 1)

                    walk(0, FIRST_STEPS, BANK_FIRST)
                    pe.wait_ge(ones_ready, 4)
                    with pe.Fori(0, NG - 1) as group:
                        walk(group, STEPS, BANK_STEPS)
                    walk(NG - 1, LAST_STEPS, BANK_LAST)

                @block.scalar
                def _(act):
                    def walk(g, steps):
                        for step in steps:
                            kind, s = step[0], step[2]
                            if kind == "scores":
                                tile, h = TILE_AT[s] + step[3], step[4]
                                r = max(step[3] - TPC * ORDER[s], 0)
                                if h == 0:
                                    act.wait_ge(values_done, g * TILES + tile + 1)
                                item = tile * GH + h
                                act.wait_ge(scores_ready, g * GH * TILES + item + 1)
                                act.activation(probs[:, tile % P_SLOTS, h, 0:CH - r * P], PS[:, item % S_BANKS, 0:CH - r * P],
                                               ACT.Exp, scale=SCALE).then_inc(exp_done, 1)
                            elif kind == "out_evac":
                                act.wait_ge(values_done, g * TILES + TILE_AT[s] + KEY_TILES[s] + P_SLOTS)
                                act.wait_ge(out_turned, g * NCH + s + 1)
                                act.activation(o_t[:, s % 2], PS[:, 6, :], ACT.Identity).then_inc(out_evacuated, 1)
                            elif kind == "burst" and step[3] == BURST_PARTS - 1:
                                act.wait_ge(burst_done, g * N_BURST + s + 2)
                                act.wait_ge(stp_stored[s % 2], g * (16 * N_BURST // 2) + 16 * (s // 2) + 16)
                                act.activation(stp_sb[:, s % 2], PS[:, 7, :], ACT.Identity).then_inc(bank_free, 1)

                    act.wait_ge(ones_ready, 2)
                    for k in range(0, NCH, NCH // 2):
                        act.activation(K_st[KS:KR, :, k * CH:(k + NCH // 2) * CH], K_first[KS:KR, :, 0:NCH // 2 * CH],
                                       ACT.Identity).then_inc(ones_ready, 1)
                    with act.Fori(0, NG - 1) as group:
                        walk(group, STEPS)
                    walk(NG - 1, LAST_STEPS)

                @block.vector
                def _(dve):
                    def walk(group, steps):
                        for step in steps:
                            kind, g, s = step[0], group + step[1], step[2]
                            if kind == "max":
                                c, n = ORDER[s], step[3]
                                hj, blk = n // (c + 1), n % (c + 1)
                                item = MAX_AT[s] + n
                                width = CH if blk < c else (hj % TPC + 1) * P
                                dve.wait_ge(max_ready, g * N_MAX + item + 1)
                                dve.tensor_reduce(pmax[:, s % 2, hj, blk:blk + 1], PS[:, S_BANKS + item % M_BANKS, 0:width], AX.X,
                                                  ALU.max).then_inc(max_done, 1)
                            elif kind == "fold":
                                dve.wait_ge(max_done, g * N_MAX + MAX_AT[s] + MAXES[s] + M_BANKS)
                                dve.tensor_reduce(neg_max[:, s % 2, :], pmax[:, s % 2, :, 0:ORDER[s] + 1], AX.X, ALU.max,
                                                  negate=True).then_inc(folded, 1)
                            elif kind == "shift_split":
                                dve.wait_ge(shift_turned, g * NCH + s + 1)
                                dve.wait_ge(shift_loaded[s % 2], g * (SHIFTED * NCH // 2) + SHIFTED * (s // 2 + 1))
                                turned = PS[0:GH * TPC, 7, 0:P]
                                dve.tensor_copy(shift[:, s % 2, 0, :], turned).then_inc(shift_high, 1)
                                dve.wait_ge(shift_high, g * NCH + s + 1)
                                dve.tensor_tensor(shift[:, s % 2, 1, :], turned, shift[:, s % 2, 0, :], ALU.subtract)\
                                    .then_inc(bank_free, 1)
                            elif kind == "out_norm":
                                dve.wait_ge(out_turned, g * NCH + s + 3)
                                dve.wait_ge(y_stored[s % 2], g * (16 * NCH // 2) + 16 * (s // 2) + 16)
                                sums = PS[:, 7, :].rearrange("p (j h v) -> p j h v", j=TPC, h=GH)
                                dve.reciprocal(rden[:, :, :], sums[:, :, :, HD]).then_inc(denom_ready, 1)
                                dve.wait_ge(denom_ready, g * NCH + s + 1)
                                dve.tensor_tensor(y_sb[:, s % 2].rearrange("p j (h v) -> p j h v", h=GH),
                                                  sums[:, :, :, 0:HD],
                                                  rden[:, :, :].unsqueeze(3).broadcast_to([P, TPC, GH, HD]), ALU.mult)\
                                    .then_inc(bank_free, 1)
                            elif kind == "unit":
                                b, i = s // BURST, s % BURST
                                col = (b % HALF) * HD + i
                                dve.wait_ge(u_made, g * UNITS + s + 1)
                                if i == 0:
                                    dve.wait_ge(burst_done, g * N_BURST + b + 1)
                                dve.wait_ge(weighted, g * UNITS + s + 1)
                                dve.tensor_tensor_scan(state[:, i], retention[:, col:col + 1].broadcast_to([P, CH]),
                                                       v_exp[:, s % RING], carry[:, col:col + 1], ALU.mult, ALU.add)\
                                    .then_inc(scanned, 1)

                    dve.memset(PS[:, 6, :], 0.0).then_inc(ones_ready, 1)
                    walk(0, FIRST_STEPS)
                    with dve.Fori(0, NG - 1) as group:
                        walk(group, STEPS)
                    walk(NG - 1, LAST_STEPS)

        early.close()

        fin = ExitStack()
        with fin:
            x1 = sb("x1", [P, NT, D], where=fin)
            xn2 = sb("xn2", [P, NT, D], where=fin)
            soft = sb("soft", [P, 2, TPC, D], where=fin)
            stp = sb("stp", [P, 2, HALF, CH], where=fin)
            xres = sb("xres", [P, 2, TPC, D], where=fin)
            xb = sb("xb", [P, 2, TPC, D], where=fin)
            diff = sb("diff", [P, 2, TPC, D], where=fin)
            y = sb("y", [P, 2, TPC, D], where=fin)
            y_t = sb("y_t", [P, 2, HALF, CH], where=fin)
            stats = sb("stats2", [P, TPC, 6], where=fin)
            mv = sb("mv2", [P, TPC, 2], where=fin)
            rstd = sb("rstd2", [P, 2 * TPC], where=fin)
            var_eps = sb("var_eps2", [P, TPC], where=fin)
            nmr = sb("nmr2", [P, 2 * TPC], where=fin)
            amax = sb("amax", [P, NCH], where=fin)
            small = sb("small", [P, 8], where=fin)
            scl = sb("scl", [P, 2, TPC * D], where=fin)
            magic = sb("magic", [P, 2, TPC * D], where=fin)
            moved = sb("moved", [P, 2, TPC * D], where=fin)
            r_bf = sb("r_bf", [P, 2, TPC, D], BF16, where=fin)
            r_t = sb("r_t", [P, 2, HALF, CH], BF16, where=fin)
            o_bf = sb("o_bf", [P, 2, TPC, D], BF16, where=fin)
            o_f = sb("o_f", [P, 2, TPC, D], where=fin)
            x_tiles = x.rearrange("(t p) n -> p t n", p=P)
            soft_tiles = y_soft.rearrange("g (t p) v -> g p t v", p=P)
            out_tiles = out.rearrange("(t p) n -> p t n", p=P)

            def tiles(it, par):
                return bass.ds(it * (2 * TPC) + par * TPC, TPC)

            def pipeline(engine, *stages):
                depth = max(lag for lag, _ in stages)
                peeled = depth + depth % 2

                def step(it, par, whole):
                    for lag, stage in stages:
                        if whole or 0 <= it * 2 + par - lag < NCH:
                            stage(it + (par - lag) // 2, (par - lag) % 2)

                for k in range(peeled):
                    step(k // 2, k % 2, False)
                with engine.Fori(peeled // 2, NCH // 2) as it:
                    step(it, 0, True)
                    step(it, 1, True)
                for k in range(NCH, NCH + depth):
                    step(k // 2, k % 2, False)

            with nc.Block() as block:
                @block.sync
                def _(sp):
                    with sp.Fori(0, NCH // 2) as it:
                        for par in range(2):
                            sp.wait_ge(diff_made, it * 2 + par + 1)
                            sp.wait_ge(stp_turned, it * 2 + par + 1)
                            for g in range(NG):
                                sp.dma_start(soft[:, par, :, g * GH * HD:(g + 1) * GH * HD], soft_tiles[g, :, tiles(it, par), :])\
                                    .then_inc(soft_loaded[par], 16)
                            sp.dma_start(stp[:, par], y_stp_t[:, :, bass.ds(it * (2 * CH) + par * CH + PAD, CH)]
                                         .rearrange("f p t -> p f t")).then_inc(soft_loaded[par], 16)
                            sp.wait_ge(xb_made, it * 2 + par + 1)
                            sp.sem_inc(beats, 1)
                            sp.dma_start(xres[:, par], x_tiles[:, tiles(it, par), :]).then_inc(x_again[par], 16)
                    with sp.Fori(0, NCH // 2) as it:
                        for par in range(2):
                            sp.wait_ge(out_made, it * 2 + par + 3)
                            sp.dma_start(out_tiles[:, tiles(it, par), :], o_f[:, par]).then_inc(out_stored[par], 16)
                    for par in range(2):
                        sp.wait_ge(out_stored[par], 16 * (NCH // 2 + 1))

                @block.gpsimd
                def _(pool):
                    def weigh(it, par):
                        pool.wait_ge(gate_chain, 3)
                        pool.wait_ge(diff_made, it * 2 + par + 3)
                        pool.tensor_tensor(diff[:, par].rearrange("p j (h v) -> p j h v", h=H),
                                           diff[:, par].rearrange("p j (h v) -> p j h v", h=H),
                                           alpha[:, tiles(it, par), :].unsqueeze(3).broadcast_to([P, TPC, H, HD]),
                                           ALU.mult).then_inc(diff_weighted, 1)

                    def power(it, par):
                        pool.wait_ge(var2, it * 2 + par + 1)
                        pool.tensor_tensor(rstd[:, par * TPC:(par + 1) * TPC], var_eps[:, :], neg_half[:, :], ALU.pow)\
                            .then_inc(rstd2, 1)

                    def residual(it, par):
                        pool.wait_ge(x_again[par], it * 16 + 16)
                        pool.wait_ge(x1_made, it * 2 + par + 1)
                        pool.tensor_tensor(xb[:, par], xres[:, par],
                                           outb_sb[:, :].unsqueeze(1).broadcast_to([P, TPC, D]), ALU.add)\
                            .then_inc(xb_made, 1)

                    pipeline(pool, (1, residual), (0, weigh), (2, power))
                    pool.wait_ge(peak_ready, 1)
                    pool.partition_all_reduce(small[:, 1:2], small[:, 0:1], P, bass.bass_isa.ReduceOp.max)\
                        .then_inc(amax_all, 1)

                    def round_off(it, par):
                        pool.wait_ge(shifted, it * 2 + par + 1)
                        pool.wait_ge(r_turned, it * 2 + par + 1)
                        pool.tensor_tensor(r_bf[:, par].rearrange("p j n -> p (j n)"), moved[:, par], magic[:, par],
                                           ALU.subtract).then_inc(rounded, 1)

                    def add_ffn(it, par):
                        pool.wait_ge(ffn_biased, it * 2 + par + 3)
                        pool.wait_ge(out_stored[par], it * 16 + 16)
                        pool.tensor_tensor(o_f[:, par], x1[:, tiles(it, par), :], o_bf[:, par], ALU.add)\
                            .then_inc(out_made, 1)

                    pipeline(pool, (2, add_ffn), (0, round_off))

                @block.tensor
                def _(pe):
                    def turn_stp(it, par):
                        pe.wait_ge(soft_loaded[par], it * LOADS_PER_CHUNK + LOADS_PER_CHUNK)
                        pe.wait_ge(y_made, it * 2 + par + 1)
                        for half in range(HALF):
                            for j in range(TPC):
                                mm = pe.transpose(PS[:, 2 * par + half, j * P:(j + 1) * P],
                                                  stp[:, par, half, j * P:(j + 1) * P], ident[:, :])
                        mm.then_inc(stp_turned, 1)

                    def turn_y(it, par):
                        pe.wait_ge(y_made, it * 2 + par + 3)
                        pe.wait_ge(yt_evac, it * 4 + par * 2 + 2)
                        for c in range(HALF):
                            for j in range(TPC):
                                mm = pe.transpose(PS[:, 4 + c, j * P:(j + 1) * P], y[:, par, j, c * P:(c + 1) * P],
                                                  ident[:, :])
                        mm.then_inc(y_turned, 1)

                    def project(it, par):
                        pe.wait_ge(yt_evac, it * 4 + par * 2 + 4)
                        pe.wait_ge(x1_made, it * 2 + par + 2)
                        for j in range(TPC):
                            for c in range(HALF):
                                mm = pe.matmul(PS[:, 6 + j // 2, (j % 2) * D:(j % 2 + 1) * D],
                                               y_t[:, par, c, j * P:(j + 1) * P], outw_sb[:, c, :],
                                               start=(c == 0), stop=(c == HALF - 1))
                        mm.then_inc(attn_ready, 1)

                    pipeline(pe, (0, turn_stp), (2, project), (1, turn_y))

                    def turn_rounded(it, par):
                        pe.wait_ge(rounded, it * 2 + par + 3)
                        pe.wait_ge(rt_evac, it * 2 + par + 1)
                        turned = PS[:, par, :].bitcast(BF16)
                        for c in range(HALF):
                            for j in range(TPC):
                                mm = pe.transpose(turned[:, c * CH + j * P:c * CH + (j + 1) * P],
                                                  r_bf[:, par, j, c * P:(c + 1) * P], ident_bf[:, :])
                        mm.then_inc(r_turned, 1)

                    def ffn(it, par):
                        pe.wait_ge(rt_evac, it * 2 + par + 3)
                        pe.wait_ge(ffn_biased, it * 2 + par + 1)
                        for j in range(TPC):
                            for c in range(HALF):
                                mm = pe.matmul(PS[:, 2 + 2 * par + j // 2, (j % 2) * D:(j % 2 + 1) * D],
                                               r_t[:, par, c, j * P:(j + 1) * P], wq[:, c, :],
                                               start=(c == 0), stop=(c == HALF - 1))
                        mm.then_inc(ffn_ready, 1)

                    pipeline(pe, (0, turn_rounded), (0, ffn))

                @block.scalar
                def _(act):
                    def columns(it, par):
                        act.wait_ge(y_turned, it * 2 + par + 1)
                        act.wait_ge(attn_ready, it * 2 + par + 1)
                        for c in range(HALF):
                            act.activation(y_t[:, par, c, :], PS[:, 4 + c, :], ACT.Identity).then_inc(yt_evac, 1)

                    def normalise(it, par):
                        act.wait_ge(nmr2, it * 2 + par + 1)
                        for j in range(TPC):
                            row = bass.ds(it * (2 * TPC) + par * TPC + j, 1)
                            ins = act.activation(xn2[:, row, :], x1[:, row, :], ACT.Identity,
                                                 bias=nmr[:, par * TPC + j:par * TPC + j + 1],
                                                 scale=rstd[:, par * TPC + j:par * TPC + j + 1])
                        ins.then_inc(xn2_made, 1)

                    act.wait_ge(gate_chain, 1)
                    act.activation(alpha[:, :, :], z[:, :, :], ACT.Exp, scale=-1.0).then_inc(gate_exp, 1)
                    pipeline(act, (1, columns), (2, normalise))

                    def rounded_columns(it, par):
                        act.wait_ge(r_turned, it * 2 + par + 3)
                        act.wait_ge(ffn_ready, it * 2 + par + 1)
                        act.activation(r_t[:, par].rearrange("p c t -> p (c t)"), PS[:, par, :].bitcast(BF16),
                                       ACT.Identity).then_inc(rt_evac, 1)

                    pipeline(act, (0, rounded_columns))

                @block.vector
                def _(dve):
                    def by_head(rows):
                        return rows.rearrange("p j (h i) -> p j h i", h=HPH)

                    def recurrence(par, half):
                        return PS[:, 2 * par + half, :].rearrange("p (j i h) -> p j h i", j=TPC, i=HD)

                    def difference(it, par):
                        dve.wait_ge(stp_turned, it * 2 + par + 3)
                        for f in range(HALF):
                            cols = slice(f * P, (f + 1) * P)
                            ins = dve.tensor_tensor(by_head(diff[:, par, :, cols]), recurrence(par, f),
                                                    by_head(soft[:, par, :, cols]), ALU.subtract)
                        ins.then_inc(diff_made, 1)

                    def merge(it, par):
                        dve.wait_ge(diff_weighted, it * 2 + par + 1)
                        for f in range(HALF):
                            cols = slice(f * P, (f + 1) * P)
                            ins = dve.tensor_tensor(by_head(y[:, par, :, cols]), recurrence(par, f),
                                                    by_head(diff[:, par, :, cols]), ALU.subtract)
                        ins.then_inc(y_made, 1)

                    def add_attention(it, par):
                        n1 = it * 2 + par + 1
                        dve.wait_ge(attn_ready, it * 2 + par + 3)
                        dve.wait_ge(xb_made, it * 2 + par + 3)
                        dve.tensor_tensor(x1[:, tiles(it, par), :],
                                          PS[:, 6:8, :].rearrange("p b (j n) -> p (b j) n", n=D), xb[:, par], ALU.add)\
                            .then_inc(x1_made, 1)
                        dve.wait_ge(x1_made, it * 2 + par + 3)
                        dve.sem_inc(beats, 1)
                        for j in range(TPC):
                            ins = dve.bn_stats(stats[:, j, :], x1[:, bass.ds(it * (2 * TPC) + par * TPC + j, 1), :]
                                               .rearrange("p a n -> p (a n)"))
                        ins.then_inc(stats2, 1)
                        dve.wait_ge(stats2, n1)
                        dve.sem_inc(beats, 1)
                        for j in range(TPC):
                            ins = dve.bn_aggr(mv[:, j, :], stats[:, j, :])
                        ins.then_inc(mv2, 1)
                        dve.wait_ge(mv2, n1)
                        dve.tensor_scalar(var_eps[:, :], mv[:, :, 1], EPS, None, ALU.add).then_inc(var2, 1)

                    def mean_by_rstd(it, par):
                        dve.wait_ge(rstd2, it * 2 + par + 1)
                        dve.scalar_tensor_tensor(out=nmr[:, par * TPC:(par + 1) * TPC], in0=mv[:, :, 0], scalar=-1.0,
                                                 in1=rstd[:, par * TPC:(par + 1) * TPC], op0=ALU.mult, op1=ALU.mult)\
                            .then_inc(nmr2, 1)

                    def largest(it, par):
                        dve.wait_ge(xn2_made, it * 2 + par + 1)
                        dve.tensor_reduce(amax[:, bass.ds(it * 2 + par, 1)],
                                          xn2[:, tiles(it, par), :].rearrange("p j n -> p (j n)"), AX.X, ALU.max,
                                          apply_absolute_value=True).then_inc(amax_made, 1)

                    dve.tensor_tensor(z[:, :, :], z[:, :, :], b2_sb[:, :].unsqueeze(1).broadcast_to([P, NT, H]), ALU.add)\
                        .then_inc(gate_chain, 1)
                    dve.wait_ge(gate_exp, 1)
                    dve.tensor_scalar(alpha[:, :, :], alpha[:, :, :], 1.0, None, ALU.add).then_inc(gate_chain, 1)
                    dve.wait_ge(gate_chain, 2)
                    dve.reciprocal(alpha[:, :, :], alpha[:, :, :]).then_inc(gate_chain, 1)
                    pipeline(dve, (1, merge), (0, difference), (2, add_attention), (3, largest), (2, mean_by_rstd))
                    dve.wait_ge(amax_made, NCH)
                    dve.tensor_reduce(small[:, 0:1], amax[:, :], AX.X, ALU.max).then_inc(peak_ready, 1)
                    n_scale = 0

                    def link(ins):
                        nonlocal n_scale
                        n_scale += 1
                        ins.then_inc(scale_chain, 1)
                        dve.wait_ge(scale_chain, n_scale)

                    dve.wait_ge(amax_all, 1)
                    link(dve.tensor_scalar(small[:, 2:3], small[:, 1:2], 1e-12, None, ALU.max))
                    link(dve.reciprocal(small[:, 3:4], small[:, 2:3]))
                    link(dve.tensor_scalar(small[:, 4:5], small[:, 3:4], FP8_MAX, FP8_MAX, ALU.mult, ALU.min))
                    link(dve.reciprocal(small[:, 5:6], small[:, 4:5]))
                    link(dve.tensor_tensor(small[:, 6:7], small[:, 5:6], w_step[:, :], ALU.mult))

                    def quantise(it, par):
                        n1 = it * 2 + par + 1
                        dve.wait_ge(rounded, n1)
                        dve.tensor_scalar(scl[:, par], xn2[:, tiles(it, par), :].rearrange("p j n -> p (j n)"),
                                          small[:, 4:5], FP8_MAX, ALU.mult, ALU.min).then_inc(scaled, 1)
                        dve.wait_ge(scaled, n1)
                        dve.tensor_scalar(magic[:, par].bitcast(I32), scl[:, par].bitcast(I32), EXPONENT_BITS, None,
                                          ALU.bitwise_and).then_inc(exponent_done, 1)
                        dve.wait_ge(exponent_done, n1)
                        dve.tensor_scalar(magic[:, par], magic[:, par], FP8_MIN_NORMAL, ROUND_TO_3_BITS, ALU.max,
                                          ALU.mult).then_inc(magic_done, 1)
                        dve.wait_ge(magic_done, n1)
                        dve.scalar_tensor_tensor(out=moved[:, par], in0=scl[:, par], scalar=-FP8_MAX, in1=magic[:, par],
                                                 op0=ALU.max, op1=ALU.add).then_inc(shifted, 1)

                    def dequantise(it, par):
                        dve.wait_ge(ffn_ready, it * 2 + par + 3)
                        dve.wait_ge(out_made, it * 2 + par + 1)
                        dve.scalar_tensor_tensor(out=o_bf[:, par],
                                                 in0=PS[:, 2 + 2 * par:4 + 2 * par, :].rearrange("p b (j n) -> p (b j) n", n=D),
                                                 scalar=small[:, 6:7],
                                                 in1=ffnb_sb[:, :].unsqueeze(1).broadcast_to([P, TPC, D]),
                                                 op0=ALU.mult, op1=ALU.add).then_inc(ffn_biased, 1)

                    pipeline(dve, (2, dequantise), (0, quantise))


def kernel(L0_attn_x, L0_attn_Wqkv_w, L0_attn_Wqkv_b, L0_attn_out_w, L0_attn_out_b, L0_attn_W_static,
           L0_attn_Lambda_raw, L0_attn_Gamma, L0_attn_gate_w1, L0_attn_gate_b1, L0_attn_gate_w2,
           L0_attn_gate_b2, L0_ffn_weight, L0_ffn_bias):
    import numpy as np
    import concourse.bacc as bacc
    from concourse.bass_utils import run_bass_kernel_spmd

    def by_row(a):
        return np.asarray(a).reshape(HALF, HPH, HD, HD).transpose(1, 3, 0, 2).reshape(P, HALF * HD)

    inputs = {
        "x": np.asarray(L0_attn_x).reshape(T, D),
        "wqkv": np.asarray(L0_attn_Wqkv_w),
        "bqkv": np.asarray(L0_attn_Wqkv_b).reshape(6, P).T,
        "out_w": np.asarray(L0_attn_out_w),
        "out_b": np.asarray(L0_attn_out_b).reshape(1, D),
        "w_static": by_row(L0_attn_W_static),
        "lam": by_row(L0_attn_Lambda_raw),
        "gamma": by_row(L0_attn_Gamma),
        "gate_w1": np.asarray(L0_attn_gate_w1),
        "gate_b1": np.asarray(L0_attn_gate_b1).reshape(GATE, 1),
        "gate_w2": np.asarray(L0_attn_gate_w2),
        "gate_b2": np.asarray(L0_attn_gate_b2).reshape(1, H),
        "ffn_wt": np.asarray(L0_ffn_weight).T,
        "ffn_b": np.asarray(L0_ffn_bias).reshape(1, D),
    }
    inputs = {n: np.ascontiguousarray(a) for n, a in inputs.items()}
    nc = bacc.Bacc("TRN2", target_bir_lowering=False, num_devices=1)
    args = {n: nc.dram_tensor(n, a.shape, F32, kind="ExternalInput").ap() for n, a in inputs.items()}
    out = nc.dram_tensor("out", [T, D], F32, kind="ExternalOutput").ap()
    preln_attention_ffn_kernel(nc, out=out, **args)
    r = run_bass_kernel_spmd(nc, [inputs], core_ids=[0])
    return np.asarray(r.results[0]["out"]).reshape(1, T, D)
```
